# Optimizing a Trainium2 kernel written in Bass

```python
import numpy as np
import jax
import jax.numpy as jnp

def _softmax(x, axis=-1):
    return jax.nn.softmax(x, axis=axis)

def _gelu(x):
    return jax.nn.gelu(x, approximate=True)

def _silu(x):
    return jax.nn.silu(x)

def _sigmoid(x):
    return jax.nn.sigmoid(x)

def _layernorm(x, axis=-1, eps=1e-05):
    m = jnp.mean(x, axis=axis, keepdims=True)
    v = jnp.var(x, axis=axis, keepdims=True)
    return (x - m) / jnp.sqrt(v + eps)

def _scatter_add(tgt, idx, src, axis=0):
    return tgt.at[idx].add(src)

def _segment_sum(src, seg, n):
    return jax.ops.segment_sum(src, seg, n)
kernel_name = 'mk_gnn_ffn_d2_gnn_r32_f34daf'

def setup_inputs(seed: int=0):
    np.random.seed(seed)
    _w = jnp.asarray

    def _rec_inputs():
        import jax
        import jax.numpy as jnp
        _gk = jax.random.key(seed)
        x = -0.0003713 + 1 * jax.random.normal(jax.random.fold_in(_gk, 1), (3125, 256), jnp.float32)
        _s = jax.random.randint(jax.random.fold_in(_gk, 2), (25000,), 0, 3125, jnp.int32)
        _d = jax.random.randint(jax.random.fold_in(_gk, 3), (25000,), 0, 3125, jnp.int32)
        _loop = jnp.arange(3125, dtype=jnp.int32)
        src = jnp.concatenate([_s, _d, _loop])
        dst = jnp.concatenate([_d, _s, _loop])
        _o = jnp.argsort(dst, stable=True)
        src = src[_o]
        dst = dst[_o]
        return (x, src, dst)
    x, src, dst = _rec_inputs()

    def _L0_gnn_setup():
        import jax, jax.numpy as jnp
        import numpy as np
        N = 50000
        E_RAND = 25000
        F_IN = 256
        F_OUT = 256
        ALPHA = 0.2
        key = jax.random.key(seed)
        k1, k2, k3, k4 = jax.random.split(key, 4)
        x = jax.random.normal(k1, (N, F_IN), dtype=jnp.float32)
        edge_rand = jax.random.randint(k2, (2, E_RAND), 0, N)
        loops = jnp.arange(N)
        edge = jnp.concatenate([edge_rand, jnp.stack([loops, loops])], axis=1)
        W = jax.random.normal(k3, (F_IN, F_OUT), dtype=jnp.float32) * 0.05
        a = jax.random.normal(k4, (2 * F_OUT,), dtype=jnp.float32) * 0.05
        return {'x': x, 'edge': edge, 'W': W, 'a': a}
    _L0_gnn_all = _L0_gnn_setup()
    _L0_gnn_in = {k: v for k, v in _L0_gnn_all.items() if k in ('W', 'a')}
    del _L0_gnn_all

    def _L0_ffn_setup():
        import math
        import jax, jax.numpy as jnp
        import numpy as np
        CAPACITY_FACTOR = 1.25
        key = jax.random.key(seed)
        ks = jax.random.split(key, 5)
        B, L, D, F, E = (8, 256, 256, 1024, 8)
        h = jax.random.normal(ks[0], (B, L, D), dtype=jnp.float32)
        gate_w = jax.random.normal(ks[1], (D, E), dtype=jnp.float32) * 0.02
        gate_b = jnp.zeros((E,), dtype=jnp.float32)
        w1 = jax.random.normal(ks[2], (E, D, F), dtype=jnp.float32) * (1.0 / math.sqrt(D))
        b1 = jnp.zeros((E, F), dtype=jnp.float32)
        w2 = jax.random.normal(ks[3], (E, F, D), dtype=jnp.float32) * (1.0 / math.sqrt(F))
        b2 = jnp.zeros((E, D), dtype=jnp.float32)
        return {'h': h, 'gate_w': gate_w, 'gate_b': gate_b, 'w1': w1, 'b1': b1, 'w2': w2, 'b2': b2}
    _L0_ffn_all = _L0_ffn_setup()
    _L0_ffn_in = {k: v for k, v in _L0_ffn_all.items() if k in ('gate_w', 'gate_b', 'w1', 'b1', 'w2', 'b2')}
    del _L0_ffn_all

    def _L1_gnn_setup():
        import jax, jax.numpy as jnp
        import numpy as np
        N_NODES = 50000
        N_EDGES = 25000
        IN_CH = 256
        HID_CH = 256
        OUT_CH = 256
        N_LAYERS = 3
        key = jax.random.key(seed)
        ks = jax.random.split(key, 8)
        s_in = 1.0 / np.sqrt(IN_CH)
        s_h = 1.0 / np.sqrt(HID_CH)
        return {'x': jax.random.normal(ks[0], (N_NODES, IN_CH), dtype=jnp.float32), 'W_in': jax.random.normal(ks[1], (IN_CH, HID_CH), dtype=jnp.float32) * s_in, 'b_in': jnp.zeros((HID_CH,), dtype=jnp.float32), 'W_agg': jax.random.normal(ks[2], (N_LAYERS, HID_CH, HID_CH), dtype=jnp.float32) * s_h, 'W_self': jax.random.normal(ks[3], (N_LAYERS, HID_CH, HID_CH), dtype=jnp.float32) * s_h, 'b_hid': jnp.zeros((N_LAYERS, HID_CH), dtype=jnp.float32), 'W_out': jax.random.normal(ks[4], (HID_CH, OUT_CH), dtype=jnp.float32) * s_h, 'b_out': jnp.zeros((OUT_CH,), dtype=jnp.float32), 'edge_index': jax.random.randint(ks[5], (2, N_EDGES), 0, N_NODES, dtype=jnp.int64)}
    _L1_gnn_all = _L1_gnn_setup()
    _L1_gnn_in = {k: v for k, v in _L1_gnn_all.items() if k in ('W_in', 'b_in', 'W_agg', 'W_self', 'b_hid', 'W_out', 'b_out')}
    del _L1_gnn_all

    def _L1_ffn_setup():
        import jax, jax.numpy as jnp
        import numpy as np
        B, A = (128, 8)
        IN, OUT = (256, 256)
        SH1, SH2 = (256, 128)
        EH1, EH2 = (128, 64)
        E, TOPK = (4, 2)

        def _shared_mlp(x, W1, b1, W2, b2, W3, b3):
            h = jax.nn.relu(x @ W1 + b1)
            h = jax.nn.relu(h @ W2 + b2)
            return h @ W3 + b3

        def _experts_mlp(x, eW1, eb1, eW2, eb2, eW3, eb3):
            h = jax.nn.relu(jnp.einsum('baf,efh->ebah', x, eW1) + eb1[:, None, None, :])
            h = jax.nn.relu(jnp.einsum('ebah,ehg->ebag', h, eW2) + eb2[:, None, None, :])
            o = jnp.einsum('ebag,ego->ebao', h, eW3) + eb3[:, None, None, :]
            return jnp.moveaxis(o, 0, -1)
        key = jax.random.key(seed)
        ks = jax.random.split(key, 16)
        s = 0.05
        return {'x': jax.random.normal(ks[0], (B, A, IN), jnp.float32), 'sW1': jax.random.normal(ks[1], (IN, SH1), jnp.float32) * s, 'sb1': jnp.zeros((SH1,), jnp.float32), 'sW2': jax.random.normal(ks[2], (SH1, SH2), jnp.float32) * s, 'sb2': jnp.zeros((SH2,), jnp.float32), 'sW3': jax.random.normal(ks[3], (SH2, OUT), jnp.float32) * s, 'sb3': jnp.zeros((OUT,), jnp.float32), 'eW1': jax.random.normal(ks[4], (E, IN, EH1), jnp.float32) * s, 'eb1': jnp.zeros((E, EH1), jnp.float32), 'eW2': jax.random.normal(ks[5], (E, EH1, EH2), jnp.float32) * s, 'eb2': jnp.zeros((E, EH2), jnp.float32), 'eW3': jax.random.normal(ks[6], (E, EH2, OUT), jnp.float32) * s, 'eb3': jnp.zeros((E, OUT), jnp.float32), 'gW': jax.random.normal(ks[7], (IN, E), jnp.float32) * s, 'gb': jnp.zeros((E,), jnp.float32)}
    _L1_ffn_all = _L1_ffn_setup()
    _L1_ffn_in = {k: v for k, v in _L1_ffn_all.items() if k in ('sW1', 'sb1', 'sW2', 'sb2', 'sW3', 'sb3', 'eW1', 'eb1', 'eW2', 'eb2', 'eW3', 'eb3', 'gW', 'gb')}
    del _L1_ffn_all
    return {'x': x, 'src': src, 'dst': dst, 'L0_gnn_W': _L0_gnn_in['W'], 'L0_gnn_a': _L0_gnn_in['a'], 'L0_ffn_gate_w': _L0_ffn_in['gate_w'], 'L0_ffn_gate_b': _L0_ffn_in['gate_b'], 'L0_ffn_w1': _L0_ffn_in['w1'], 'L0_ffn_b1': _L0_ffn_in['b1'], 'L0_ffn_w2': _L0_ffn_in['w2'], 'L0_ffn_b2': _L0_ffn_in['b2'], 'L1_gnn_W_in': _L1_gnn_in['W_in'], 'L1_gnn_b_in': _L1_gnn_in['b_in'], 'L1_gnn_W_agg': _L1_gnn_in['W_agg'], 'L1_gnn_W_self': _L1_gnn_in['W_self'], 'L1_gnn_b_hid': _L1_gnn_in['b_hid'], 'L1_gnn_W_out': _L1_gnn_in['W_out'], 'L1_gnn_b_out': _L1_gnn_in['b_out'], 'L1_ffn_sW1': _L1_ffn_in['sW1'], 'L1_ffn_sb1': _L1_ffn_in['sb1'], 'L1_ffn_sW2': _L1_ffn_in['sW2'], 'L1_ffn_sb2': _L1_ffn_in['sb2'], 'L1_ffn_sW3': _L1_ffn_in['sW3'], 'L1_ffn_sb3': _L1_ffn_in['sb3'], 'L1_ffn_eW1': _L1_ffn_in['eW1'], 'L1_ffn_eb1': _L1_ffn_in['eb1'], 'L1_ffn_eW2': _L1_ffn_in['eW2'], 'L1_ffn_eb2': _L1_ffn_in['eb2'], 'L1_ffn_eW3': _L1_ffn_in['eW3'], 'L1_ffn_eb3': _L1_ffn_in['eb3'], 'L1_ffn_gW': _L1_ffn_in['gW'], 'L1_ffn_gb': _L1_ffn_in['gb']}

def reference(x, src, dst, L0_gnn_W, L0_gnn_a, L0_ffn_gate_w, L0_ffn_gate_b, L0_ffn_w1, L0_ffn_b1, L0_ffn_w2, L0_ffn_b2, L1_gnn_W_in, L1_gnn_b_in, L1_gnn_W_agg, L1_gnn_W_self, L1_gnn_b_hid, L1_gnn_W_out, L1_gnn_b_out, L1_ffn_sW1, L1_ffn_sb1, L1_ffn_sW2, L1_ffn_sb2, L1_ffn_sW3, L1_ffn_sb3, L1_ffn_eW1, L1_ffn_eb1, L1_ffn_eW2, L1_ffn_eb2, L1_ffn_eW3, L1_ffn_eb3, L1_ffn_gW, L1_ffn_gb):
    import jax
    import jax.numpy as jnp

    def _L0_gnn_ref(x, edge, W, a):
        import jax, jax.numpy as jnp
        import numpy as np
        N = 50000
        E_RAND = 25000
        F_IN = 256
        F_OUT = 256
        ALPHA = 0.2
        n = x.shape[0]
        f_out = W.shape[1]
        h = x @ W
        src, dst = (edge[0], edge[1])
        s = h @ a[:f_out]
        t = h @ a[f_out:]
        logit = s[src] + t[dst]
        e = jnp.exp(-jax.nn.leaky_relu(logit, ALPHA))
        rowsum = jax.ops.segment_sum(e, src, num_segments=n)
        msg = e[:, None] * h[dst]
        h_prime = jax.ops.segment_sum(msg, src, num_segments=n)
        h_prime = h_prime / rowsum[:, None]
        return jax.nn.relu(h_prime)

    def _L0_ffn_ref(h, gate_w, gate_b, w1, b1, w2, b2):
        import math
        import jax, jax.numpy as jnp
        import numpy as np
        CAPACITY_FACTOR = 1.25
        B, L, D = h.shape
        E = gate_w.shape[1]
        T = B * L
        C = max(1, math.ceil(CAPACITY_FACTOR * T / E))
        x = h.reshape(T, D)
        logits = x @ gate_w + gate_b
        probs = jax.nn.softmax(logits, axis=-1)
        idx = jnp.argmax(probs, axis=-1)
        prb = jnp.take_along_axis(probs, idx[:, None], axis=1)[:, 0]
        one_hot = jax.nn.one_hot(idx, E, dtype=jnp.float32)
        pos = (jnp.cumsum(one_hot, axis=0) * one_hot).sum(-1).astype(jnp.int32) - 1
        kept = pos < C
        pos_safe = jnp.where(kept, pos, C)
        buf = jnp.zeros((E, C, D), dtype=h.dtype).at[idx, pos_safe].set(x, mode='drop')
        hmid = jax.nn.relu(jnp.einsum('ecd,edf->ecf', buf, w1) + b1[:, None, :])
        ybuf = jnp.einsum('ecf,efd->ecd', hmid, w2) + b2[:, None, :]
        pos_g = jnp.minimum(pos, C - 1)
        y_tok = ybuf[idx, pos_g] * (prb * kept)[:, None]
        y = y_tok.reshape(B, L, D)
        y = jnp.nan_to_num(y, nan=0.0, posinf=10000.0, neginf=-10000.0)
        return y

    def _L1_gnn_ref(x, W_in, b_in, W_agg, W_self, b_hid, W_out, b_out, edge_index):
        import jax, jax.numpy as jnp
        import numpy as np
        N_NODES = 50000
        N_EDGES = 25000
        IN_CH = 256
        HID_CH = 256
        OUT_CH = 256
        N_LAYERS = 3
        n = x.shape[0]
        dst = edge_index[0]
        src = edge_index[1]
        n_layers = W_agg.shape[0]
        h = x @ W_in + b_in
        deg = jax.ops.segment_sum(jnp.ones_like(dst, dtype=h.dtype), dst, num_segments=n)
        deg = jnp.maximum(deg, 1.0)[:, None]
        for l in range(n_layers):
            agg = jax.ops.segment_sum(h[src], dst, num_segments=n) / deg
            h = jax.nn.relu(agg @ W_agg[l] + h @ W_self[l] + b_hid[l])
        return h @ W_out + b_out

    def _L1_ffn_ref(x, sW1, sb1, sW2, sb2, sW3, sb3, eW1, eb1, eW2, eb2, eW3, eb3, gW, gb):
        import jax, jax.numpy as jnp
        import numpy as np
        B, A = (128, 8)
        IN, OUT = (256, 256)
        SH1, SH2 = (256, 128)
        EH1, EH2 = (128, 64)
        E, TOPK = (4, 2)

        def _shared_mlp(x, W1, b1, W2, b2, W3, b3):
            h = jax.nn.relu(x @ W1 + b1)
            h = jax.nn.relu(h @ W2 + b2)
            return h @ W3 + b3

        def _experts_mlp(x, eW1, eb1, eW2, eb2, eW3, eb3):
            h = jax.nn.relu(jnp.einsum('baf,efh->ebah', x, eW1) + eb1[:, None, None, :])
            h = jax.nn.relu(jnp.einsum('ebah,ehg->ebag', h, eW2) + eb2[:, None, None, :])
            o = jnp.einsum('ebag,ego->ebao', h, eW3) + eb3[:, None, None, :]
            return jnp.moveaxis(o, 0, -1)
        all_out = _experts_mlp(x, eW1, eb1, eW2, eb2, eW3, eb3)
        shared = _shared_mlp(x, sW1, sb1, sW2, sb2, sW3, sb3)
        gates = jax.nn.softmax(x @ gW + gb, axis=-1)
        topv, topi = jax.lax.top_k(gates, TOPK)
        topw = jax.nn.softmax(topv, axis=-1)
        sel = jnp.take_along_axis(all_out, topi[:, :, None, :], axis=-1)
        gated = jnp.sum(sel * topw[:, :, None, :], axis=-1)
        return shared + gated
    edge_index = jnp.stack([src, dst])
    x = x + _L0_gnn_ref(_layernorm(x, axis=-1), edge_index, L0_gnn_W, L0_gnn_a)
    x = x + _L0_ffn_ref(_layernorm(x, axis=-1)[None], L0_ffn_gate_w, L0_ffn_gate_b, L0_ffn_w1, L0_ffn_b1, L0_ffn_w2, L0_ffn_b2)[0]
    x = x + _L1_gnn_ref(_layernorm(x, axis=-1), L1_gnn_W_in, L1_gnn_b_in, L1_gnn_W_agg, L1_gnn_W_self, L1_gnn_b_hid, L1_gnn_W_out, L1_gnn_b_out, edge_index)
    x = x + _L1_ffn_ref(_layernorm(x, axis=-1)[None], L1_ffn_sW1, L1_ffn_sb1, L1_ffn_sW2, L1_ffn_sb2, L1_ffn_sW3, L1_ffn_sb3, L1_ffn_eW1, L1_ffn_eb1, L1_ffn_eW2, L1_ffn_eb2, L1_ffn_eW3, L1_ffn_eb3, L1_ffn_gW, L1_ffn_gb)[0]
    return x

_drawn_inputs = setup_inputs


def setup_inputs(seed=0):
    import zlib

    import numpy as np

    out = dict(_drawn_inputs(seed))
    spreads = {'L0_ffn_gate_b': (0.0, 0.1),
     'L0_ffn_b1': (0.0, 0.574),
     'L0_ffn_b2': (0.0, 0.42),
     'L1_gnn_b_in': (0.0, 0.1),
     'L1_gnn_b_hid': (0.0, 0.1),
     'L1_gnn_b_out': (0.0, 0.1),
     'L1_ffn_sb1': (0.0, 0.44),
     'L1_ffn_sb2': (0.0, 0.1),
     'L1_ffn_sb3': (0.0, 0.1),
     'L1_ffn_eb1': (0.0, 0.8),
     'L1_ffn_eb2': (0.0, 0.507),
     'L1_ffn_eb3': (0.0, 0.1),
     'L1_ffn_gb': (0.0, 0.445)}
    factors = {}
    for name, (base, spread) in spreads.items():
        noise = np.random.default_rng([zlib.crc32(name.encode()), seed]).standard_normal(out[name].shape)
        drawn = base * np.exp(spread * noise) if base else spread * noise
        out[name] = jnp.asarray(drawn.astype(out[name].dtype))
    for name, factor in factors.items():
        out[name] = (out[name] * factor).astype(out[name].dtype)
    return out
```

```python
from contextlib import ExitStack

import concourse.bass as bass
from concourse import mybir

F32 = mybir.dt.float32
F16 = mybir.dt.float16
BF16 = mybir.dt.bfloat16
I32 = mybir.dt.int32
U8 = mybir.dt.uint8
ALU = mybir.AluOpType
ACT = mybir.ActivationFunctionType
AX = mybir.AxisListType

P = 128
N = 3125
B = 125
NB = N // B
D = 256
KD = D // P
M = 53125
W = 5
NW = N // W
WB = B // W
EW = 128
EP = M // B
CB = 4
CN = CB * B
MAGIC = 1.5 * 2.0 ** 23
EPS = 1e-5


class Space:

    def __init__(self, nc):
        self.nc, self.ctx, self.sems = nc, ExitStack(), []

    def __enter__(self):
        return self

    def __exit__(self, *a):
        self.ctx.close()
        if self.sems:
            self.nc.clear_and_free_semaphores(self.sems)
            self.nc.all_engine_barrier()

    def sb(self, name, shape, dt=F32):
        return self.ctx.enter_context(self.nc.sbuf_tensor(name, list(shape), dt))

    def ps(self, name, shape, dt=F32):
        return self.ctx.enter_context(self.nc.psum_tensor(name, list(shape), dt))

    def sem(self, name):
        self.sems.append(self.nc.alloc_semaphore(name))
        return self.sems[-1]


def bc(ap, n, at):
    dims = [list(x) for x in ap.ap]
    dims.insert(at, [0, n])
    return bass.AP(ap.tensor, ap.offset, dims)


def split_dma(engine, out, in_, sem):
    for a, b in ((0, 112), (112, B)):
        engine.dma_start(out[a:b], in_[a:b]).then_inc(sem, 16)


def constants(nc, keep):
    c = {
        "ident": keep.sb("ident", [P, P]), "ident_h": keep.sb("ident_h", [P, P], F16),
        "iota_i": keep.sb("iota_i", [P, P], I32), "iota": keep.sb("iota", [P, P], BF16),
        "wbase_i": keep.sb("wbase_i", [B, W], I32), "wbase": keep.sb("wbase", [B, W]),
        "ones": keep.sb("ones", [P, P]), "ones_h": keep.sb("ones_h", [P, 1], F16),
    }
    return c


UN = 5


def gap(u, n):
    return next(d for d in range(1, UN + 1) if ((u - d) % UN) % n == u % n)


def blocks(engine, body):
    for u in range(UN):
        body(u, u, True)
    with engine.Fori(1, NB // UN) as i:
        for u in range(UN):
            body(UN * i + u, u, False)


def staggered(engine, *steps):
    lag = len(steps) - 1

    def turn(base, o, first):
        for d, step in enumerate(steps):
            t = base + o - d
            if isinstance(base, int) and not 0 <= t < NB:
                continue
            step(t, (o - d) % UN, first and t < UN)
    for o in range(UN + lag):
        turn(0, o, True)
    with engine.Fori(1, NB // UN - 1) as i:
        for o in range(lag, UN + lag):
            turn(UN * i, o, False)
    for o in range(lag, UN + lag + lag):
        turn(NB - UN, o, False)


def skip(t, u, first):
    pass


def chunks(engine, body):
    body(0, 0, CB)
    with engine.Fori(0, (NB // CB - 2) // 2) as i:
        body(2 * i + 1, 1, CB)
        body(2 * i + 2, 0, CB)
    body(NB // CB - 1, 1, CB)
    body(NB // CB, 0, NB % CB)


NC = NB // CB + 1


class Norm:

    def __init__(self, s, tag, stats):
        self.st = stats
        self.mean, self.dif, self.var, self.rstd, self.shift = (
            s.sb(tag + n, [B, NB]) for n in ("mean", "dif", "var", "rstd", "shift"))
        self.eps = s.sb(tag + "eps", [B, 1])
        self.xn = s.sb(tag + "xn", [B, UN, D])
        self.xt = s.sb(tag + "xt", [P, UN, KD, B])
        self.pt = [s.ps(f"{tag}pt{i}", [P, KD, B]) for i in range(3)]
        self.s_v, self.s_var, self.s_std, self.s_rstd, self.s_xn, self.s_tr, self.s_xt, self.s_used = (
            s.sem(tag + n) for n in ("v", "var", "std", "rstd", "sxn", "str", "sxt", "used"))

    def stats(self, nc, dve):
        v = nc.vector
        m1, q1, m2, q2 = (self.st[:, :, i] for i in (1, 2, 4, 5))
        v.memset(self.eps[:], EPS)
        v.tensor_tensor(self.mean[:], m1, m2, ALU.add)
        v.tensor_tensor(self.dif[:], m1, m2, ALU.subtract)
        v.tensor_tensor(self.var[:], q1, q2, ALU.add).then_inc(self.s_v, 1)
        dve.wait_ge(self.s_v, 1)
        v.tensor_scalar(self.mean[:], self.mean[:], 0.5, None, ALU.mult)
        v.tensor_scalar(self.var[:], self.var[:], 1.0 / D, None, ALU.mult)
        v.scalar_tensor_tensor(self.dif[:], self.dif[:], 0.25, self.dif[:], ALU.mult, ALU.mult).then_inc(self.s_v, 1)
        dve.wait_ge(self.s_v, 2)
        v.tensor_tensor(self.var[:], self.var[:], self.dif[:], ALU.add).then_inc(self.s_var, 1)
        dve.wait_ge(self.s_std, 1)
        v.reciprocal(self.rstd[:], self.dif[:]).then_inc(self.s_v, 1)
        dve.wait_ge(self.s_v, 3)
        v.scalar_tensor_tensor(self.shift[:], self.mean[:], -1.0, self.rstd[:], ALU.mult, ALU.mult).then_inc(self.s_rstd, 1)

    def std(self, nc, act):
        act.wait_ge(self.s_var, 1)
        nc.scalar.activation(self.dif[:], self.var[:], ACT.Sqrt, bias=self.eps[:, 0:1]).then_inc(self.s_std, 1)
        act.wait_ge(self.s_rstd, 1)

    def rows(self, nc, act, X, t, u, first):
        if not first:
            act.wait_ge(self.s_tr, t - UN + 1)
        nc.scalar.activation(self.xn[:, u, :], X[:, t, :], ACT.Identity, bias=self.shift[:, bass.ds(t, 1)],
                             scale=self.rstd[:, bass.ds(t, 1)]).then_inc(self.s_xn, 1)

    def turn(self, nc, pe, ident, t, u, first):
        pe.wait_ge(self.s_xn, t + 1)
        if not first or u >= 3:
            pe.wait_ge(self.s_xt, t - gap(u, 3) + 1)
        for k in range(KD):
            tr = nc.tensor.transpose(self.pt[u % 3][:, k, :], self.xn[:, u, k * P:(k + 1) * P], ident[0:B, 0:B])
        tr.then_inc(self.s_tr, 1)

    def out(self, nc, dve, t, u, first):
        if not first:
            dve.wait_ge(self.s_used, t - UN + 1)
        dve.wait_ge(self.s_tr, t + 1)
        return nc.vector.tensor_copy(self.xt[:, u, :, :], self.pt[u % 3][:]).then_inc(self.s_xt, 1)


class AttentionRows:

    def __init__(self, nc, s, io, c, X, ph, pw, norm):
        self.nc, self.io, self.c, self.X, self.ph, self.pw, self.norm = nc, io, c, X, ph, pw, norm
        self.st_cols = s.sb("st_cols", [B, NB, 2])
        self.s_col = s.sb("s_col", [B, NB])
        self.s_rows = s.sb("s_rows", [NB, B])
        self.w_cat = s.sb("w_cat", [P, KD, D + 2])
        self.w_t = s.sb("w_t", [P, KD, D])
        self.a_row = s.sb("a_row", [2 * KD, P])
        self.a_cols = s.sb("a_cols", [P, 2 * KD])
        (self.s_st, self.s_w, self.s_h1, self.s_fin, self.s_srow, self.s_wt, self.s_acol, self.s_wa, self.s_wcat, self.s_x,
         self.s_m, self.s_wl, self.s_al, self.s_so) = (
            s.sem("C_" + n) for n in ("st", "w", "h1", "fin", "srow", "wt", "acol", "wa", "wcat", "x", "m", "wl", "al", "so"))

    def load(self, sp):
        split_dma(sp, self.X[:], self.io["x"].rearrange("(t p) d -> p t d", p=B), self.s_x)
        sp.dma_start(self.w_cat[:, :, 0:D], self.io["L0_gnn_W"].rearrange("(k p) f -> p k f", p=P)).then_inc(self.s_wl, 16)
        sp.dma_start(self.a_row[:], self.io["L0_gnn_a"].rearrange("(r p) -> r p", p=P)).then_inc(self.s_al, 16)

    def store(self, sp):
        sp.wait_ge(self.s_srow, 1)
        sp.dma_start(self.io["s_dram"].rearrange("(b n) -> b n", n=B), self.s_rows[:]).then_inc(self.s_so, 16)
        sp.wait_ge(self.s_so, 16)

    def vector(self, dve):
        nc, io, norm, X, ph, pw = self.nc, self.io, self.norm, self.X, self.ph, self.pw
        v, w_cat, st_cols, h1 = nc.vector, self.w_cat, self.st_cols, io["h1"]
        dve.wait_ge(self.s_x, 32)
        with dve.Fori(0, NB) as t:
            v.bn_stats(io["stats"][:, t, :], X[:, t, :]).then_inc(self.s_m, 1)
        dve.wait_ge(self.s_m, NB)
        norm.stats(nc, dve)
        dve.wait_ge(self.s_wt, 1)
        v.tensor_copy(self.a_cols[:], pw[:, 0:2 * KD]).then_inc(self.s_acol, 1)
        for k in range(KD):
            dve.wait_ge(self.s_wt, 2 + k)
            v.tensor_copy(self.w_t[:, :, k * P:(k + 1) * P], pw[:, 0:KD * P].rearrange("p (f i) -> p f i", f=KD)).then_inc(self.s_acol, 1)
        dve.wait_ge(self.s_wa, 1)
        v.tensor_copy(w_cat[:, :, D:D + 2], pw[:, 0:2 * KD].rearrange("p (k a) -> p k a", a=2)).then_inc(self.s_wcat, 1)

        def out(t, u, first):
            norm.out(nc, dve, t, u, first)

        def columns(t, u, first):
            dve.wait_ge(norm.s_used, t + 1)
            v.tensor_copy(st_cols[:, t, :], ph[u % 3][:, D:D + 2]).then_inc(self.s_st, 1)

        def weighted(t, u, first):
            dve.wait_ge(self.s_w, t + 1)
            v.tensor_scalar(h1[:, t, 0:D], ph[u % 3][:, 0:D], h1[:, t, D:D + 1], None, ALU.mult).then_inc(self.s_h1, 1)
        staggered(dve, out, columns, weighted)
        v.tensor_copy(self.s_col[:], st_cols[:, :, 0]).then_inc(self.s_fin, 1)
        v.tensor_scalar(io["t_bias"][:], st_cols[:, :, 1], -0.8, None, ALU.mult)
        dve.wait_ge(self.s_fin, 2)
        v.tensor_copy(self.s_rows[:], pw[0:NB, 0:B]).then_inc(self.s_srow, 1)

    def scalar(self, act):
        nc, io, norm, X = self.nc, self.io, self.norm, self.X
        st_cols, h1 = self.st_cols, io["h1"]
        norm.std(nc, act)

        def body(t, u, first):
            norm.rows(nc, act, X, t, u, first)

        def weight(t, u, first):
            act.wait_ge(self.s_st, t + 1)
            nc.scalar.activation(h1[:, t, D:D + 1], st_cols[:, t, 1:2], ACT.Exp, scale=-0.2).then_inc(self.s_w, 1)
        staggered(act, body, skip, weight)

    def tensor(self, pe):
        nc, norm, c, ph, pw = self.nc, self.norm, self.c, self.ph, self.pw
        t_, w_cat = nc.tensor, self.w_cat
        pe.wait_ge(self.s_al, 16)
        pe.wait_ge(self.s_wl, 16)
        t_.transpose(pw[:, 0:2 * KD], self.a_row[:], c["ident"][0:2 * KD, 0:2 * KD]).then_inc(self.s_wt, 1)
        for k in range(KD):
            pe.wait_ge(self.s_acol, 1 + k)
            for f in range(KD):
                tr = t_.transpose(pw[:, f * P:(f + 1) * P], w_cat[:, k, f * P:(f + 1) * P], c["ident"][:])
            tr.then_inc(self.s_wt, 1)
        pe.wait_ge(self.s_acol, 1 + KD)
        for k in range(KD):
            for f in range(KD):
                mm = t_.matmul(pw[:, 2 * k:2 * k + 2], self.w_t[:, f, k * P:(k + 1) * P],
                               self.a_cols[:].rearrange("p (a f) -> p f a", f=KD)[:, f, :], start=(f == 0), stop=(f == KD - 1))
        mm.then_inc(self.s_wa, 1)
        pe.wait_ge(self.s_wcat, 1)

        def turn(t, u, first):
            norm.turn(nc, pe, c["ident"], t, u, first)

        def body(t, u, first):
            pe.wait_ge(norm.s_xt, t + 1)
            if not first or u >= 3:
                pe.wait_ge(self.s_h1, t - gap(u, 3) + 1)
            for k in range(KD):
                mm = t_.matmul(ph[u % 3][:], norm.xt[:, u, k, :], w_cat[:, k, :], start=(k == 0), stop=(k == KD - 1))
            mm.then_inc(norm.s_used, 1)
        staggered(pe, turn, body)
        pe.wait_ge(self.s_fin, 1)
        t_.transpose(pw[0:NB, 0:B], self.s_col[:], c["ident"][0:B, 0:B]).then_inc(self.s_fin, 1)


def edge_windows(nc, io, c, keep, X):
    with Space(nc) as s:
        src_i, dst_i = (s.sb(n, [B, EP], I32) for n in ("src_i", "dst_i"))
        srcf, dstf = keep["srcf"], keep["dstf"]
        quot, rest, wrest, tmp = (s.sb(n, [B, EP]) for n in ("quot", "rest", "wrest", "tmp"))
        quot_b, wrest_b = s.sb("quot_b", [B, EP], BF16), s.sb("wrest_b", [B, EP, 2], BF16)
        oh_q, oh_w = s.sb("oh_q", [B, EP, NB], BF16), s.sb("oh_w", [B, EP, NB + 1], BF16)
        blk = s.sb("blk", [B, W, NB])
        picked = s.sb("picked", [B, W, NB])
        hist = s.sb("hist", [B, NB])
        hist_in = s.sb("hist_in", [B, NB])
        hist_ex = s.sb("hist_ex", [B, NB])
        hist_all = s.sb("hist_all", [B, 1])
        hist_rows = s.sb("hist_rows", [B, NB])
        zero25 = s.sb("zero25", [B, NB])
        sel, sel_in, sel_lt = (s.sb(n, [B, NB]) for n in ("sel", "sel_in", "sel_lt"))
        starts_f = s.sb("starts_f", [NB, WB])
        starts_i = s.sb("starts_i", [NB, WB], I32)
        start = s.sb("start", [B, W], I32)
        g_src, g_dst = (s.sb(n, [B, W, EW], I32) for n in ("g_src", "g_dst"))
        gs, gd, ghi, g1, g2 = (s.sb(n, [B, W, EW]) for n in ("gs", "gd", "ghi", "g1", "g2"))
        held = s.sb("held", [B, 1])
        norm = Norm(s, "n1", io["stats"])
        nodes = AttentionRows(nc, s, io, c, X, [s.ps(f"ph{i}", [B, D + 2]) for i in range(3)], s.ps("pw", [P, 512]), norm)
        ph = s.ps("hist_pairs", [B, W, NB])
        pst = nodes.pw[0:NB, 0:WB]
        pcnt = nodes.pw[:, WB:WB + 1]
        pt = [norm.pt[i][:].rearrange("p k b -> p (k b)") for i in range(2)]
        s_dst, s_src, s_const, s_conv, s_oh, s_hist = (s.sem("A_" + n) for n in ("dst", "src", "const", "conv", "oh", "hist"))
        s_v, s_st, s_starts, s_stout, s_stin = (s.sem("A_" + n) for n in ("v", "st", "starts", "stout", "stin"))
        s_gs, s_gd = ([s.sem(f"A_{n}{k}") for k in range(W)] for n in ("gs", "gd"))
        s_code, s_tr, s_tc, s_cnt, s_id, s_zero = (s.sem("A_" + n) for n in ("code", "tr", "tc", "cnt", "id", "zero"))
        starts_dram = io["starts_dram"]
        groups = [(e, min(e + 85, EP)) for e in range(0, EP, 85)]

        with nc.Block() as block:
            @block.sync
            def _(sp):
                sp.dma_start(dst_i[:], io["dst"].rearrange("(p e) -> p e", p=B)).then_inc(s_dst, 16)
                sp.dma_start(src_i[:], io["src"].rearrange("(p e) -> p e", p=B)).then_inc(s_src, 16)
                nodes.load(sp)
                sp.wait_ge(s_zero, 1)
                for k in range(4):
                    sp.dma_start(io["buf_dram"].rearrange("(k p r) d -> k p (r d)", k=4, p=P)[k],
                                 keep["zeros"][:]).then_inc(io["s_buf_zero"], 16)
                sp.wait_ge(s_starts, 1)
                sp.dma_start(starts_dram.rearrange("(q w) -> q w", q=NB), starts_i[:]).then_inc(s_stout, 16)
                sp.wait_ge(s_stout, 16)
                sp.dma_start(start[:], starts_dram.rearrange("(p k) -> p k", k=W)).then_inc(s_stin, 16)
                nodes.store(sp)
                sp.wait_ge(io["s_buf_zero"], 64)

            @block.gpsimd
            def _(pool):
                g = nc.gpsimd
                g.iota(c["iota_i"][:], [[1, P]], base=0, channel_multiplier=0).then_inc(s_const, 1)
                g.iota(c["wbase_i"][:], [[W, W]], base=0, channel_multiplier=W * W).then_inc(s_const, 1)
                g.memset(c["ident"][:], 0.0).then_inc(s_id, 1)
                g.memset(blk[:], 1.0).then_inc(s_id, 1)
                pool.wait_ge(s_id, 2)
                g.affine_select(out=c["ident"][:], in_=c["ident"][:], compare_op=ALU.not_equal, fill=1.0, base=0,
                                pattern=[[-1, P]], channel_multiplier=1).then_inc(s_const, 1)
                g.affine_select(out=blk[:], in_=blk[:], compare_op=ALU.is_ge, fill=0.0, base=0,
                                pattern=[[-NB, W], [0, NB]], channel_multiplier=1).then_inc(s_id, 1)
                pool.wait_ge(s_id, 3)
                g.affine_select(out=blk[:], in_=blk[:], compare_op=ALU.is_ge, fill=0.0, base=NB - 1,
                                pattern=[[NB, W], [0, NB]], channel_multiplier=-1).then_inc(s_const, 1)
                g.memset(keep["zeros"][:], 0.0).then_inc(s_zero, 1)
                pool.wait_ge(s_stin, 16)
                for k in range(W):
                    for ids, got, sg in ((io["dst"], g_dst, s_gd), (io["src"], g_src, s_gs)):
                        g.indirect_dma_start(got[:, k, :], None, ids.rearrange("(m o) -> m o", o=1),
                                             bass.IndirectOffsetOnAxis(ap=start[:, k:k + 1], axis=0)
                                             ).then_inc(sg[k], 16)
                for k in range(W):
                    pool.wait_ge(s_gd[k], 16)
                    pool.wait_ge(s_gs[k], 16)

            @block.vector
            def _(dve):
                v = nc.vector
                n = [0]

                def step(ins):
                    n[0] += 1
                    ins.then_inc(s_v, 1)
                    dve.wait_ge(s_v, n[0])

                def floor_div(out, x, t, by):
                    step(v.tensor_scalar(t, x, float(-(by // 2)), 1.0 / by, ALU.add, ALU.mult))
                    step(v.tensor_scalar(t, t, MAGIC, None, ALU.add))
                    step(v.tensor_scalar(out, t, -MAGIC, None, ALU.add))

                v.memset(c["ones"][:], 1.0)
                v.memset(c["ones_h"][:], 1.0)
                dve.wait_ge(s_const, 4)
                v.tensor_copy(c["ident_h"][:], c["ident"][:])
                v.tensor_copy(c["wbase"][:], c["wbase_i"][:])
                step(v.tensor_copy(c["iota"][:], c["iota_i"][:]))
                dve.wait_ge(s_dst, 16)
                step(v.tensor_copy(dstf[:], dst_i[:]))
                floor_div(quot[:], dstf[:], tmp[:], B)
                step(v.scalar_tensor_tensor(rest[:], quot[:], float(-B), dstf[:], ALU.mult, ALU.add))
                floor_div(wrest[:], rest[:], tmp[:], W)
                v.tensor_copy(quot_b[:], quot[:])
                step(v.tensor_copy(wrest_b[:], bc(wrest[:], 2, 2)))
                for a, b in groups:
                    v.tensor_tensor(oh_q[:, a:b, :], bc(quot_b[:, a:b], NB, 2), bc(c["iota"][0:B, 0:NB], b - a, 1), ALU.is_equal)
                    ins = v.tensor_tensor(oh_w[:, a:b, :].rearrange("p e (q r) -> p e q r", r=2),
                                          bc(wrest_b[:, a:b, :], (NB + 1) // 2, 2),
                                          bc(c["iota"][0:B, 0:NB + 1].rearrange("p (q r) -> p q r", r=2), b - a, 1),
                                          ALU.is_equal)
                    ins.then_inc(s_oh, 1)
                dve.wait_ge(s_src, 16)
                step(v.tensor_copy(srcf[:], src_i[:]))
                step(v.tensor_reduce(sel[:], c["ident"][0:B, 0:B].rearrange("p (a q) -> p q a", q=NB), AX.X, ALU.add))
                step(v.memset(zero25[:], 0.0))
                step(v.tensor_tensor_scan(sel_in[:], sel[:], zero25[:], 0.0, ALU.add, ALU.add))
                step(v.tensor_tensor(sel_lt[:], sel_in[:], sel[:], ALU.subtract))
                dve.wait_ge(s_hist, 1)
                step(v.tensor_tensor(picked[:], ph[:], blk[:], ALU.mult))
                step(v.tensor_reduce(hist[:], picked[:].rearrange("p a w -> p w a"), AX.X, ALU.add))
                step(v.tensor_reduce(hist_all[:], hist[:], AX.X, ALU.add))
                step(v.tensor_scalar(hist_rows[:], zero25[:], hist_all[:, 0:1], None, ALU.add))
                step(v.tensor_tensor_scan(hist_in[:], hist[:], zero25[:], 0.0, ALU.add, ALU.add))
                v.tensor_tensor(hist_ex[:], hist_in[:], hist[:], ALU.subtract).then_inc(s_st, 1)
                dve.wait_ge(s_st, 2)
                step(v.tensor_scalar(starts_f[:], pst, float(M - EW), None, ALU.min))
                v.tensor_copy(starts_i[:], starts_f[:]).then_inc(s_starts, 1)
                nodes.vector(dve)
                for k in range(W):
                    dve.wait_ge(s_gd[k], 16)
                    dve.wait_ge(s_gs[k], 16)
                step(v.tensor_copy(gs[:], g_src[:]))
                step(v.tensor_copy(gd[:], g_dst[:]))
                floor_div(ghi[:], gs[:], g1[:], B)
                step(v.scalar_tensor_tensor(gs[:], ghi[:], float(-B), gs[:], ALU.mult, ALU.add))
                step(v.tensor_tensor(gd[:], gd[:], bc(c["wbase"][:], EW, 2), ALU.subtract))
                step(v.tensor_scalar(g1[:], gd[:], 0.0, None, ALU.is_ge))
                step(v.tensor_scalar(g2[:], gd[:], float(W - 1), None, ALU.is_le))
                step(v.tensor_tensor(g1[:], g1[:], g2[:], ALU.mult))
                v.tensor_reduce(held[:], g1[:], AX.XY, ALU.add).then_inc(s_cnt, 1)
                step(v.scalar_tensor_tensor(ghi[:], ghi[:], float(W), gd[:], ALU.mult, ALU.add))
                step(v.tensor_scalar(ghi[:], ghi[:], 1.0, None, ALU.add))
                step(v.tensor_tensor(ghi[:], ghi[:], g1[:], ALU.mult))
                v.tensor_scalar(ghi[:], ghi[:], -1.0, None, ALU.add).then_inc(s_code, 1)
                for i in range(2 * W):
                    dve.wait_ge(s_tr, i + 1)
                    out = keep["lo"] if i % 2 == 0 else keep["code"]
                    v.tensor_copy(out[:].rearrange("e (p k) r -> e p k r", k=W)[:, :, i // 2, :], bc(pt[i % 2][0:EW, 0:B], 2, 2)).then_inc(s_tc, 1)
                dve.wait_ge(s_cnt, 2)
                v.tensor_copy(keep["captured"][:], pcnt[0:1, :])

            @block.scalar
            def _(act):
                nodes.scalar(act)

            @block.tensor
            def _(pe):
                t = nc.tensor
                per = EP // W
                for g, (a, b) in enumerate(groups):
                    pe.wait_ge(s_oh, g + 1)
                    for e in range(a, b, W):
                        mm = t.matmul(ph[:].rearrange("p a w -> p (a w)"), oh_q[:, e:e + W, :].rearrange("p e q -> p (e q)"),
                                      oh_w[:, e:e + W, 0:NB], start=(e == 0), stop=(e == EP - W))
                mm.then_inc(s_hist, 1)
                pe.wait_ge(s_st, 1)
                t.matmul(pst, sel[:], hist_ex[:], start=True, stop=False)
                t.matmul(pst, sel_lt[:], hist_rows[:], start=False, stop=True).then_inc(s_st, 1)
                pe.wait_ge(s_starts, 1)
                nodes.tensor(pe)
                pe.wait_ge(s_cnt, 1)
                t.matmul(pcnt, c["ones"][0:B, :], held[:], start=True, stop=True).then_inc(s_cnt, 1)
                pe.wait_ge(s_code, 1)
                for i in range(2 * W):
                    if i >= 2:
                        pe.wait_ge(s_tc, i - 1)
                    t.transpose(pt[i % 2][0:EW, 0:B], (gs if i % 2 == 0 else ghi)[:, i // 2, :],
                                c["ident"][0:B, 0:B]).then_inc(s_tr, 1)


def count_matrix(nc, io, c, keep):
    with Space(nc) as s:
        oh_lo, oh_code = (s.sb(n, [EW, 2, WB, P], BF16) for n in ("oh_lo", "oh_code"))
        ai = s.sb("ai", [B, 2, NB, B], F16)
        at = s.sb("at", [B, 2, N], F16)
        degs = s.sb("degs", [B, NB])
        dinv = s.sb("dinv", [B, NB])
        dinv_t = s.sb("dinv_t", [NB, B])
        count = [s.ps(f"count{i}", [P, CB, B]) for i in range(3)]
        turned = [s.ps(f"turned{i}", [B, 8, P], F16) for i in range(4)]
        small = s.ps("small", [P, 2 * P + NB])
        pdeg = small[0:B, 2 * P:]
        pdt = small[0:NB, 0:B]
        s_oh, s_mm, s_ai, s_tr, s_at, s_deg, s_degacc, s_fin = (
            s.sem("B_" + n) for n in ("oh", "mm", "ai", "tr", "at", "deg", "degacc", "fin"))
        s_store = [s.sem(f"B_store{i}") for i in range(2)]
        s_dinv = s.sem("B_dinv")
        lo_v = keep["lo"][:].rearrange("e (b w) r -> e b w r", w=WB)
        code_v = keep["code"][:].rearrange("e (b w) r -> e b w r", w=WB)
        at_rows = io["AT_dram"].rearrange("(b j) i -> b j i", j=B)
        wgroups = [(w, min(w + CB, WB)) for w in range(0, WB, CB)]
        tgroups = [(h, min(h + 8, NB)) for h in range(0, NB, 8)]
        NG, NT = len(wgroups), len(tgroups)
        captured = keep["captured"][0:1, 0:1]

        src_row = s.sb("src_row", [B, N])
        src_row_i = s.sb("src_row_i", [B, N], I32)
        dst_rel = s.sb("dst_rel", [B, EP])
        oh_src = s.sb("oh_src", [B, 2, N], BF16)
        oh_dst = s.sb("oh_dst", [B, 2, B], BF16)
        g_iota, g_row, g_rel, g_oh, g_mm, g_done, g_at = (s.sem("G_" + n) for n in ("iota", "row", "rel", "oh", "mm", "done", "at"))
        cgroups = [(i, min(i + CB, NB)) for i in range(0, NB, CB)]

        def bank(i):
            if i < 3:
                return count[i][0:B].rearrange("j w n -> j (w n)")
            if i < 6:
                return turned[i - 3][:].rearrange("j b n -> j (b n)").bitcast(F32)
            return small[0:B, P:P + B]

        with nc.Block() as block:
            @block.vector
            def _(dve):
                v = nc.vector
                nv = 0

                def one_hots(jb, k, first):
                    if not first:
                        dve.wait_ge(s_mm, NG * (jb - 1))
                    for a, b in wgroups:
                        for oh, code in ((oh_lo, lo_v), (oh_code, code_v)):
                            ins = v.tensor_tensor(oh[:, k, a:b, :].rearrange("e w (n r) -> e w n r", r=2),
                                                  bc(code[:, jb, a:b, :], P // 2, 2),
                                                  bc(c["iota"][:].rearrange("e (n r) -> e n r", r=2), b - a, 1), ALU.is_equal)
                        ins.then_inc(s_oh, 1)

                def rows(jb, k, first):
                    if not first:
                        dve.wait_ge(s_store[k], 32 * (jb // 2) if isinstance(jb, int) else 32 * jb_half[0])
                        dve.wait_ge(s_deg, jb - 1)
                    for i, (a, b) in enumerate(tgroups):
                        dve.wait_ge(s_tr, NT * jb + i + 1)
                        v.tensor_copy(at[:, k, a * B:b * B].rearrange("j (h n) -> j h n", n=B),
                                      turned[i][:, 0:b - a, 0:B]).then_inc(s_at, 1)

                def degrees(jb, k):
                    dve.wait_ge(s_deg, jb + 1)
                    dve.wait_ge(s_degacc, jb + 1)
                    v.tensor_tensor(degs[:], pdeg, degs[:], ALU.add).then_inc(s_degacc, 1)

                v.memset(degs[:], 0.0).then_inc(s_degacc, 1)
                how = dve.value_load(captured, min_val=0, max_val=M)
                jb_half = [None]
                with dve.If(how == M):
                    one_hots(0, 0, True)
                    one_hots(1, 1, True)
                    rows(0, 0, True)
                    one_hots(2, 0, False)
                    rows(1, 1, True)
                    degrees(0, 0)
                    with dve.Fori(0, 11) as h:
                        one_hots(2 * h + 3, 1, False)
                        jb_half[0] = h + 1
                        rows(2 * h + 2, 0, False)
                        degrees(2 * h + 1, 1)
                        one_hots(2 * h + 4, 0, False)
                        rows(2 * h + 3, 1, False)
                        degrees(2 * h + 2, 0)
                    rows(24, 0, False)
                    degrees(23, 1)
                    degrees(24, 0)
                with dve.If(how != M):
                    dve.wait_ge(g_iota, 1)
                    v.tensor_copy(src_row[:], src_row_i[:]).then_inc(g_row, 1)
                    v.tensor_copy(dst_rel[:], keep["dstf"][:]).then_inc(g_row, 1)
                    dve.wait_ge(g_row, 2)
                    with dve.Fori(0, NB) as jb:
                        def pair(e, k, first):
                            if not first:
                                dve.wait_ge(g_mm, jb * EP + e - 1)
                            v.tensor_scalar(oh_dst[:, k, :], c["iota"][0:B, 0:B], dst_rel[:, bass.ds(e, 1)], None, ALU.is_equal)
                            v.tensor_scalar(oh_src[:, k, :], src_row[:], keep["srcf"][:, bass.ds(e, 1)], None, ALU.is_equal).then_inc(g_oh, 1)
                        pair(0, 0, True)
                        pair(1, 1, True)
                        pair(2, 0, False)
                        with dve.Fori(0, (EP - 3) // 2) as h:
                            pair(2 * h + 3, 1, False)
                            pair(2 * h + 4, 0, False)
                        dve.wait_ge(g_mm, (jb + 1) * EP)
                        v.tensor_scalar(dst_rel[:], dst_rel[:], float(-B), None, ALU.add).then_inc(g_rel, 1)
                        dve.wait_ge(g_rel, jb + 1)
                        dve.wait_ge(s_deg, jb + 1)
                        v.tensor_tensor(degs[:], pdeg, degs[:], ALU.add).then_inc(s_degacc, 1)
                        dve.wait_ge(s_degacc, jb + 2)
                dve.wait_ge(s_degacc, NB + 1)
                v.tensor_scalar(degs[:], degs[:], 1.0, None, ALU.max).then_inc(s_fin, 1)
                dve.wait_ge(s_fin, 1)
                v.reciprocal(dinv[:], degs[:]).then_inc(s_fin, 1)
                dve.wait_ge(s_fin, 3)
                v.tensor_copy(dinv_t[:], pdt).then_inc(s_fin, 1)

            @block.scalar
            def _(act):
                a_ = nc.scalar

                def counts(jb, k, first):
                    if not first:
                        act.wait_ge(s_tr, NT * (jb - 1))
                    for i, (a, b) in enumerate(wgroups):
                        act.wait_ge(s_mm, NG * jb + i + 1)
                        a_.activation(ai[:, k, :, a * W:b * W].rearrange("n h (w d) -> n w h d", d=W),
                                      count[i % 3][0:B, 0:b - a, :].rearrange("n w (h d) -> n w h d", d=W),
                                      ACT.Copy).then_inc(s_ai, 1)

                how = act.value_load(captured, min_val=0, max_val=M)
                with act.If(how == M):
                    counts(0, 0, True)
                    counts(1, 1, True)
                    counts(2, 0, False)
                    with act.Fori(0, 11) as h:
                        counts(2 * h + 3, 1, False)
                        counts(2 * h + 4, 0, False)
                with act.If(how != M):
                    with act.Fori(0, NB) as jb:
                        act.wait_ge(g_done, jb + 1)
                        for i, (a, b) in enumerate(cgroups):
                            ins = a_.activation(at[:, 0, a * B:b * B], bank(i)[:, 0:(b - a) * B], ACT.Copy)
                        ins.then_inc(g_at, 1)
                        act.wait_ge(s_store[0], 32 * (jb + 1))

            @block.tensor
            def _(pe):
                t = nc.tensor

                def before(jb, i):
                    return NG * jb + i - 2 if i >= 3 else NG * (jb - 1) + max(g for g in range(NG) if g % 3 == i) + 1

                def windows(jb, k):
                    for i, (a, b) in enumerate(wgroups):
                        pe.wait_ge(s_oh, NG * jb + i + 1)
                        if i >= 3 or not (isinstance(jb, int) and jb == 0):
                            pe.wait_ge(s_ai, before(jb, i))
                        for w in range(a, b):
                            mm = t.matmul(count[i % 3][:, w - a, :], oh_lo[:, k, w, :], oh_code[:, k, w, 0:B], start=True, stop=True)
                        mm.then_inc(s_mm, 1)

                def turn(jb, k):
                    pe.wait_ge(s_ai, NG * (jb + 1))
                    for i, (a, b) in enumerate(tgroups):
                        if not (isinstance(jb, int) and jb == 0):
                            pe.wait_ge(s_at, NT * (jb - 1) + i + 1)
                        for h in range(a, b):
                            mm = t.transpose(turned[i][:, h - a, 0:B], ai[:, k, h, :], c["ident_h"][0:B, 0:B])
                        mm.then_inc(s_tr, 1)

                def degree(jb, k):
                    pe.wait_ge(s_at, NT * (jb + 1))
                    pe.wait_ge(s_degacc, jb + 1)
                    for h in range(NB):
                        mm = t.matmul(pdeg[:, h:h + 1], at[:, k, h * B:(h + 1) * B], c["ones_h"][0:B, :], start=True, stop=True)
                    mm.then_inc(s_deg, 1)

                how = pe.value_load(captured, min_val=0, max_val=M)
                with pe.If(how == M):
                    windows(0, 0)
                    turn(0, 0)
                    windows(1, 1)
                    turn(1, 1)
                    degree(0, 0)
                    windows(2, 0)
                    with pe.Fori(0, 11) as h:
                        turn(2 * h + 2, 0)
                        windows(2 * h + 3, 1)
                        degree(2 * h + 1, 1)
                        turn(2 * h + 3, 1)
                        windows(2 * h + 4, 0)
                        degree(2 * h + 2, 0)
                    turn(24, 0)
                    degree(23, 1)
                    degree(24, 0)
                with pe.If(how != M):
                    with pe.Fori(0, NB) as jb:
                        def chunk(e, k, start=False, stop=False):
                            pe.wait_ge(g_oh, jb * EP + e + 1)
                            for i, (a, b) in enumerate(cgroups):
                                mm = t.matmul(bank(i)[:, 0:(b - a) * B], oh_dst[:, k, :], oh_src[:, k, a * B:b * B],
                                              start=start, stop=stop)
                            mm.then_inc(g_mm, 1)
                            return mm
                        chunk(0, 0, start=True)
                        with pe.Fori(0, (EP - 3) // 2) as h:
                            chunk(2 * h + 1, 1)
                            chunk(2 * h + 2, 0)
                        chunk(EP - 2, 1)
                        chunk(EP - 1, 0, stop=True)
                        pe.drain().then_inc(g_done, 1)
                        pe.wait_ge(g_at, jb + 1)
                        for h in range(NB):
                            mm = t.matmul(pdeg[:, h:h + 1], at[:, 0, h * B:(h + 1) * B], c["ones_h"][0:B, :], start=True, stop=True)
                        mm.then_inc(s_deg, 1)
                pe.wait_ge(s_fin, 2)
                t.transpose(pdt, dinv[:], c["ident"][0:B, 0:B]).then_inc(s_fin, 1)

            @block.gpsimd
            def _(pool):
                how = pool.value_load(captured, min_val=0, max_val=M)
                with pool.If(how != M):
                    nc.gpsimd.iota(src_row_i[:], [[1, N]], base=0, channel_multiplier=0).then_inc(g_iota, 1)

            @block.sync
            def _(sp):
                how = sp.value_load(captured, min_val=0, max_val=M)
                with sp.If(how == M):
                    with sp.Fori(0, 12) as h:
                        for k in range(2):
                            sp.wait_ge(s_at, NT * (2 * h + k + 1))
                            split_dma(sp, at_rows[2 * h + k], at[:, k, :], s_store[k])
                    sp.wait_ge(s_at, NT * NB)
                    split_dma(sp, at_rows[NB - 1], at[:, 0, :], s_store[0])
                    sp.wait_ge(s_store[0], 32 * 13)
                    sp.wait_ge(s_store[1], 32 * 12)
                with sp.If(how != M):
                    with sp.Fori(0, NB) as jb:
                        sp.wait_ge(g_at, jb + 1)
                        split_dma(sp, at_rows[jb], at[:, 0, :], s_store[0])
                    sp.wait_ge(s_store[0], 32 * NB)
                sp.wait_ge(s_fin, 4)
                sp.dma_start(io["dinv_dram"].rearrange("(b n) -> b n", n=B), dinv_t[:]).then_inc(s_dinv, 16)
                sp.wait_ge(s_dinv, 16)


def graph_attention(nc, io, c, X):
    HW = D + 1
    with Space(nc) as s:
        h1, t_bias = io["h1"], io["t_bias"]
        s_part = s.sb("s_part", [B, 2, CN])
        a_chunk = s.sb("a_chunk", [B, 2, NB, CN], F16)
        s_sl, s_chunk = ([s.sem(f"C_{n}{i}") for i in range(2)] for n in ("sl", "chunk"))
        s_first = [s.sem(f"C_first{i}") for i in range(NB // UN)]
        s_exp, s_e, s_mm, s_rs, s_o, s_res = (s.sem("C_" + n) for n in ("exp", "e", "mm", "rs", "o", "res"))
        at_v = io["AT_dram"].rearrange("(b j) i -> j b i", j=B)

        def loads(c_, k, loop):
            return c_ // 2 + 1 if isinstance(c_, int) else loop[0] + 1 + (1 - k)

        with Space(nc) as s2:
            et, e = (s2.sb(n, [B, UN, CN]) for n in ("et", "e"))
            rs = s2.sb("rs", [B, 2, CB])
            o = s2.sb("o", [B, 2, CB, D])
            acc = [[s2.ps(f"acc{k}_{b}", [B, HW]) for b in range(CB)] for k in range(2)]
            with nc.Block() as block:
                @block.sync
                def _(sp):
                    sp.dma_start(s_part[:, 0], bc(io["s_dram"][0:CN], B, 0)).then_inc(s_sl[0], 16)
                    for i, sem in enumerate(s_first):
                        js = slice(UN * i, UN * (i + 1))
                        split_dma(sp, a_chunk[:, 0, js, :], at_v[:, js, 0:CN], sem)
                    sp.dma_start(s_part[:, 1], bc(io["s_dram"][CN:2 * CN], B, 0)).then_inc(s_sl[1], 16)
                    split_dma(sp, a_chunk[:, 1], at_v[:, :, CN:2 * CN], s_chunk[1])

                    def body(c_, k, nb):
                        sp.wait_ge(s_e, NB * (c_ - 1))
                        split_dma(sp, a_chunk[:, k, :, 0:nb * B], at_v[:, :, bass.ds(c_ * CN, nb * B)], s_chunk[k])
                        sp.dma_start(s_part[:, k, 0:nb * B], bc(io["s_dram"][bass.ds(c_ * CN, nb * B)], B, 0)).then_inc(s_sl[k], 16)
                    with sp.Fori(1, NC // 2) as i:
                        body(2 * i, 0, CB)
                        body(2 * i + 1, 1, CB)
                    body(NC - 1, 0, NB % CB)

                @block.scalar
                def _(act):
                    def body(c_, k, nb):
                        act.wait_ge(s_sl[k], 16 * loads(c_, k, loop))
                        for j in range(NB):
                            n = c_ * NB + j
                            if not (isinstance(c_, int) and n < UN):
                                act.wait_ge(s_e, n - UN + 1)
                            nc.scalar.activation(et[:, j % UN, 0:nb * B], s_part[:, k, 0:nb * B], ACT.Exp,
                                                 bias=t_bias[:, j:j + 1], scale=-0.8).then_inc(s_exp, 1)
                    loop = []
                    body(0, 0, CB)
                    with act.Fori(0, (NC - 3) // 2) as i:
                        loop.append(i)
                        body(2 * i + 1, 1, CB)
                        body(2 * i + 2, 0, CB)
                    body(NC - 2, 1, CB)
                    body(NC - 1, 0, NB % CB)

                @block.vector
                def _(dve):
                    v = nc.vector
                    dve.sem_inc(s_o, 1)

                    def finish(c_, k, nb):
                        dve.wait_ge(s_mm, NB * (c_ + 1))
                        for b in range(nb):
                            ins = v.reciprocal(rs[:, k, b:b + 1], acc[k][b][:, D:D + 1])
                        ins.then_inc(s_rs, 1)
                        dve.wait_ge(s_rs, c_ + 1)
                        for b in range(nb):
                            ins = v.tensor_scalar(o[:, k, b, :], acc[k][b][:, 0:D], rs[:, k, b:b + 1], 0.0, ALU.mult, ALU.max)
                        ins.then_inc(s_o, 1)
                        dve.wait_ge(s_o, c_ + 2)
                        xs = X[:, bass.ds(c_ * CB, nb), :]
                        v.tensor_tensor(xs, xs, o[:, k, 0:nb, :], ALU.add).then_inc(s_res, 1)
                        dve.wait_ge(s_res, c_ + 1)
                        for b in range(nb):
                            v.bn_stats(io["stats"][:, c_ * CB + b, :], X[:, c_ * CB + b, :])

                    def body(c_, k, nb):
                        if not (isinstance(c_, int) and c_ == 0):
                            dve.wait_ge(s_chunk[k], 32 * (loads(c_, k, loop) - (1 - k)))
                        for j in range(NB):
                            if isinstance(c_, int) and c_ == 0 and j % UN == 0:
                                dve.wait_ge(s_first[j // UN], 32)
                            n = c_ * NB + j
                            dve.wait_ge(s_exp, n + 1)
                            if not (isinstance(c_, int) and n < UN):
                                dve.wait_ge(s_mm, n - UN + 1)
                            v.scalar_tensor_tensor(e[:, j % UN, 0:nb * B], et[:, j % UN, 0:nb * B], 1.0,
                                                   a_chunk[:, k, j, 0:nb * B], ALU.min, ALU.mult).then_inc(s_e, 1)
                            if j == 3 and not (isinstance(c_, int) and c_ == 0):
                                finish(c_ - 1, 1 - k, CB)
                    loop = []
                    body(0, 0, CB)
                    with dve.Fori(0, (NC - 3) // 2) as i:
                        loop.append(i)
                        body(2 * i + 1, 1, CB)
                        body(2 * i + 2, 0, CB)
                    body(NC - 2, 1, CB)
                    body(NC - 1, 0, NB % CB)
                    finish(NC - 1, 0, NB % CB)

                @block.tensor
                def _(pe):
                    def body(c_, k, nb):
                        if not (isinstance(c_, int) and c_ < 2):
                            pe.wait_ge(s_o, c_)
                        for j in range(NB):
                            pe.wait_ge(s_e, c_ * NB + j + 1)
                            for b in range(nb):
                                mm = nc.tensor.matmul(acc[k][b][:], e[:, j % UN, b * B:(b + 1) * B], h1[:, j, :],
                                                      start=(j == 0), stop=(j == NB - 1))
                            mm.then_inc(s_mm, 1)
                    chunks(pe, body)


def float16_scale(nc, dve, sem, done, scale, inverse, bound):
    v = nc.vector
    q = inverse
    v.tensor_scalar(q.bitcast(I32), bound.bitcast(I32), 0x7F800000, None, ALU.bitwise_and).then_inc(sem, 1)
    dve.wait_ge(sem, done + 1)
    v.tensor_scalar(q, q, 2.0 ** -60, 2.0 ** 60, ALU.max, ALU.min).then_inc(sem, 1)
    dve.wait_ge(sem, done + 2)
    v.reciprocal(scale, q).then_inc(sem, 1)
    dve.wait_ge(sem, done + 3)
    v.tensor_scalar(scale, scale, 2.0 ** 14, None, ALU.mult).then_inc(sem, 1)
    v.tensor_scalar(q, q, 2.0 ** -14, None, ALU.mult).then_inc(sem, 1)
    dve.wait_ge(sem, done + 5)
    return done + 5


def mixture(nc, io, c, X):
    E, F = io["L0_ffn_gate_w"].shape[1], io["L0_ffn_w1"].shape[2]
    C = -(-5 * N // (4 * E))
    KF = F // P
    MT = -(-C // P)
    rows = [min(P, C - m * P) for m in range(MT)]
    buf, ybuf = io["buf_dram"], io["ybuf_dram"]
    with Space(nc) as s:
        rows_all = s.sb("rows_all", [B, NB, D])
        slot_in, slot_out = (s.sb(n, [B, NB], I32) for n in ("slot_in", "slot_out"))
        weight = s.sb("weight", [B, NB])
        s_tok = s.sem("D_tok")

        with Space(nc) as s1:
            norm = Norm(s1, "n2", io["stats"])
            gw = s1.sb("gw", [P, KD, E])
            gb = s1.sb("gb", [B, E])
            tri = s1.sb("tri", [B, B])
            rank_i = s1.sb("rank_i", [B, E], I32)
            rank = s1.sb("rank", [B, E])
            lg, ex, pr, eq, oh, tot, tin = (s1.sb(n, [B, NB, E]) for n in ("lg", "ex", "pr", "eq", "oh", "tot", "tin"))
            mx, sm, pm, best, pos, kept, place, zero = (s1.sb(n, [B, NB]) for n in ("mx", "sm", "pm", "best", "pos", "kept", "place", "zero"))
            plog = s1.ps("plog", [B, NB, E])
            pcum = s1.ps("pcum", [B, NB, E])
            ptot = s1.ps("ptot", [B, NB, E])
            s_gw, s_gb, s_tri, s_copy, s_v, s_sh, s_ex, s_oh, s_cum = (
                s1.sem("D_" + n) for n in ("gw", "gb", "tri", "copy", "v", "sh", "ex", "oh", "cum"))
            with nc.Block() as block:
                @block.sync
                def _(sp):
                    sp.dma_start(gw[:], io["L0_ffn_gate_w"].rearrange("(k p) e -> p k e", p=P)).then_inc(s_gw, 16)
                    sp.dma_start(gb[:], bc(io["L0_ffn_gate_b"], B, 0)).then_inc(s_gb, 16)

                @block.gpsimd
                def _(pool):
                    g = nc.gpsimd
                    g.iota(rank_i[:], [[-1, E]], base=E, channel_multiplier=0).then_inc(s_tri, 1)
                    g.memset(tri[:], 1.0).then_inc(s_tri, 1)
                    pool.wait_ge(s_tri, 2)
                    g.affine_select(out=tri[:], in_=tri[:], compare_op=ALU.is_ge, fill=0.0, base=0,
                                    pattern=[[1, B]], channel_multiplier=-1).then_inc(s_tri, 1)

                    def body(t, u, first):
                        pool.wait_ge(norm.s_xn, t + 1)
                        g.tensor_copy(rows_all[:, t, :], norm.xn[:, u, :]).then_inc(s_copy, 1)
                    blocks(pool, body)

                @block.scalar
                def _(act):
                    norm.std(nc, act)

                    def body(t, u, first):
                        if not first:
                            act.wait_ge(s_copy, t - UN + 1)
                        norm.rows(nc, act, X, t, u, first)
                    blocks(act, body)
                    act.wait_ge(s_sh, 1)
                    nc.scalar.activation(ex[:], lg[:], ACT.Exp).then_inc(s_ex, 1)

                @block.tensor
                def _(pe):
                    pe.wait_ge(s_gw, 16)

                    def turn(t, u, first):
                        norm.turn(nc, pe, c["ident"], t, u, first)

                    def body(t, u, first):
                        pe.wait_ge(norm.s_xt, t + 1)
                        for k in range(KD):
                            mm = nc.tensor.matmul(plog[:, t, :], norm.xt[:, u, k, :], gw[:, k, :], start=(k == 0), stop=(k == KD - 1))
                        mm.then_inc(norm.s_used, 1)
                    staggered(pe, turn, body)
                    pe.wait_ge(s_oh, 1)
                    ohf = oh[:].rearrange("p t e -> p (t e)")
                    nc.tensor.matmul(pcum[:].rearrange("p t e -> p (t e)"), tri[:], ohf, start=True, stop=True)
                    nc.tensor.matmul(ptot[:].rearrange("p t e -> p (t e)"), c["ones"][0:B, 0:B], ohf, start=True, stop=True).then_inc(s_cum, 1)

                @block.vector
                def _(dve):
                    v = nc.vector
                    n = [0]

                    def step(ins):
                        n[0] += 1
                        ins.then_inc(s_v, 1)
                        dve.wait_ge(s_v, n[0])

                    norm.stats(nc, dve)
                    v.memset(zero[:], 0.0)
                    blocks(dve, lambda t, u, first: norm.out(nc, dve, t, u, first))
                    dve.wait_ge(s_gb, 16)
                    dve.wait_ge(s_tri, 3)
                    dve.wait_ge(norm.s_used, NB)
                    v.tensor_copy(rank[:], rank_i[:])
                    step(v.tensor_tensor(lg[:], plog[:], bc(gb[:], NB, 1), ALU.add))
                    step(v.tensor_reduce(mx[:], lg[:], AX.X, ALU.max))
                    v.tensor_tensor(lg[:], lg[:], bc(mx[:], E, 2), ALU.subtract).then_inc(s_sh, 1)
                    dve.wait_ge(s_ex, 1)
                    step(v.tensor_reduce(sm[:], ex[:], AX.X, ALU.add))
                    step(v.reciprocal(mx[:], sm[:]))
                    step(v.tensor_tensor(pr[:], ex[:], bc(mx[:], E, 2), ALU.mult))
                    step(v.tensor_reduce(pm[:], pr[:], AX.X, ALU.max))
                    step(v.tensor_tensor(eq[:], pr[:], bc(pm[:], E, 2), ALU.is_equal))
                    step(v.tensor_tensor(eq[:], eq[:], bc(rank[:], NB, 1), ALU.mult))
                    step(v.tensor_reduce(best[:], eq[:], AX.X, ALU.max))
                    v.tensor_tensor(oh[:], eq[:], bc(best[:], E, 2), ALU.is_equal).then_inc(s_oh, 1)
                    dve.wait_ge(s_cum, 1)
                    step(v.tensor_copy(tot[:], ptot[:]))
                    for e in range(E):
                        ins = v.tensor_tensor_scan(tin[:, :, e], tot[:, :, e], zero[:], 0.0, ALU.add, ALU.add)
                    step(ins)
                    step(v.tensor_tensor(tin[:], tin[:], tot[:], ALU.subtract))
                    step(v.tensor_tensor(tin[:], tin[:], pcum[:], ALU.add))
                    step(v.tensor_tensor(tin[:], tin[:], oh[:], ALU.mult))
                    step(v.tensor_reduce(pos[:], tin[:], AX.X, ALU.add))
                    step(v.tensor_scalar(kept[:], pos[:], float(C), None, ALU.is_le))
                    v.tensor_tensor(weight[:], pm[:], kept[:], ALU.mult)
                    step(v.tensor_scalar(place[:], pos[:], float(C), -1.0, ALU.min, ALU.add))
                    step(v.tensor_scalar(best[:], best[:], -float(C), float(E * C), ALU.mult, ALU.add))
                    step(v.tensor_tensor(place[:], place[:], best[:], ALU.add))
                    v.tensor_copy(slot_out[:], place[:])
                    step(v.tensor_scalar(kept[:], kept[:], -8192.0, 8192.0, ALU.mult, ALU.add))
                    step(v.tensor_tensor(place[:], place[:], kept[:], ALU.add))
                    v.tensor_copy(slot_in[:], place[:]).then_inc(s_tok, 1)

        with Space(nc) as s2:
            w1, w2 = s2.sb("w1", [P, 2, KD, F]), s2.sb("w2", [P, 2, KF, D])
            w1p, w2p = s2.sb("w1p", [P, 2, 2, KD, F], F16), s2.sb("w2p", [P, 2, 2, KF, D], F16)
            b1_rows = s2.sb("b1_rows", [E * KF, P])
            b1 = s2.sb("b1", [P, E * KF])
            b2 = s2.sb("b2", [P, E, D])
            xe = s2.sb("xe", [P, 2, MT, D])
            xt = s2.sb("xte", [P, 2, 2, KD, C], F16)
            hm = s2.sb("hm", [P, KF, C])
            hmp = s2.sb("hmp", [P, 2, KF, C], F16)
            yo = s2.sb("yo", [P, MT, D])
            most = s2.sb("most", [P, 2, 2])
            b_most = s2.sb("b_most", [P, 1])
            b_bound = s2.sb("b_bound", [P, 1])
            bound, scale, inv = (s2.sb(n, [P, 2, 3]) for n in ("bounds", "scales", "inverses"))
            inv_y = s2.sb("inv_y", [P, 2])
            pt = [s2.ps(f"pte{k}", [P, C]) for k in range(KD)]
            ph = [s2.ps(f"phe{i}", [P, C]) for i in range(3)]
            py = [s2.ps(f"pye{i}", [P, D]) for i in range(2)]
            ptot = s2.ps("ptot_e", [P, 3])
            s_scat, s_b1, s_b2, s_b1t, s_b1c, s_bm, s_bt = (s2.sem("E_" + n) for n in ("scat", "b1", "b2", "b1t", "b1c", "bm", "bt"))
            s_w1, s_w2, s_xe = ([s2.sem(f"E_{n}{k}") for k in range(2)] for n in ("w1", "w2", "xe"))
            s_y = [s2.sem(f"E_y{m}") for m in range(MT)]
            s_most, s_tot, s_sc, s_scaled, s_tr, s_xhi, s_xlo, s_whi, s_wlo, s_mm1, s_hm, s_hhi, s_hlo, s_mm2, s_yo = (
                s2.sem("E_" + n) for n in ("most", "tot", "sc", "scaled", "tr", "xhi", "xlo", "whi", "wlo", "mm1", "hm", "hhi",
                                           "hlo", "mm2", "yo"))
            s_kept = s2.sem("E_kept")
            C0 = KF

            def experts(engine, step):
                with engine.Fori(0, E // 2 - 1) as i:
                    step(2 * i, 0, i, True, True)
                    step(2 * i + 1, 1, i, True, True)
                step(E - 2, 0, E // 2 - 1, True, False)
                step(E - 1, 1, E // 2 - 1, False, False)

            with nc.Block() as block:
                @block.sync
                def _(sp):
                    sp.dma_start(b1_rows[:], io["L0_ffn_b1"].rearrange("e (f p) -> (e f) p", p=P)).then_inc(s_b1, 16)
                    sp.dma_start(b2[:], bc(io["L0_ffn_b2"], P, 0)).then_inc(s_b2, 16)

                    def weights(e, k):
                        sp.dma_start(w1[:, k], io["L0_ffn_w1"][e].rearrange("(k p) f -> p k f", p=P)).then_inc(s_w1[k], 16)
                        sp.dma_start(w2[:, k], io["L0_ffn_w2"][e].rearrange("(f p) d -> p f d", p=P)).then_inc(s_w2[k], 16)

                    def token_rows(e, k):
                        sp.dma_start(xe[:, k], buf[bass.ds(e * C, MT * P), :].rearrange("(m p) d -> p m d", p=P)).then_inc(s_xe[k], 16)
                    weights(0, 0)
                    weights(1, 1)
                    sp.wait_ge(s_scat, 16 * NB)
                    token_rows(0, 0)
                    token_rows(1, 1)
                    with sp.Fori(1, E // 2) as i:
                        for k in range(2):
                            e = 2 * i + k
                            sp.wait_ge(s_wlo, 2 * (e - 1))
                            weights(e, k)
                            sp.wait_ge(s_tr, e - 1)
                            token_rows(e, k)

                @block.gpsimd
                def _(pool):
                    for t in range(NB):
                        nc.gpsimd.indirect_dma_start(buf, bass.IndirectOffsetOnAxis(ap=slot_in[:, t:t + 1], axis=0),
                                                     rows_all[:, t, :], None, bounds_check=E * C - 1,
                                                     oob_is_err=False).then_inc(s_scat, 16)

                    def step(e, k, r, one, two):
                        for m in range(MT):
                            pool.wait_ge(s_yo, C0 + MT * e + m + 1)
                            pool.dma_start(ybuf[bass.ds(e * C + m * P, rows[m]), :], yo[0:rows[m], m, :]).then_inc(s_y[m], 16)
                        for m in range(MT):
                            pool.wait_ge(s_y[m], 16 * (e + 1))
                        pool.sem_inc(s_kept, 1)
                    experts(pool, step)

                @block.tensor
                def _(pe):
                    t_ = nc.tensor
                    pe.sem_inc(s_mm1, C0)
                    pe.sem_inc(s_mm2, C0)
                    pe.wait_ge(s_b1, 16)
                    t_.transpose(ph[0][:, 0:E * KF], b1_rows[:], c["ident"][0:E * KF, 0:E * KF]).then_inc(s_b1t, 1)
                    pe.wait_ge(s_bm, 1)
                    t_.matmul(ptot[:, 0:1], c["ones"][:], b_most[:], start=True, stop=True).then_inc(s_bt, 1)
                    pe.wait_ge(s_bt, 2)

                    def prepare(e, k, r):
                        pe.wait_ge(s_most, 2 * (e + 1))
                        pe.wait_ge(s_scaled, e + 1)
                        t_.matmul(ptot[:, 0:2], c["ones"][:], most[:, k, :], start=True, stop=True).then_inc(s_tot, 1)
                        pe.wait_ge(s_xe[k], 16 * (r + 1))
                        pe.wait_ge(s_xlo, C0 + e)
                        for m in range(MT):
                            for f in range(KD):
                                tr = t_.transpose(pt[f][:, m * P:m * P + rows[m]], xe[0:rows[m], k, m, f * P:(f + 1) * P],
                                                  c["ident"][0:rows[m], 0:rows[m]])
                        tr.then_inc(s_tr, 1)
                    PAIRS_ = ((0, 1), (1, 0), (0, 0))

                    def step(e, k, r, one, two):
                        pe.wait_ge(s_xlo, C0 + e + 1)
                        pe.wait_ge(s_wlo, 2 * e + 1)
                        for f in range(KF):
                            pe.wait_ge(s_hm, C0 + KF * e + f - 2)
                            for n, (a, b) in enumerate(PAIRS_):
                                for j in range(KD):
                                    mm = t_.matmul(ph[f % 3][:], w1p[:, k, a, j, f * P:(f + 1) * P], xt[:, k, b, j, :],
                                                   start=(n == 0 and j == 0), stop=(n == 2 and j == KD - 1))
                            mm.then_inc(s_mm1, 1)
                        if one:
                            prepare(e + 1, 1 - k, r + k)
                        pe.wait_ge(s_wlo, 2 * e + 2)
                        pe.wait_ge(s_hlo, C0 + KF * (e + 1))
                        for m in range(MT):
                            pe.wait_ge(s_yo, C0 + MT * e + m - 1)
                            for n, (a, b) in enumerate(PAIRS_):
                                for f in range(KF):
                                    mm = t_.matmul(py[m % 2][0:rows[m], :], hmp[:, a, f, m * P:m * P + rows[m]], w2p[:, k, b, f, :],
                                                   start=(n == 0 and f == 0), stop=(n == 2 and f == KF - 1))
                            mm.then_inc(s_mm2, 1)
                    prepare(0, 0, 0)
                    experts(pe, step)

                @block.scalar
                def _(act):
                    a_ = nc.scalar
                    act.sem_inc(s_hm, C0)
                    act.sem_inc(s_hhi, C0)
                    act.wait_ge(s_b1c, 1)

                    def rows_hi(e, k):
                        act.wait_ge(s_tr, e + 1)
                        act.wait_ge(s_mm1, C0 + KF * (e - 1))
                        for f in range(KD):
                            ins = a_.activation(xt[:, k, 0, f, :], pt[f][:], ACT.Copy)
                        ins.then_inc(s_xhi, 1)

                    def weights_hi(e, k):
                        act.wait_ge(s_scaled, e + 2)
                        act.wait_ge(s_mm1, C0 + KF * (e - 1))
                        a_.activation(w1p[:, k, 0], w1[:, k], ACT.Copy, scale=scale[:, k, 0:1]).then_inc(s_whi, 1)
                        act.wait_ge(s_mm2, C0 + MT * (e - 1))
                        a_.activation(w2p[:, k, 0], w2[:, k], ACT.Copy, scale=scale[:, k, 1:2]).then_inc(s_whi, 1)

                    def step(e, k, r, one, two):
                        act.wait_ge(s_mm2, C0 + MT * e)
                        for f in range(KF):
                            act.wait_ge(s_mm1, C0 + KF * e + f + 1)
                            act.wait_ge(s_hlo, C0 + KF * (e - 1) + f + 1)
                            a_.activation(hm[:, f, :], ph[f % 3][:], ACT.Relu, scale=inv[:, k, 0:1],
                                          bias=b1[:, bass.ds(e * KF + f, 1)]).then_inc(s_hm, 1)
                            act.wait_ge(s_hm, C0 + KF * e + f + 1)
                            a_.activation(hmp[:, 0, f, :], hm[:, f, :], ACT.Copy, scale=scale[:, k, 2:3]).then_inc(s_hhi, 1)
                        if one:
                            rows_hi(e + 1, 1 - k)
                            weights_hi(e + 1, 1 - k)
                    rows_hi(0, 0)
                    weights_hi(0, 0)
                    experts(act, step)

                @block.vector
                def _(dve):
                    v = nc.vector
                    for s_, n in ((s_scaled, 1), (s_kept, 1), (s_xlo, C0), (s_hlo, C0), (s_yo, C0)):
                        dve.sem_inc(s_, n)
                    dve.wait_ge(s_b1t, 1)
                    v.tensor_copy(b1[:], ph[0][:, 0:E * KF]).then_inc(s_b1c, 1)
                    dve.wait_ge(s_b1c, 1)
                    v.tensor_reduce(b_most[:], b1[:], AX.X, ALU.max, apply_absolute_value=True).then_inc(s_bm, 1)
                    dve.wait_ge(s_bt, 1)
                    v.tensor_copy(b_bound[:], ptot[:, 0:1]).then_inc(s_bt, 1)
                    dve.wait_ge(s_b2, 16)
                    STEPS = 8

                    def largest(e, k, r, n):
                        w, s_w = ((w1, s_w1), (w2, s_w2))[n]
                        dve.wait_ge(s_w[k], 16 * (r + 1))
                        v.tensor_reduce(most[:, k, n:n + 1], w[:, k], AX.XY, ALU.max, apply_absolute_value=True).then_inc(s_most, 1)

                    def scales(e, k):
                        dve.wait_ge(s_tot, e + 1)
                        done = STEPS * e
                        v.tensor_copy(bound[:, k, 0:2], ptot[:, 0:2]).then_inc(s_sc, 1)
                        dve.wait_ge(s_sc, done + 1)
                        v.scalar_tensor_tensor(bound[:, k, 2:3], bound[:, k, 0:1], float(D), b_bound[:], ALU.mult, ALU.add).then_inc(s_sc, 1)
                        dve.wait_ge(s_sc, done + 2)
                        done = float16_scale(nc, dve, s_sc, done + 2, scale[:, k, :], inv[:, k, :], bound[:, k, :])
                        v.tensor_tensor(inv_y[:, k:k + 1], inv[:, k, 1:2], inv[:, k, 2:3], ALU.mult).then_inc(s_sc, 1)
                        dve.wait_ge(s_sc, done + 1)
                        dve.sem_inc(s_scaled, 1)

                    def rows_lo(e, k):
                        dve.wait_ge(s_xhi, e + 1)
                        for f in range(KD):
                            ins = v.tensor_tensor(xt[:, k, 1, f, :], pt[f][:], xt[:, k, 0, f, :], ALU.subtract)
                        ins.then_inc(s_xlo, 1)

                    def weights_lo(e, k, n):
                        w, wp = ((w1, w1p), (w2, w2p))[n]
                        dve.wait_ge(s_whi, 2 * e + n + 1)
                        v.scalar_tensor_tensor(wp[:, k, 1], w[:, k], scale[:, k, n:n + 1], wp[:, k, 0],
                                               ALU.mult, ALU.subtract).then_inc(s_wlo, 1)

                    def step(e, k, r, one, two):
                        for f in range(KF):
                            dve.wait_ge(s_hhi, C0 + KF * e + f + 1)
                            v.scalar_tensor_tensor(hmp[:, 1, f, :], hm[:, f, :], scale[:, k, 2:3], hmp[:, 0, f, :],
                                                   ALU.mult, ALU.subtract).then_inc(s_hlo, 1)
                        if one:
                            scales(e + 1, 1 - k)
                            rows_lo(e + 1, 1 - k)
                        dve.wait_ge(s_kept, e + 1)
                        for m in range(MT):
                            if one and m < 2:
                                weights_lo(e + 1, 1 - k, m)
                            if two and m >= 2:
                                largest(e + 2, k, r + 1, m - 2)
                            dve.wait_ge(s_mm2, C0 + MT * e + m + 1)
                            v.scalar_tensor_tensor(yo[0:rows[m], m, :], py[m % 2][0:rows[m], :], inv_y[0:rows[m], k:k + 1],
                                                   b2[0:rows[m], e, :], ALU.mult, ALU.add).then_inc(s_yo, 1)
                    assert MT == 4
                    for e in range(2):
                        for n in range(2):
                            largest(e, e, 0, n)
                    scales(0, 0)
                    rows_lo(0, 0)
                    weights_lo(0, 0, 0)
                    weights_lo(0, 0, 1)
                    experts(dve, step)

        with Space(nc) as s3:
            low, high = (s3.sb(n, [B, UN, D]) for n in ("low", "high"))
            finite = s3.sb("finite", [B, UN, D], U8)
            s_g = [s3.sem(f"F_g{t}") for t in range(NB)]
            s_v, s_val = s3.sem("F_v"), s3.sem("F_val")
            with nc.Block() as block:
                @block.gpsimd
                def _(pool):
                    for t in range(NB):
                        nc.gpsimd.indirect_dma_start(rows_all[:, t, :], None, ybuf[0:E * C, :],
                                                     bass.IndirectOffsetOnAxis(ap=slot_out[:, t:t + 1], axis=0)).then_inc(s_g[t], 16)

                @block.vector
                def _(dve):
                    v = nc.vector
                    n = [0]

                    def step(ins):
                        n[0] += 1
                        ins.then_inc(s_v, 1)
                        dve.wait_ge(s_v, n[0])
                    for q in range(NB // UN):
                        val = rows_all[:, UN * q:UN * (q + 1), :]
                        dve.wait_ge(s_val, UN * (q + 1))
                        v.tensor_scalar(finite[:], val, 0.0, 0.0, ALU.mult, ALU.is_equal)
                        v.tensor_scalar(low[:], val, 0.0, -1e4, ALU.min, ALU.max)
                        step(v.tensor_scalar(high[:], val, 0.0, 1e4, ALU.max, ALU.min))
                        step(v.tensor_tensor(low[:], low[:], high[:], ALU.add))
                        step(v.copy_predicated(low[:], finite[:], val))
                        xs = X[:, UN * q:UN * (q + 1), :]
                        step(v.tensor_tensor(xs, xs, low[:], ALU.add))
                        for t in range(UN * q, UN * (q + 1)):
                            v.bn_stats(io["stats"][:, t, :], X[:, t, :])

                @block.scalar
                def _(act):
                    for t in range(NB):
                        act.wait_ge(s_g[t], 16)
                        nc.scalar.activation(rows_all[:, t, :], rows_all[:, t, :], ACT.Copy, scale=weight[:, t:t + 1]).then_inc(s_val, 1)


class Chunk:

    def __init__(self, l, c, i=None):
        at = c if i is None else 2 * i + c
        self.c, self.nb = at, NB % CB if i is None and c == NC - 1 else CB
        self.g, self.g2 = NC * l + at, (NC * l + c) // 2 + (0 if i is None else i)
        self.k = (NC * l + c) % 2
        self.pairs = -(-self.nb // 2)
        self.before = PAIRS * l + 2 * at

    def nodes(self):
        return bass.ds(self.c * CN, self.nb * B)


PAIRS = -(-NB // 2)


def layer(engine, l, step):
    step(Chunk(l, 0), None)
    with engine.Fori(0, (NC - 3) // 2) as i:
        step(Chunk(l, 1, i), Chunk(l, 0, i))
        step(Chunk(l, 2, i), Chunk(l, 1, i))
    step(Chunk(l, NC - 2), Chunk(l, NC - 3))
    step(Chunk(l, NC - 1), Chunk(l, NC - 2))
    step(None, Chunk(l, NC - 1))


def mean_network(nc, io, c, X):
    LAYERS = io["L1_gnn_W_agg"].shape[0]
    C0 = 4
    with Space(nc) as s:
        h_t = s.sb("h_t", [P, KD, N])
        parts = [s.sb(f"parts{i}", [B, 2, NB, D], F16) for i in range(2)]
        dinv = s.sb("dinv_all", [P, N])
        w_agg, w_self = (s.sb(n, [P, LAYERS, KD, D]) for n in ("w_agg", "w_self"))
        w_out = s.sb("w_out", [P, KD, D])
        bias = s.sb("bias", [P, KD * (LAYERS + 1)])
        b_out = s.sb("b_out", [B, D])
        b_sum = s.sb("b_sum", [P, KD * (LAYERS + 1)])
        bound = s.sb("bound", [P, LAYERS])
        scale = s.sb("scale", [P, LAYERS, 2])
        s_wl, s_dl, s_ol = (s.sem("H_" + n) for n in ("wl", "dl", "ol"))

        with Space(nc) as s1:
            norm = Norm(s1, "n3", io["stats"])
            w_in = s1.sb("w_in", [P, KD, D])
            b_in = s1.sb("b_in", [B, D])
            b_rows = s1.sb("b_rows", [KD * (LAYERS + 1), P])
            hn = s1.sb("hn", [B, UN, D])
            pn = [s1.ps(f"pn{i}", [B, D]) for i in range(2)]
            pf = [s1.ps(f"pf{i}", [P, KD, B]) for i in range(2)]
            w_sq = s1.sb("w_sq", [P, KD, D])
            b_abs = s1.sb("b_abs", [P, KD * (LAYERS + 1)])
            col, root = s1.sb("col", [P, 1]), s1.sb("root", [P, 1])
            pb_all = s1.ps("pb_all", [P, 2 * KD * (LAYERS + 1) + D])
            pb, pb_sum, p_sq = (pb_all[:, a:b] for a, b in ((0, KD * (LAYERS + 1)), (KD * (LAYERS + 1), 2 * KD * (LAYERS + 1)),
                                                            (2 * KD * (LAYERS + 1), 2 * KD * (LAYERS + 1) + D)))
            s_abs, s_sq, s_col, s_root, s_sc = (s1.sem("H_" + n) for n in ("abs", "sq", "col", "root", "sc"))
            s_in, s_bin, s_br, s_bt, s_bc, s_pn, s_hn, s_hi, s_lo, s_ht = (
                s1.sem("H_" + n) for n in ("in", "bin", "br", "bt", "bc", "pn", "hn", "hi", "lo", "ht"))
            with nc.Block() as block:
                @block.sync
                def _(sp):
                    sp.dma_start(w_in[:], io["L1_gnn_W_in"].rearrange("(k p) f -> p k f", p=P)).then_inc(s_in, 16)
                    sp.dma_start(b_rows[0:KD], io["L1_gnn_b_in"].rearrange("(m p) -> m p", p=P)).then_inc(s_br, 16)
                    sp.dma_start(b_rows[KD:], io["L1_gnn_b_hid"].rearrange("l (m p) -> (l m) p", p=P)).then_inc(s_br, 16)
                    sp.dma_start(b_in[:], bc(io["L1_gnn_b_in"], B, 0)).then_inc(s_bin, 16)
                    for l in range(LAYERS):
                        sp.dma_start(w_agg[:, l], io["L1_gnn_W_agg"][l].rearrange("(k p) f -> p k f", p=P)).then_inc(s_wl, 16)
                        sp.dma_start(w_self[:, l], io["L1_gnn_W_self"][l].rearrange("(k p) f -> p k f", p=P)).then_inc(s_wl, 16)
                    sp.dma_start(w_out[:], io["L1_gnn_W_out"].rearrange("(k p) f -> p k f", p=P)).then_inc(s_wl, 16)
                    sp.dma_start(b_out[:], bc(io["L1_gnn_b_out"], B, 0)).then_inc(s_ol, 16)
                    sp.dma_start(dinv[:], bc(io["dinv_dram"], P, 0)).then_inc(s_dl, 16)
                    sp.wait_ge(s_wl, 16 * (2 * LAYERS + 1))
                    sp.wait_ge(s_ol, 16)
                    sp.wait_ge(s_dl, 16)

                @block.vector
                def _(dve):
                    v = nc.vector
                    norm.stats(nc, dve)
                    dve.wait_ge(s_bt, 1)
                    v.tensor_copy(bias[:], pb).then_inc(s_bc, 1)
                    dve.wait_ge(s_sq, 1)
                    v.tensor_reduce(col[:], p_sq, AX.X, ALU.max).then_inc(s_col, 1)
                    v.tensor_copy(b_sum[:], pb_sum).then_inc(s_col, 1)
                    dve.wait_ge(s_root, 1)
                    dve.wait_ge(s_col, 2)
                    v.scalar_tensor_tensor(bound[:, 0:1], root[:], b_sum[:, 0:1], b_sum[:, 1:2], ALU.add, ALU.add).then_inc(s_sc, 1)
                    dve.wait_ge(s_sc, 1)
                    float16_scale(nc, dve, s_sc, 1, scale[:, 0, 0:1], scale[:, 0, 1:2], bound[:, 0:1])
                    dve.wait_ge(s_bin, 16)

                    def out(t, u, first):
                        norm.out(nc, dve, t, u, first)

                    def biased(t, u, first):
                        dve.wait_ge(s_pn, t + 1)
                        if not first:
                            dve.wait_ge(s_lo, t - UN + 1)
                            dve.wait_ge(s_hi, t - UN + 1)
                        v.tensor_tensor(hn[:, u, :], pn[u % 2][:], b_in[:], ALU.add).then_inc(s_hn, 1)

                    def second_part(t, u, first):
                        dve.wait_ge(s_hi, t + 1)
                        v.scalar_tensor_tensor(parts[0][:, 1, t, :], hn[:, u, :], scale[0:B, 0, 0:1], parts[0][:, 0, t, :],
                                               ALU.mult, ALU.subtract).then_inc(s_lo, 1)
                    staggered(dve, out, biased, second_part)

                @block.scalar
                def _(act):
                    act.wait_ge(s_in, 16)
                    nc.scalar.activation(w_sq[:], w_in[:], ACT.Square).then_inc(s_abs, 1)
                    norm.std(nc, act)
                    act.wait_ge(s_bc, 1)
                    nc.scalar.activation(b_abs[:], bias[:], ACT.Abs).then_inc(s_abs, 1)
                    act.wait_ge(s_col, 1)
                    nc.scalar.activation(root[:], col[:], ACT.Sqrt, scale=float(D)).then_inc(s_root, 1)

                    def rows(t, u, first):
                        norm.rows(nc, act, X, t, u, first)

                    def after(t, u, first):
                        act.wait_ge(s_hn, t + 1)
                        nc.scalar.activation(parts[0][:, 0, t, :], hn[:, u, :], ACT.Copy, scale=scale[0:B, 0, 0:1]).then_inc(s_hi, 1)
                        act.wait_ge(norm.s_used, t + 1)
                        for m in range(KD):
                            ins = nc.scalar.activation(h_t[:, m, bass.ds(t * B, B)], pf[u % 2][:, m, :], ACT.Identity,
                                                       bias=bias[:, m:m + 1])
                        ins.then_inc(s_ht, 1)
                    staggered(act, rows, skip, after)

                @block.tensor
                def _(pe):
                    t_ = nc.tensor
                    pe.wait_ge(s_br, 32)
                    t_.transpose(pb, b_rows[:], c["ident"][0:KD * (LAYERS + 1), 0:KD * (LAYERS + 1)]).then_inc(s_bt, 1)
                    pe.wait_ge(s_in, 16)
                    pe.wait_ge(s_abs, 2)
                    t_.matmul(pb_sum, c["ones"][:], b_abs[:], start=True, stop=True)
                    for k in range(KD):
                        mm = t_.matmul(p_sq, c["ones"][:], w_sq[:, k, :], start=(k == 0), stop=(k == KD - 1))
                    mm.then_inc(s_sq, 1)

                    def turn(t, u, first):
                        norm.turn(nc, pe, c["ident"], t, u, first)

                    def body(t, u, first):
                        pe.wait_ge(norm.s_xt, t + 1)
                        if not first or u >= 2:
                            pe.wait_ge(s_hn, t - gap(u, 2) + 1)
                            pe.wait_ge(s_ht, t - gap(u, 2) + 1)
                        for k in range(KD):
                            mm = t_.matmul(pn[u % 2][:], norm.xt[:, u, k, :], w_in[:, k, :], start=(k == 0), stop=(k == KD - 1))
                        mm.then_inc(s_pn, 1)
                        for m in range(KD):
                            for k in range(KD):
                                mm = t_.matmul(pf[u % 2][:, m, :], w_in[:, k, m * P:(m + 1) * P], norm.xt[:, u, k, :], start=(k == 0), stop=(k == KD - 1))
                        mm.then_inc(norm.s_used, 1)
                    staggered(pe, turn, body)

        with Space(nc) as s2:
            a_chunk = s2.sb("a_chunk2", [B, 2, NB, CN], F16)
            agg = s2.sb("agg", [P, 2, KD, CN])
            hs = s2.sb("hs", [P, 2, KD, CN])
            pa = [[s2.ps(f"pa{k}{m}", [P, CN]) for m in range(KD)] for k in range(2)]
            pw = [s2.ps(f"pw{m}", [P, CN]) for m in range(KD)]
            pt = [s2.ps(f"pt2{i}", [B, 2, D]) for i in range(2)]
            s_chunk = [s2.sem(f"I_chunk{i}") for i in range(2)]
            s_pa, s_agg, s_pw, s_hs, s_ht, s_pt, s_hi, s_lo, s_xb = (
                s2.sem("I_" + n) for n in ("pa", "agg", "pw", "hs", "ht", "pt", "hi", "lo", "xb"))
            at_v = io["AT_dram"].rearrange("(b j) i -> j b i", j=B)
            s_abs, s_norm, s_sc = (s2.sem("I_" + n) for n in ("abs", "norm", "sc"))
            abs_agg, abs_self = agg[:, :, :, 0:D], hs[:, :, :, 0:D]
            norms = [pw[l][:, 0:D] for l in range(LAYERS - 1)]
            assert LAYERS - 1 <= KD

            with nc.Block() as block:
                @block.sync
                def _(sp):
                    def load(ch):
                        split_dma(sp, a_chunk[:, ch.k, :, 0:ch.nb * B], at_v[:, :, ch.nodes()], s_chunk[ch.k])
                    for l in range(LAYERS):
                        def step(ch, _):
                            if ch is None:
                                return
                            sp.wait_ge(s_pa, C0 + 2 * (ch.g - 1))
                            load(ch)
                        layer(sp, l, step)

                @block.gpsimd
                def _(pool):
                    pool.sem_inc(s_ht, C0)
                    nc.gpsimd.tensor_tensor(X[:], X[:], bc(b_out[:], NB, 1), ALU.add).then_inc(s_xb, 1)
                    for l in range(LAYERS - 1):
                        def step(_, ch):
                            if ch is None:
                                return
                            pool.wait_ge(s_hs, C0 + 2 * (ch.g + 1))
                            nc.gpsimd.tensor_copy(h_t[:, :, ch.nodes()], hs[:, ch.k, :, 0:ch.nb * B]).then_inc(s_ht, 1)
                        layer(pool, l, step)

                @block.tensor
                def _(pe):
                    t_ = nc.tensor
                    pe.sem_inc(s_pa, C0)
                    pe.sem_inc(s_pw, C0)
                    pe.sem_inc(s_pt, C0)
                    pe.wait_ge(s_abs, 1)
                    for l in range(LAYERS - 1):
                        for n, w in enumerate((abs_agg, abs_self)):
                            for k in range(KD):
                                mm = t_.matmul(norms[l], c["ones"][:], w[:, l, k, :], start=(n == 0 and k == 0), stop=(n == 1 and k == KD - 1))
                    mm.then_inc(s_norm, 1)

                    def gather(l, ch, m):
                        if m == 0:
                            pe.wait_ge(s_chunk[ch.k], 32 * (ch.g2 + 1))
                        pe.wait_ge(s_agg, C0 + 2 * (ch.g - 2) + m + 1)
                        for q in range(2):
                            for j in range(NB):
                                mm = t_.matmul(pa[ch.k][m][:, 0:ch.nb * B], parts[l % 2][:, q, j, m * P:(m + 1) * P],
                                               a_chunk[:, ch.k, j, 0:ch.nb * B], start=(q == 0 and j == 0), stop=(q == 1 and j == NB - 1))
                        mm.then_inc(s_pa, 1)

                    def weights(l, ch):
                        w = ch.nb * B
                        pe.wait_ge(s_agg, C0 + 2 * (ch.g + 1))
                        pe.wait_ge(s_hs, C0 + 2 * ch.g)
                        if l:
                            pe.wait_ge(s_ht, C0 + ch.g - NC + 1)
                        for m in range(KD):
                            ms = slice(m * P, (m + 1) * P)
                            for k in range(KD):
                                t_.matmul(pw[m][:, 0:w], w_agg[:, l, k, ms], agg[:, ch.k, k, 0:w], start=(k == 0), stop=False)
                            for k in range(KD):
                                mm = t_.matmul(pw[m][:, 0:w], w_self[:, l, k, ms], h_t[:, k, ch.nodes()], start=False, stop=(k == KD - 1))
                            mm.then_inc(s_pw, 1)

                    def turn(l, ch):
                        pe.wait_ge(s_hs, C0 + 2 * (ch.g + 1))
                        pe.wait_ge(s_lo, C0 + ch.before)
                        for b in range(ch.nb):
                            bs = slice(b * B, (b + 1) * B)
                            for m in range(KD):
                                if l < LAYERS - 1:
                                    mm = t_.transpose(pt[b // 2][:, b % 2, m * P:(m + 1) * P], hs[:, ch.k, m, bs], c["ident"][:])
                                else:
                                    mm = t_.matmul(pt[b // 2][:, b % 2, :], hs[:, ch.k, m, bs], w_out[:, m, :], start=(m == 0), stop=(m == KD - 1))
                            if b % 2 or b == ch.nb - 1:
                                mm.then_inc(s_pt, 1)

                    for l in range(LAYERS):
                        def step(ch, pr, l=l):
                            if ch is not None:
                                if pr is None and l:
                                    pe.wait_ge(s_lo, C0 + PAIRS * l)
                                gather(l, ch, 0)
                            if pr is not None:
                                weights(l, pr)
                            if ch is not None:
                                gather(l, ch, 1)
                            if pr is not None:
                                turn(l, pr)
                        layer(pe, l, step)

                @block.scalar
                def _(act):
                    act.sem_inc(s_hs, C0)
                    act.sem_inc(s_hi, C0)
                    nc.scalar.activation(abs_agg, w_agg[:, 0:LAYERS - 1], ACT.Abs)
                    nc.scalar.activation(abs_self, w_self[:, 0:LAYERS - 1], ACT.Abs).then_inc(s_abs, 1)
                    act.wait_ge(s_sc, 8 * (LAYERS - 1))
                    for l in range(LAYERS):
                        def step(_, ch, l=l):
                            if ch is None:
                                return
                            w = ch.nb * B
                            last = isinstance(ch.c, int) and ch.c == 0
                            act.wait_ge(s_pt, C0 + ch.before - (1 if last else 2))
                            if l < LAYERS - 1:
                                act.wait_ge(s_ht, C0 + ch.g - 1)
                            else:
                                act.wait_ge(s_ht, C0 + NC * (LAYERS - 1))
                            for m in range(KD):
                                act.wait_ge(s_pw, C0 + 2 * ch.g + m + 1)
                                nc.scalar.activation(hs[:, ch.k, m, 0:w], pw[m][:, 0:w], ACT.Relu,
                                                     bias=bias[:, KD * (l + 1) + m:KD * (l + 1) + m + 1]).then_inc(s_hs, 1)
                            if l < LAYERS - 1:
                                for i in range(ch.pairs):
                                    n = min(2, ch.nb - 2 * i)
                                    act.wait_ge(s_pt, C0 + ch.before + i + 1)
                                    nc.scalar.activation(parts[(l + 1) % 2][:, 0, bass.ds(ch.c * CB + 2 * i, n), :], pt[i][:, 0:n, :],
                                                         ACT.Copy, scale=scale[0:B, l + 1, 0:1]).then_inc(s_hi, 1)
                        layer(act, l, step)

                @block.vector
                def _(dve):
                    v = nc.vector
                    dve.sem_inc(s_agg, C0)
                    dve.sem_inc(s_lo, C0)
                    dve.wait_ge(s_norm, 1)
                    n = 0
                    for l in range(LAYERS - 1):
                        at = bound[:, l + 1:l + 2]
                        v.tensor_reduce(at, norms[l], AX.X, ALU.max).then_inc(s_sc, 1)
                        dve.wait_ge(s_sc, n + 1)
                        v.tensor_scalar(at, at, bound[:, l:l + 1], b_sum[:, KD * (l + 1):KD * (l + 1) + 1], ALU.mult, ALU.add).then_inc(s_sc, 1)
                        dve.wait_ge(s_sc, n + 2)
                        v.tensor_scalar(at, at, b_sum[:, KD * (l + 1) + 1:KD * (l + 2)], None, ALU.add).then_inc(s_sc, 1)
                        dve.wait_ge(s_sc, n + 3)
                        n = float16_scale(nc, dve, s_sc, n + 3, scale[:, l + 1, 0:1], scale[:, l + 1, 1:2], at)
                    for l in range(LAYERS):
                        def step(ch, pr, l=l):
                            if ch is not None:
                                w = ch.nb * B
                                dve.wait_ge(s_pw, C0 + 2 * (ch.g - 1))
                                for m in range(KD):
                                    dve.wait_ge(s_pa, C0 + 2 * ch.g + m + 1)
                                    v.scalar_tensor_tensor(agg[:, ch.k, m, 0:w], pa[ch.k][m][:, 0:w], scale[:, l, 1:2], dinv[:, ch.nodes()],
                                                           ALU.mult, ALU.mult).then_inc(s_agg, 1)
                            if pr is not None:
                                for i in range(pr.pairs):
                                    n = min(2, pr.nb - 2 * i)
                                    bs = bass.ds(pr.c * CB + 2 * i, n)
                                    if l < LAYERS - 1:
                                        dve.wait_ge(s_hi, C0 + pr.before + i + 1)
                                        v.scalar_tensor_tensor(parts[(l + 1) % 2][:, 1, bs, :], pt[i][:, 0:n, :], scale[0:B, l + 1, 0:1],
                                                               parts[(l + 1) % 2][:, 0, bs, :], ALU.mult, ALU.subtract).then_inc(s_lo, 1)
                                    else:
                                        dve.wait_ge(s_pt, C0 + pr.before + i + 1)
                                        dve.wait_ge(s_xb, 1)
                                        v.tensor_tensor(X[:, bs, :], pt[i][:, 0:n, :], X[:, bs, :], ALU.add).then_inc(s_lo, 1)
                                        dve.wait_ge(s_lo, C0 + pr.before + i + 1)
                                        for b in range(n):
                                            v.bn_stats(io["stats"][:, pr.c * CB + 2 * i + b, :], X[:, pr.c * CB + 2 * i + b, :])
                        layer(dve, l, step)


def gated_networks(nc, io, c, X):
    H1, H2 = io["L1_ffn_sW1"].shape[1], io["L1_ffn_sW2"].shape[1]
    E, _, G1 = io["L1_ffn_eW1"].shape
    G2 = io["L1_ffn_eW2"].shape[2]
    KH = H1 // P
    Q = E // 2
    assert H2 == G1 == P and 2 * G2 == P and KH == 2
    NBIAS = KH + 1 + E + Q
    with Space(nc) as s:
        x_t = s.sb("x_t", [P, KD, N])
        top = s.sb("top", [B, NB, E + 1])
        top_t = s.sb("top_t", [E + 1, N])
        sw1, sw2, sw3 = s.sb("sw1", [P, KD, H1]), s.sb("sw2", [P, KH, H2]), s.sb("sw3", [P, D])
        ew1, ew2, ew3 = s.sb("ew1", [P, E, KD, G1]), s.sb("ew2", [P, E, G2]), s.sb("ew3", [P, Q, D])
        b_last = s.sb("b_last", [E + 1, D])
        bias = s.sb("biasf", [P, NBIAS])
        spread = s.sb("spread", [E + 1, Q, 2 * G2])
        s_wl = s.sem("J_wl")

        with Space(nc) as s1:
            norm = Norm(s1, "n4", io["stats"])
            gw = s1.sb("gw4", [P, KD, E])
            gb = s1.sb("gb4", [B, E])
            rank_i, rank = s1.sb("rank4_i", [B, E], I32), s1.sb("rank4", [B, E])
            b_rows = s1.sb("b_rows4", [NBIAS, P])
            lg, ex, gate, eq, first_, rest, both = (s1.sb("j" + n, [B, NB, E]) for n in ("lg", "ex", "gate", "eq", "first", "rest", "both"))
            mx, sm = (s1.sb("j" + n, [B, NB]) for n in ("mx", "sm"))
            top_rows = s1.sb("top_rows", [NB * (E + 1), B])
            plog = s1.ps("plog4", [B, NB, E])
            pb = s1.ps("pb4", [P, P])
            s_gw, s_gb, s_br, s_bt, s_c, s_copy, s_v, s_sh, s_ex, s_top, s_tt, s_tc, s_to, s_tl = (
                s1.sem("J_" + n) for n in ("gw", "gb", "br", "bt", "c", "copy", "v", "sh", "ex", "top", "tt", "tc", "to", "tl"))
            with nc.Block() as block:
                @block.sync
                def _(sp):
                    sp.dma_start(gw[:], io["L1_ffn_gW"].rearrange("(k p) e -> p k e", p=P)).then_inc(s_gw, 16)
                    sp.dma_start(gb[:], bc(io["L1_ffn_gb"], B, 0)).then_inc(s_gb, 16)
                    at = 0
                    for b_, n in ((io["L1_ffn_sb1"].rearrange("(r p) -> r p", p=P), KH), (io["L1_ffn_sb2"].rearrange("(r p) -> r p", p=P), 1),
                                  (io["L1_ffn_eb1"], E), (io["L1_ffn_eb2"].rearrange("(q r) g -> q (r g)", r=2), Q)):
                        sp.dma_start(b_rows[at:at + n], b_).then_inc(s_br, 16)
                        at += n
                    loads = [(sw1[:], io["L1_ffn_sW1"].rearrange("(k p) h -> p k h", p=P)),
                             (sw2[:], io["L1_ffn_sW2"].rearrange("(k p) h -> p k h", p=P)), (sw3[:], io["L1_ffn_sW3"]),
                             (ew2[:], io["L1_ffn_eW2"].rearrange("e p g -> p e g")),
                             (ew3[:], io["L1_ffn_eW3"].rearrange("(q r) g o -> (r g) q o", r=2)),
                             (b_last[0:E], io["L1_ffn_eb3"]), (b_last[E:E + 1], io["L1_ffn_sb3"].rearrange("(o d) -> o d", o=1))]
                    loads += [(ew1[:, e], io["L1_ffn_eW1"][e].rearrange("(k p) h -> p k h", p=P)) for e in range(E)]
                    for o, i in loads:
                        sp.dma_start(o, i).then_inc(s_wl, 16)
                    sp.wait_ge(s_tc, 1)
                    sp.dma_start(io["top_dram"].rearrange("t e n -> (t e) n"), top_rows[:]).then_inc(s_to, 16)
                    sp.wait_ge(s_to, 16)
                    sp.dma_start(top_t[:].rearrange("e (t n) -> e t n", n=B), io["top_dram"].rearrange("t e n -> e t n")).then_inc(s_tl, 16)
                    sp.wait_ge(s_tl, 16)
                    sp.wait_ge(s_wl, 16 * len(loads))

                @block.gpsimd
                def _(pool):
                    g = nc.gpsimd
                    g.iota(rank_i[:], [[-1, E]], base=E, channel_multiplier=0).then_inc(s_c, 1)
                    g.memset(spread[:], 1.0).then_inc(s_c, 1)
                    pool.wait_ge(s_c, 2)
                    g.affine_select(out=spread[:], in_=spread[:], compare_op=ALU.is_ge, fill=0.0, base=0,
                                    pattern=[[2 * G2, Q], [1, 2 * G2]], channel_multiplier=-G2).then_inc(s_c, 1)
                    pool.wait_ge(s_c, 3)
                    g.affine_select(out=spread[:], in_=spread[:], compare_op=ALU.is_ge, fill=0.0, base=G2 - 1,
                                    pattern=[[-2 * G2, Q], [-1, 2 * G2]], channel_multiplier=G2).then_inc(s_c, 1)

                    def body(t, u, first):
                        pool.wait_ge(norm.s_xt, t + 1)
                        g.tensor_copy(x_t[:, :, bass.ds(t * B, B)], norm.xt[:, u, :, :]).then_inc(s_copy, 1)
                    blocks(pool, body)

                @block.scalar
                def _(act):
                    norm.std(nc, act)
                    blocks(act, lambda t, u, first: norm.rows(nc, act, X, t, u, first))
                    act.wait_ge(s_sh, 1)
                    nc.scalar.activation(ex[:], lg[:], ACT.Exp).then_inc(s_ex, 1)
                    act.wait_ge(s_sh, 2)
                    nc.scalar.activation(ex[:], lg[:], ACT.Exp).then_inc(s_ex, 1)

                @block.tensor
                def _(pe):
                    pe.wait_ge(s_br, 64)
                    nc.tensor.transpose(pb[:, 0:NBIAS], b_rows[:], c["ident"][0:NBIAS, 0:NBIAS]).then_inc(s_bt, 1)
                    pe.wait_ge(s_gw, 16)

                    def turn(t, u, first):
                        norm.turn(nc, pe, c["ident"], t, u, first)

                    def body(t, u, first):
                        pe.wait_ge(norm.s_xt, t + 1)
                        for k in range(KD):
                            mm = nc.tensor.matmul(plog[:, t, :], norm.xt[:, u, k, :], gw[:, k, :], start=(k == 0), stop=(k == KD - 1))
                        mm.then_inc(norm.s_used, 1)
                    staggered(pe, turn, body)
                    pe.wait_ge(s_top, 1)
                    nc.tensor.transpose(pb[0:NB * (E + 1), 0:B], top[:].rearrange("p t e -> p (t e)"), c["ident"][0:B, 0:B]).then_inc(s_tt, 1)

                @block.vector
                def _(dve):
                    v = nc.vector
                    n = [0]

                    def step(ins):
                        n[0] += 1
                        ins.then_inc(s_v, 1)
                        dve.wait_ge(s_v, n[0])

                    def first_max(out, x):
                        step(v.tensor_reduce(mx[:], x[:], AX.X, ALU.max))
                        step(v.tensor_tensor(eq[:], x[:], bc(mx[:], E, 2), ALU.is_equal))
                        step(v.tensor_tensor(eq[:], eq[:], bc(rank[:], NB, 1), ALU.mult))
                        step(v.tensor_reduce(sm[:], eq[:], AX.X, ALU.max))
                        step(v.tensor_tensor(out[:], eq[:], bc(sm[:], E, 2), ALU.is_equal))

                    norm.stats(nc, dve)
                    dve.wait_ge(s_bt, 1)
                    v.tensor_copy(bias[:], pb[:, 0:NBIAS])

                    def body(t, u, first):
                        if not first:
                            dve.wait_ge(s_copy, t - UN + 1)
                        norm.out(nc, dve, t, u, first)
                    blocks(dve, body)
                    dve.wait_ge(s_gb, 16)
                    dve.wait_ge(s_c, 4)
                    dve.wait_ge(norm.s_used, NB)
                    v.tensor_copy(rank[:], rank_i[:])
                    step(v.tensor_tensor(lg[:], plog[:], bc(gb[:], NB, 1), ALU.add))
                    step(v.tensor_reduce(mx[:], lg[:], AX.X, ALU.max))
                    v.tensor_tensor(lg[:], lg[:], bc(mx[:], E, 2), ALU.subtract).then_inc(s_sh, 1)
                    dve.wait_ge(s_sh, 1)
                    dve.wait_ge(s_ex, 1)
                    step(v.tensor_reduce(sm[:], ex[:], AX.X, ALU.add))
                    step(v.reciprocal(mx[:], sm[:]))
                    step(v.tensor_tensor(gate[:], ex[:], bc(mx[:], E, 2), ALU.mult))
                    first_max(first_, gate)
                    step(v.scalar_tensor_tensor(rest[:].rearrange("p t e -> p (t e)"), first_[:].rearrange("p t e -> p (t e)"), -4.0,
                                                gate[:].rearrange("p t e -> p (t e)"), ALU.mult, ALU.add))
                    step(v.tensor_reduce(mx[:], gate[:], AX.X, ALU.max))
                    v.tensor_tensor(lg[:], gate[:], bc(mx[:], E, 2), ALU.subtract).then_inc(s_sh, 1)
                    dve.wait_ge(s_sh, 2)
                    first_max(both, rest)
                    step(v.tensor_tensor(both[:], both[:], first_[:], ALU.add))
                    dve.wait_ge(s_ex, 2)
                    step(v.tensor_tensor(ex[:], ex[:], both[:], ALU.mult))
                    step(v.tensor_reduce(sm[:], ex[:], AX.X, ALU.add))
                    step(v.reciprocal(mx[:], sm[:]))
                    v.memset(top[:, :, E:E + 1], 1.0)
                    v.tensor_tensor(top[:, :, 0:E], ex[:], bc(mx[:], E, 2), ALU.mult).then_inc(s_top, 1)
                    dve.wait_ge(s_tt, 1)
                    v.tensor_copy(top_rows[:], pb[0:NB * (E + 1), 0:B]).then_inc(s_tc, 1)

        with Space(nc) as s2:
            a1 = s2.sb("shared1", [P, 2, KH, CN])
            g1 = s2.sb("expert1", [P, 2, E, CN])
            a2 = s2.sb("shared2", [P, 2, CN])
            g2, g2w = (s2.sb(n, [P, 2, Q, CN]) for n in ("expert2", "expert2_w"))
            top_c = s2.sb("top_chunk", [E + 1, 2, CN])
            y = s2.sb("y_out", [B, 2, CB, D])
            ring = [s2.ps(f"ring{i}", [P, CN]) for i in range(3)]
            pg = [s2.ps(f"pg{q}", [P, CN]) for q in range(Q)]
            po = [s2.ps(f"po{i}", [B, 2, D]) for i in range(2)]
            s_p, s_a, s_g, s_g2w, s_po, s_y, s_tc = (s2.sem("K_" + n) for n in ("p", "a", "g", "g2w", "po", "y", "tc"))
            s_out = [s2.sem(f"K_out{k}") for k in range(2)]
            NP_ = KH + E + 1 + Q
            assert NP_ % 3 == 0
            C0 = 2 * NP_
            out_v = io["out"].rearrange("(t p) d -> p t d", p=B)
            dest = [lambda k, m=m: a1[:, k, m] for m in range(KH)] + [lambda k, e=e: g1[:, k, e] for e in range(E)] + \
                   [lambda k: a2[:, k]] + [lambda k, q=q: g2[:, k, q] for q in range(Q)]
            bias_of = list(range(KH)) + [KH + 1 + e for e in range(E)] + [KH] + [KH + 1 + E + q for q in range(Q)]

            with nc.Block() as block:
                @block.sync
                def _(sp):
                    def step(_, ch):
                        if ch is None:
                            return
                        sp.wait_ge(s_y, C0 + ch.before + ch.pairs)
                        for a, b in ((0, 112), (112, B)):
                            sp.dma_start(out_v[a:b, bass.ds(ch.c * CB, ch.nb), :], y[a:b, ch.k, 0:ch.nb, :]).then_inc(s_out[ch.k], 16)
                    layer(sp, 0, step)
                    sp.wait_ge(s_out[0], 32 * ((NC + 1) // 2 + 1))
                    sp.wait_ge(s_out[1], 32 * (NC // 2 + 1))

                @block.gpsimd
                def _(pool):
                    pool.sem_inc(s_tc, C0)

                    def step(ch, _):
                        if ch is None:
                            return
                        pool.wait_ge(s_po, C0 + ch.before - 2)
                        nc.gpsimd.tensor_copy(top_c[:, ch.k, 0:ch.nb * B], top_t[:, ch.nodes()]).then_inc(s_tc, 1)
                    layer(pool, 0, step)

                @block.tensor
                def _(pe):
                    t_ = nc.tensor
                    pe.sem_inc(s_p, C0)
                    pe.sem_inc(s_g, C0)
                    pe.sem_inc(s_po, C0)

                    def products(ch):
                        w, k = ch.nb * B, ch.k
                        xs = [x_t[:, j, ch.nodes()] for j in range(KD)]

                        def bank(n):
                            pe.wait_ge(s_a, C0 + NP_ * ch.c + n - 2)
                            return ring[n % 3]

                        def done(n):
                            pe.wait_ge(s_a, C0 + NP_ * ch.c + n + 1)
                        for n in range(KH + E):
                            r = bank(n)
                            for j in range(KD):
                                lhs = sw1[:, j, n * P:(n + 1) * P] if n < KH else ew1[:, n - KH, j, :]
                                mm = t_.matmul(r[:, 0:w], lhs, xs[j], start=(j == 0), stop=(j == KD - 1))
                            mm.then_inc(s_p, 1)
                        r = bank(KH + E)
                        for j in range(KH):
                            mm = t_.matmul(r[:, 0:w], sw2[:, j, :], a1[:, k, j, 0:w], start=(j == 0), stop=(j == KH - 1))
                        mm.then_inc(s_p, 1)
                        for q in range(Q):
                            r = bank(KH + E + 1 + q)
                            done(KH + 2 * q + 1)
                            for e in range(2):
                                mm = t_.matmul(r[e * G2:(e + 1) * G2, 0:w], ew2[:, 2 * q + e, :], g1[:, k, 2 * q + e, 0:w], start=True, stop=True)
                            mm.then_inc(s_p, 1)
                        pe.wait_ge(s_tc, C0 + ch.c + 1)
                        for q in range(Q):
                            pe.wait_ge(s_g2w, C0 + Q * (ch.c - 1) + q + 1)
                            t_.matmul(pg[q][:, 0:w], spread[:, q, :], top_c[:, k, 0:w], start=True, stop=True).then_inc(s_g, 1)

                    def outputs(ch):
                        k = ch.k
                        pe.wait_ge(s_g2w, C0 + Q * (ch.c + 1))
                        pe.wait_ge(s_a, C0 + NP_ * (ch.c + 1))
                        pe.wait_ge(s_y, C0 + ch.before)
                        for b in range(ch.nb):
                            bs = slice(b * B, (b + 1) * B)
                            o = po[b // 2][:, b % 2, :]
                            t_.matmul(o, a2[:, k, bs], sw3[:], start=True, stop=False)
                            for q in range(Q):
                                t_.matmul(o, g2w[:, k, q, bs], ew3[:, q, :], start=False, stop=False)
                            mm = t_.matmul(o, top_c[:, k, bs], b_last[:], start=False, stop=True)
                            if b % 2 or b == ch.nb - 1:
                                mm.then_inc(s_po, 1)

                    def step(ch, pr):
                        if ch is not None:
                            products(ch)
                        if pr is not None:
                            outputs(pr)
                    layer(pe, 0, step)

                @block.scalar
                def _(act):
                    act.sem_inc(s_a, C0)

                    def step(ch, _):
                        if ch is None:
                            return
                        w = ch.nb * B
                        act.wait_ge(s_po, C0 + ch.before - 2)
                        act.wait_ge(s_g2w, C0 + Q * (ch.c - 1))
                        for n in range(NP_):
                            act.wait_ge(s_p, C0 + NP_ * ch.c + n + 1)
                            nc.scalar.activation(dest[n](ch.k)[:, 0:w], ring[n % 3][:, 0:w], ACT.Relu,
                                                 bias=bias[:, bias_of[n]:bias_of[n] + 1]).then_inc(s_a, 1)
                    layer(act, 0, step)

                @block.vector
                def _(dve):
                    v = nc.vector
                    dve.sem_inc(s_g2w, C0)
                    dve.sem_inc(s_y, C0)
                    for k in range(2):
                        dve.sem_inc(s_out[k], 32)

                    def step(ch, pr):
                        if ch is not None:
                            w = ch.nb * B
                            for q in range(Q):
                                dve.wait_ge(s_g, C0 + Q * ch.c + q + 1)
                                dve.wait_ge(s_po, C0 + ch.before - 2)
                                dve.wait_ge(s_a, C0 + NP_ * ch.c + NP_ - Q + q + 1)
                                v.tensor_tensor(g2w[:, ch.k, q, 0:w], pg[q][:, 0:w], g2[:, ch.k, q, 0:w], ALU.mult).then_inc(s_g2w, 1)
                        if pr is not None:
                            dve.wait_ge(s_out[pr.k], 32 * (pr.g2 + 1))
                            for i in range(pr.pairs):
                                nb = min(2, pr.nb - 2 * i)
                                dve.wait_ge(s_po, C0 + pr.before + i + 1)
                                v.tensor_tensor(y[:, pr.k, 2 * i:2 * i + nb, :], po[i][:, 0:nb, :],
                                                X[:, bass.ds(pr.c * CB + 2 * i, nb), :], ALU.add).then_inc(s_y, 1)
                    layer(dve, 0, step)


def program(nc, io):
    with Space(nc) as k:
        io["s_buf_zero"] = k.sem("buf_zero")
        c = constants(nc, k)
        X = k.sb("X", [B, NB, D])
        io["stats"] = k.sb("stats", [B, NB, 6])
        with Space(nc) as ka:
          io["h1"], io["t_bias"] = ka.sb("h1", [B, NB, D + 1]), ka.sb("t_bias", [B, NB])
          with Space(nc) as k1:
            keep = {"srcf": k1.sb("srcf", [B, EP]), "dstf": k1.sb("dstf", [B, EP]),
                    "zeros": k1.sb("zeros", [P, 8 * D]),
                    "lo": k1.sb("lo", [EW, NW, 2], BF16), "code": k1.sb("code", [EW, NW, 2], BF16),
                    "captured": k1.sb("captured", [1, 1], I32)}
            edge_windows(nc, io, c, keep, X)
            count_matrix(nc, io, c, keep)
          graph_attention(nc, io, c, X)
        mixture(nc, io, c, X)
        mean_network(nc, io, c, X)
        gated_networks(nc, io, c, X)


INPUTS = ['x', 'src', 'dst', 'L0_gnn_W', 'L0_gnn_a', 'L0_ffn_gate_w', 'L0_ffn_gate_b', 'L0_ffn_w1', 'L0_ffn_b1',
          'L0_ffn_w2', 'L0_ffn_b2', 'L1_gnn_W_in', 'L1_gnn_b_in', 'L1_gnn_W_agg', 'L1_gnn_W_self', 'L1_gnn_b_hid',
          'L1_gnn_W_out', 'L1_gnn_b_out', 'L1_ffn_sW1', 'L1_ffn_sb1', 'L1_ffn_sW2', 'L1_ffn_sb2', 'L1_ffn_sW3',
          'L1_ffn_sb3', 'L1_ffn_eW1', 'L1_ffn_eb1', 'L1_ffn_eW2', 'L1_ffn_eb2', 'L1_ffn_eW3', 'L1_ffn_eb3',
          'L1_ffn_gW', 'L1_ffn_gb']


def kernel(**inputs):
    import numpy as np
    import concourse.bacc as bacc
    from concourse.bass_utils import run_bass_kernel_spmd as run

    nc = bacc.Bacc("TRN2", target_bir_lowering=False, num_devices=1)
    arrays, io = {}, {}
    for name in INPUTS:
        a = np.ascontiguousarray(inputs[name])
        arrays["in_" + name] = a
        io[name] = nc.dram_tensor("in_" + name, a.shape, mybir.dt.from_np(a.dtype), kind="ExternalInput").ap()
    io["out"] = nc.dram_tensor("out_x", (N, D), F32, kind="ExternalOutput").ap()
    for name, shape, dt in (("starts_dram", (NW,), I32), ("buf_dram", (4096, D), F32), ("AT_dram", (N, N), F16),
                            ("dinv_dram", (N,), F32), ("s_dram", (N,), F32),
                            ("ybuf_dram", (4096, D), F32), ("top_dram", (NB, 5, B), F32)):
        io[name] = nc.dram_tensor(name, shape, dt).ap()
    program(nc, io)
    r = run(nc, [arrays], core_ids=[0])
    return r.results[0]["out_x"]
```

```python
from contextlib import ExitStack

import concourse.bass as bass
from concourse import mybir

F32 = mybir.dt.float32
F16 = mybir.dt.float16
BF16 = mybir.dt.bfloat16
I32 = mybir.dt.int32
U8 = mybir.dt.uint8
ALU = mybir.AluOpType
ACT = mybir.ActivationFunctionType
AX = mybir.AxisListType

P = 128
N = 3125
B = 125
NB = N // B
D = 256
KD = D // P
M = 53125
W = 5
NW = N // W
WB = B // W
EW = 128
EP = M // B
CB = 4
CN = CB * B
MAGIC = 1.5 * 2.0 ** 23
EPS = 1e-5


class Space:

    def __init__(self, nc, outer=None):
        self.nc, self.ctx, self.sems = nc, ExitStack(), []
        self.keeper = outer.keeper if outer else self

    def __enter__(self):
        return self

    def __exit__(self, *a):
        self.ctx.close()
        if self.sems:
            self.nc.clear_and_free_semaphores(self.sems)
            self.nc.all_engine_barrier()

    def sb(self, name, shape, dt=F32):
        return self.ctx.enter_context(self.nc.sbuf_tensor(name, list(shape), dt))

    def ps(self, name, shape, dt=F32):
        return self.ctx.enter_context(self.nc.psum_tensor(name, list(shape), dt))

    def sem(self, name):
        self.keeper.sems.append(self.nc.alloc_semaphore(name))
        return self.keeper.sems[-1]


def bc(ap, n, at):
    dims = [list(x) for x in ap.ap]
    dims.insert(at, [0, n])
    return bass.AP(ap.tensor, ap.offset, dims)


def split_dma(engine, out, in_, sem):
    for a, b in ((0, 112), (112, B)):
        engine.dma_start(out[a:b], in_[a:b]).then_inc(sem, 16)


def constants(nc, keep):
    c = {
        "ident": keep.sb("ident", [P, P]), "ident_h": keep.sb("ident_h", [P, P], F16),
        "iota_i": keep.sb("iota_i", [P, P], I32), "iota": keep.sb("iota", [P, P], BF16),
        "wbase_i": keep.sb("wbase_i", [B, W], I32), "wbase": keep.sb("wbase", [B, W]),
        "ones": keep.sb("ones", [P, P]), "ones_h": keep.sb("ones_h", [P, 1], F16),
    }
    return c


UN = 5


def gap(u, n):
    return next(d for d in range(1, UN + 1) if ((u - d) % UN) % n == u % n)


def blocks(engine, body):
    for u in range(UN):
        body(u, u, True)
    with engine.Fori(1, NB // UN) as i:
        for u in range(UN):
            body(UN * i + u, u, False)


def staggered(engine, *steps):
    lag = len(steps) - 1

    def turn(base, o, first):
        for d, step in enumerate(steps):
            t = base + o - d
            if isinstance(base, int) and not 0 <= t < NB:
                continue
            step(t, (o - d) % UN, first and t < UN)
    for o in range(UN + lag):
        turn(0, o, True)
    with engine.Fori(1, NB // UN - 1) as i:
        for o in range(lag, UN + lag):
            turn(UN * i, o, False)
    for o in range(lag, UN + lag + lag):
        turn(NB - UN, o, False)


def skip(t, u, first):
    pass


def chunks(engine, body):
    body(0, 0, CB)
    with engine.Fori(0, (NB // CB - 2) // 2) as i:
        body(2 * i + 1, 1, CB)
        body(2 * i + 2, 0, CB)
    body(NB // CB - 1, 1, CB)
    body(NB // CB, 0, NB % CB)


NC = NB // CB + 1


class Norm:

    def __init__(self, s, tag, stats):
        self.st = stats
        self.mean, self.dif, self.var, self.rstd, self.shift = (
            s.sb(tag + n, [B, NB]) for n in ("mean", "dif", "var", "rstd", "shift"))
        self.eps = s.sb(tag + "eps", [B, 1])
        self.xn = s.sb(tag + "xn", [B, UN, D])
        self.xt = s.sb(tag + "xt", [P, UN, KD, B])
        self.pt = [s.ps(f"{tag}pt{i}", [P, KD, B]) for i in range(3)]
        self.s_inv = s.sem(tag + "inv")
        self.s_v, self.s_var, self.s_std, self.s_rstd, self.s_xn, self.s_tr, self.s_xt, self.s_used = (
            s.sem(tag + n) for n in ("v", "var", "std", "rstd", "sxn", "str", "sxt", "used"))

    def stats(self, nc, dve):
        self.variance(nc, dve)
        self.inverse(nc, dve)

    def variance(self, nc, dve, n=0, q=slice(0, NB)):
        v = nc.vector
        m1, q1, m2, q2 = (self.st[:, q, i] for i in (1, 2, 4, 5))
        mean, dif, var = self.mean[:, q], self.dif[:, q], self.var[:, q]
        if n == 0:
            v.memset(self.eps[:], EPS)
        v.tensor_tensor(mean, m1, m2, ALU.add)
        v.tensor_tensor(dif, m1, m2, ALU.subtract)
        v.tensor_tensor(var, q1, q2, ALU.add).then_inc(self.s_v, 1)
        dve.wait_ge(self.s_v, 2 * n + 1)
        v.tensor_scalar(mean, mean, 0.5, None, ALU.mult)
        v.tensor_scalar(var, var, 1.0 / D, None, ALU.mult)
        v.scalar_tensor_tensor(dif, dif, 0.25, dif, ALU.mult, ALU.mult).then_inc(self.s_v, 1)
        dve.wait_ge(self.s_v, 2 * n + 2)
        v.tensor_tensor(var, var, dif, ALU.add).then_inc(self.s_var, 1)

    def inverse(self, nc, dve, n=0, q=slice(0, NB)):
        v = nc.vector
        dve.wait_ge(self.s_std, n + 1)
        v.reciprocal(self.rstd[:, q], self.dif[:, q]).then_inc(self.s_inv, 1)
        dve.wait_ge(self.s_inv, n + 1)
        v.scalar_tensor_tensor(self.shift[:, q], self.mean[:, q], -1.0, self.rstd[:, q], ALU.mult, ALU.mult).then_inc(self.s_rstd, 1)

    def std(self, nc, act, n=0, q=slice(0, NB)):
        act.wait_ge(self.s_var, n + 1)
        nc.scalar.activation(self.dif[:, q], self.var[:, q], ACT.Sqrt, bias=self.eps[:, 0:1]).then_inc(self.s_std, 1)

    def rows(self, nc, act, X, t, u, first):
        if not first:
            act.wait_ge(self.s_tr, t - UN + 1)
        nc.scalar.activation(self.xn[:, u, :], X[:, t, :], ACT.Identity, bias=self.shift[:, bass.ds(t, 1)],
                             scale=self.rstd[:, bass.ds(t, 1)]).then_inc(self.s_xn, 1)

    def turn(self, nc, pe, ident, t, u, first):
        pe.wait_ge(self.s_xn, t + 1)
        if not first or u >= 3:
            pe.wait_ge(self.s_xt, t - gap(u, 3) + 1)
        for k in range(KD):
            tr = nc.tensor.transpose(self.pt[u % 3][:, k, :], self.xn[:, u, k * P:(k + 1) * P], ident[0:B, 0:B])
        tr.then_inc(self.s_tr, 1)

    def out(self, nc, dve, t, u, first):
        if not first:
            dve.wait_ge(self.s_used, t - UN + 1)
        dve.wait_ge(self.s_tr, t + 1)
        return nc.vector.tensor_copy(self.xt[:, u, :, :], self.pt[u % 3][:]).then_inc(self.s_xt, 1)


class AttentionRows:

    def __init__(self, nc, s, io, c, X, ph, pw, norm):
        self.nc, self.io, self.c, self.X, self.ph, self.pw, self.norm = nc, io, c, X, ph, pw, norm
        self.st_cols = s.sb("st_cols", [B, NB, 2])
        self.s_col = s.sb("s_col", [B, NB])
        self.s_rows = s.sb("s_rows", [NB, B])
        self.w_cat = s.sb("w_cat", [P, KD, D + 2])
        self.w_t = s.sb("w_t", [P, KD, D])
        self.a_row = s.sb("a_row", [2 * KD, P])
        self.a_cols = s.sb("a_cols", [P, 2 * KD])
        (self.s_st, self.s_w, self.s_h1, self.s_fin, self.s_srow, self.s_wt, self.s_acol, self.s_wa, self.s_wcat, self.s_x,
         self.s_m, self.s_wl, self.s_al, self.s_so) = (
            s.sem("C_" + n) for n in ("st", "w", "h1", "fin", "srow", "wt", "acol", "wa", "wcat", "x", "m", "wl", "al", "so"))

    def load(self, sp):
        split_dma(sp, self.X[:], self.io["x"].rearrange("(t p) d -> p t d", p=B), self.s_x)
        sp.dma_start(self.w_cat[:, :, 0:D], self.io["L0_gnn_W"].rearrange("(k p) f -> p k f", p=P)).then_inc(self.s_wl, 16)
        sp.dma_start(self.a_row[:], self.io["L0_gnn_a"].rearrange("(r p) -> r p", p=P)).then_inc(self.s_al, 16)

    def store(self, sp):
        sp.wait_ge(self.s_srow, 1)
        sp.dma_start(self.io["s_dram"].rearrange("(b n) -> b n", n=B), self.s_rows[:]).then_inc(self.s_so, 16)
        sp.wait_ge(self.s_so, 16)

    def vector(self, dve):
        nc, io, norm, X, ph, pw = self.nc, self.io, self.norm, self.X, self.ph, self.pw
        v, w_cat, st_cols, h1 = nc.vector, self.w_cat, self.st_cols, io["h1"]
        dve.wait_ge(self.s_x, 32)
        with dve.Fori(0, NB // UN) as i:
            for u in range(UN):
                ins = v.bn_stats(io["stats"][:, UN * i + u, :], X[:, UN * i + u, :])
            ins.then_inc(self.s_m, 1)
        dve.wait_ge(self.s_m, NB // UN)
        norm.stats(nc, dve)
        dve.wait_ge(self.s_wt, 1)
        v.tensor_copy(self.a_cols[:], pw[:, 0:2 * KD]).then_inc(self.s_acol, 1)
        for k in range(KD):
            dve.wait_ge(self.s_wt, 2 + k)
            v.tensor_copy(self.w_t[:, :, k * P:(k + 1) * P], pw[:, 0:KD * P].rearrange("p (f i) -> p f i", f=KD)).then_inc(self.s_acol, 1)
        dve.wait_ge(self.s_wa, 1)
        v.tensor_copy(w_cat[:, :, D:D + 2], pw[:, 0:2 * KD].rearrange("p (k a) -> p k a", a=2)).then_inc(self.s_wcat, 1)

        def out(t, u, first):
            norm.out(nc, dve, t, u, first)

        def columns(t, u, first):
            dve.wait_ge(norm.s_used, t + 1)
            v.tensor_copy(st_cols[:, t, :], ph[u % 3][:, D:D + 2]).then_inc(self.s_st, 1)

        def weighted(t, u, first):
            dve.wait_ge(self.s_w, t + 1)
            v.tensor_scalar(h1[:, t, 0:D], ph[u % 3][:, 0:D], h1[:, t, D:D + 1], None, ALU.mult).then_inc(self.s_h1, 1)
        staggered(dve, out, columns, weighted)
        v.tensor_copy(self.s_col[:], st_cols[:, :, 0]).then_inc(self.s_fin, 1)
        v.tensor_scalar(io["t_bias"][:], st_cols[:, :, 1], -0.8, None, ALU.mult)
        dve.wait_ge(self.s_fin, 2)
        v.tensor_copy(self.s_rows[:], pw[0:NB, 0:B]).then_inc(self.s_srow, 1)

    def scalar(self, act):
        nc, io, norm, X = self.nc, self.io, self.norm, self.X
        st_cols, h1 = self.st_cols, io["h1"]
        norm.std(nc, act)
        act.wait_ge(norm.s_rstd, 1)

        def body(t, u, first):
            norm.rows(nc, act, X, t, u, first)

        def weight(t, u, first):
            act.wait_ge(self.s_st, t + 1)
            nc.scalar.activation(h1[:, t, D:D + 1], st_cols[:, t, 1:2], ACT.Exp, scale=-0.2).then_inc(self.s_w, 1)
        staggered(act, body, skip, weight)

    def tensor(self, pe):
        nc, norm, c, ph, pw = self.nc, self.norm, self.c, self.ph, self.pw
        t_, w_cat = nc.tensor, self.w_cat
        pe.wait_ge(self.s_al, 16)
        pe.wait_ge(self.s_wl, 16)
        t_.transpose(pw[:, 0:2 * KD], self.a_row[:], c["ident"][0:2 * KD, 0:2 * KD]).then_inc(self.s_wt, 1)
        for k in range(KD):
            pe.wait_ge(self.s_acol, 1 + k)
            for f in range(KD):
                tr = t_.transpose(pw[:, f * P:(f + 1) * P], w_cat[:, k, f * P:(f + 1) * P], c["ident"][:])
            tr.then_inc(self.s_wt, 1)
        pe.wait_ge(self.s_acol, 1 + KD)
        for k in range(KD):
            for f in range(KD):
                mm = t_.matmul(pw[:, 2 * k:2 * k + 2], self.w_t[:, f, k * P:(k + 1) * P],
                               self.a_cols[:].rearrange("p (a f) -> p f a", f=KD)[:, f, :], start=(f == 0), stop=(f == KD - 1))
        mm.then_inc(self.s_wa, 1)
        pe.wait_ge(self.s_wcat, 1)

        def turn(t, u, first):
            norm.turn(nc, pe, c["ident"], t, u, first)

        def body(t, u, first):
            pe.wait_ge(norm.s_xt, t + 1)
            if not first or u >= 3:
                pe.wait_ge(self.s_h1, t - gap(u, 3) + 1)
            for k in range(KD):
                mm = t_.matmul(ph[u % 3][:], norm.xt[:, u, k, :], w_cat[:, k, :], start=(k == 0), stop=(k == KD - 1))
            mm.then_inc(norm.s_used, 1)
        staggered(pe, turn, body)
        pe.wait_ge(self.s_fin, 1)
        t_.transpose(pw[0:NB, 0:B], self.s_col[:], c["ident"][0:B, 0:B]).then_inc(self.s_fin, 1)


def edge_windows(nc, io, c, keep, X, outer):
    with Space(nc, outer) as s:
        src_i, dst_i = (s.sb(n, [B, EP], I32) for n in ("src_i", "dst_i"))
        srcf, dstf = keep["srcf"], keep["dstf"]
        quot, rest, wrest, tmp = (s.sb(n, [B, EP]) for n in ("quot", "rest", "wrest", "tmp"))
        quot_b, wrest_b = s.sb("quot_b", [B, EP], BF16), s.sb("wrest_b", [B, EP, 2], BF16)
        oh_q, oh_w = s.sb("oh_q", [B, EP, NB], BF16), s.sb("oh_w", [B, EP, NB + 1], BF16)
        blk = s.sb("blk", [B, W, NB])
        picked = s.sb("picked", [B, W, NB])
        hist = s.sb("hist", [B, NB])
        hist_in = s.sb("hist_in", [B, NB])
        hist_ex = s.sb("hist_ex", [B, NB])
        hist_all = s.sb("hist_all", [B, 1])
        hist_rows = s.sb("hist_rows", [B, NB])
        zero25 = s.sb("zero25", [B, NB])
        sel, sel_in, sel_lt = (s.sb(n, [B, NB]) for n in ("sel", "sel_in", "sel_lt"))
        starts_f = s.sb("starts_f", [NB, WB])
        starts_i = s.sb("starts_i", [NB, WB], I32)
        start = s.sb("start", [B, W], I32)
        g_src, g_dst = (s.sb(n, [B, W, EW], I32) for n in ("g_src", "g_dst"))
        gs, gd, ghi, g1, g2 = (s.sb(n, [B, W, EW]) for n in ("gs", "gd", "ghi", "g1", "g2"))
        held = s.sb("held", [B, 1])
        norm = Norm(s, "n1", io["stats"])
        nodes = AttentionRows(nc, s, io, c, X, [s.ps(f"ph{i}", [B, D + 2]) for i in range(3)], s.ps("pw", [P, 512]), norm)
        ph = s.ps("hist_pairs", [B, W, NB])
        pst = nodes.pw[0:NB, 0:WB]
        pcnt = nodes.pw[:, WB:WB + 1]
        pt = [norm.pt[i][:].rearrange("p k b -> p (k b)") for i in range(2)]
        s_dst, s_src, s_const, s_conv, s_oh, s_hist = (s.sem("A_" + n) for n in ("dst", "src", "const", "conv", "oh", "hist"))
        s_v, s_st, s_starts, s_stout, s_stin = (s.sem("A_" + n) for n in ("v", "st", "starts", "stout", "stin"))
        s_gs, s_gd = ([s.sem(f"A_{n}{k}") for k in range(W)] for n in ("gs", "gd"))
        s_code, s_tr, s_tc, s_cnt, s_id, s_zero = (s.sem("A_" + n) for n in ("code", "tr", "tc", "cnt", "id", "zero"))
        starts_dram = io["starts_dram"]
        groups = [(e, min(e + 85, EP)) for e in range(0, EP, 85)]

        with nc.Block() as block:
            @block.sync
            def _(sp):
                sp.dma_start(dst_i[:], io["dst"].rearrange("(p e) -> p e", p=B)).then_inc(s_dst, 16)
                sp.dma_start(src_i[:], io["src"].rearrange("(p e) -> p e", p=B)).then_inc(s_src, 16)
                nodes.load(sp)
                sp.wait_ge(s_zero, 1)
                for k in range(4):
                    sp.dma_start(io["buf_dram"].rearrange("(k p r) d -> k p (r d)", k=4, p=P)[k],
                                 keep["zeros"][:]).then_inc(io["s_buf_zero"], 16)
                sp.wait_ge(s_starts, 1)
                sp.dma_start(starts_dram.rearrange("(q w) -> q w", q=NB), starts_i[:]).then_inc(s_stout, 16)
                sp.wait_ge(s_stout, 16)
                sp.dma_start(start[:], starts_dram.rearrange("(p k) -> p k", k=W)).then_inc(s_stin, 16)
                nodes.store(sp)
                sp.wait_ge(io["s_buf_zero"], 64)

            @block.gpsimd
            def _(pool):
                g = nc.gpsimd
                g.iota(c["iota_i"][:], [[1, P]], base=0, channel_multiplier=0).then_inc(s_const, 1)
                g.iota(c["wbase_i"][:], [[W, W]], base=0, channel_multiplier=W * W).then_inc(s_const, 1)
                g.memset(c["ident"][:], 0.0).then_inc(s_id, 1)
                g.memset(blk[:], 1.0).then_inc(s_id, 1)
                pool.wait_ge(s_id, 2)
                g.affine_select(out=c["ident"][:], in_=c["ident"][:], compare_op=ALU.not_equal, fill=1.0, base=0,
                                pattern=[[-1, P]], channel_multiplier=1).then_inc(s_const, 1)
                g.affine_select(out=blk[:], in_=blk[:], compare_op=ALU.is_ge, fill=0.0, base=0,
                                pattern=[[-NB, W], [0, NB]], channel_multiplier=1).then_inc(s_id, 1)
                pool.wait_ge(s_id, 3)
                g.affine_select(out=blk[:], in_=blk[:], compare_op=ALU.is_ge, fill=0.0, base=NB - 1,
                                pattern=[[NB, W], [0, NB]], channel_multiplier=-1).then_inc(s_const, 1)
                g.memset(keep["zeros"][:], 0.0).then_inc(s_zero, 1)
                pool.wait_ge(s_stin, 16)
                for k in range(W):
                    for ids, got, sg in ((io["dst"], g_dst, s_gd), (io["src"], g_src, s_gs)):
                        g.indirect_dma_start(got[:, k, :], None, ids.rearrange("(m o) -> m o", o=1),
                                             bass.IndirectOffsetOnAxis(ap=start[:, k:k + 1], axis=0)
                                             ).then_inc(sg[k], 16)
                for k in range(W):
                    pool.wait_ge(s_gd[k], 16)
                    pool.wait_ge(s_gs[k], 16)

            @block.vector
            def _(dve):
                v = nc.vector
                n = [0]

                def step(ins):
                    n[0] += 1
                    ins.then_inc(s_v, 1)
                    dve.wait_ge(s_v, n[0])

                def floor_div(out, x, t, by):
                    step(v.tensor_scalar(t, x, float(-(by // 2)), 1.0 / by, ALU.add, ALU.mult))
                    step(v.tensor_scalar(t, t, MAGIC, None, ALU.add))
                    step(v.tensor_scalar(out, t, -MAGIC, None, ALU.add))

                v.memset(c["ones"][:], 1.0)
                v.memset(c["ones_h"][:], 1.0)
                dve.wait_ge(s_const, 4)
                v.tensor_copy(c["ident_h"][:], c["ident"][:])
                v.tensor_copy(c["wbase"][:], c["wbase_i"][:])
                step(v.tensor_copy(c["iota"][:], c["iota_i"][:]))
                dve.wait_ge(s_dst, 16)
                step(v.tensor_copy(dstf[:], dst_i[:]))
                floor_div(quot[:], dstf[:], tmp[:], B)
                step(v.scalar_tensor_tensor(rest[:], quot[:], float(-B), dstf[:], ALU.mult, ALU.add))
                floor_div(wrest[:], rest[:], tmp[:], W)
                v.tensor_copy(quot_b[:], quot[:])
                step(v.tensor_copy(wrest_b[:], bc(wrest[:], 2, 2)))
                for a, b in groups:
                    v.tensor_tensor(oh_q[:, a:b, :], bc(quot_b[:, a:b], NB, 2), bc(c["iota"][0:B, 0:NB], b - a, 1), ALU.is_equal)
                    ins = v.tensor_tensor(oh_w[:, a:b, :].rearrange("p e (q r) -> p e q r", r=2),
                                          bc(wrest_b[:, a:b, :], (NB + 1) // 2, 2),
                                          bc(c["iota"][0:B, 0:NB + 1].rearrange("p (q r) -> p q r", r=2), b - a, 1),
                                          ALU.is_equal)
                    ins.then_inc(s_oh, 1)
                dve.wait_ge(s_src, 16)
                step(v.tensor_copy(srcf[:], src_i[:]))
                step(v.tensor_reduce(sel[:], c["ident"][0:B, 0:B].rearrange("p (a q) -> p q a", q=NB), AX.X, ALU.add))
                step(v.memset(zero25[:], 0.0))
                step(v.tensor_tensor_scan(sel_in[:], sel[:], zero25[:], 0.0, ALU.add, ALU.add))
                step(v.tensor_tensor(sel_lt[:], sel_in[:], sel[:], ALU.subtract))
                dve.wait_ge(s_hist, 1)
                step(v.tensor_tensor(picked[:], ph[:], blk[:], ALU.mult))
                step(v.tensor_reduce(hist[:], picked[:].rearrange("p a w -> p w a"), AX.X, ALU.add))
                step(v.tensor_reduce(hist_all[:], hist[:], AX.X, ALU.add))
                step(v.tensor_scalar(hist_rows[:], zero25[:], hist_all[:, 0:1], None, ALU.add))
                step(v.tensor_tensor_scan(hist_in[:], hist[:], zero25[:], 0.0, ALU.add, ALU.add))
                v.tensor_tensor(hist_ex[:], hist_in[:], hist[:], ALU.subtract).then_inc(s_st, 1)
                dve.wait_ge(s_st, 2)
                step(v.tensor_scalar(starts_f[:], pst, float(M - EW), None, ALU.min))
                v.tensor_copy(starts_i[:], starts_f[:]).then_inc(s_starts, 1)
                nodes.vector(dve)
                for k in range(W):
                    dve.wait_ge(s_gd[k], 16)
                    dve.wait_ge(s_gs[k], 16)
                step(v.tensor_copy(gs[:], g_src[:]))
                step(v.tensor_copy(gd[:], g_dst[:]))
                floor_div(ghi[:], gs[:], g1[:], B)
                step(v.scalar_tensor_tensor(gs[:], ghi[:], float(-B), gs[:], ALU.mult, ALU.add))
                step(v.tensor_tensor(gd[:], gd[:], bc(c["wbase"][:], EW, 2), ALU.subtract))
                step(v.tensor_scalar(g1[:], gd[:], 0.0, None, ALU.is_ge))
                step(v.tensor_scalar(g2[:], gd[:], float(W - 1), None, ALU.is_le))
                step(v.tensor_tensor(g1[:], g1[:], g2[:], ALU.mult))
                v.tensor_reduce(held[:], g1[:], AX.XY, ALU.add).then_inc(s_cnt, 1)
                step(v.scalar_tensor_tensor(ghi[:], ghi[:], float(W), gd[:], ALU.mult, ALU.add))
                step(v.tensor_scalar(ghi[:], ghi[:], 1.0, None, ALU.add))
                step(v.tensor_tensor(ghi[:], ghi[:], g1[:], ALU.mult))
                v.tensor_scalar(ghi[:], ghi[:], -1.0, None, ALU.add).then_inc(s_code, 1)
                for i in range(2 * W):
                    dve.wait_ge(s_tr, i + 1)
                    out = keep["lo"] if i % 2 == 0 else keep["code"]
                    v.tensor_copy(out[:].rearrange("e (p k) r -> e p k r", k=W)[:, :, i // 2, :], bc(pt[i % 2][0:EW, 0:B], 2, 2)).then_inc(s_tc, 1)
                dve.wait_ge(s_cnt, 2)
                v.tensor_copy(keep["captured"][:], pcnt[0:1, :])

            @block.scalar
            def _(act):
                nodes.scalar(act)

            @block.tensor
            def _(pe):
                t = nc.tensor
                per = EP // W
                for g, (a, b) in enumerate(groups):
                    pe.wait_ge(s_oh, g + 1)
                    for e in range(a, b, W):
                        mm = t.matmul(ph[:].rearrange("p a w -> p (a w)"), oh_q[:, e:e + W, :].rearrange("p e q -> p (e q)"),
                                      oh_w[:, e:e + W, 0:NB], start=(e == 0), stop=(e == EP - W))
                mm.then_inc(s_hist, 1)
                pe.wait_ge(s_st, 1)
                t.matmul(pst, sel[:], hist_ex[:], start=True, stop=False)
                t.matmul(pst, sel_lt[:], hist_rows[:], start=False, stop=True).then_inc(s_st, 1)
                pe.wait_ge(s_starts, 1)
                nodes.tensor(pe)
                pe.wait_ge(s_cnt, 1)
                t.matmul(pcnt, c["ones"][0:B, :], held[:], start=True, stop=True).then_inc(s_cnt, 1)
                pe.wait_ge(s_code, 1)
                for i in range(2 * W):
                    if i >= 2:
                        pe.wait_ge(s_tc, i - 1)
                    t.transpose(pt[i % 2][0:EW, 0:B], (gs if i % 2 == 0 else ghi)[:, i // 2, :],
                                c["ident"][0:B, 0:B]).then_inc(s_tr, 1)


def count_matrix(nc, io, c, keep, outer):
    with Space(nc, outer) as s:
        oh_lo, oh_code = (s.sb(n, [EW, 2, WB, P], BF16) for n in ("oh_lo", "oh_code"))
        ai = s.sb("ai", [B, 2, NB, B], F16)
        at = s.sb("at", [B, 2, N], F16)
        degs = s.sb("degs", [B, NB])
        dinv = s.sb("dinv", [B, NB])
        dinv_t = s.sb("dinv_t", [NB, B])
        count = [s.ps(f"count{i}", [P, CB, B]) for i in range(3)]
        turned = [s.ps(f"turned{i}", [B, 8, P], F16) for i in range(4)]
        small = s.ps("small", [P, 2 * P + NB])
        pdeg = small[0:B, 2 * P:]
        pdt = small[0:NB, 0:B]
        s_ata = s.sem("B_ata")
        s_oh, s_mm, s_ai, s_tr, s_at, s_deg, s_degacc, s_fin = (
            s.sem("B_" + n) for n in ("oh", "mm", "ai", "tr", "at", "deg", "degacc", "fin"))
        s_store = [s.sem(f"B_store{i}") for i in range(2)]
        s_dinv = s.sem("B_dinv")
        lo_v = keep["lo"][:].rearrange("e (b w) r -> e b w r", w=WB)
        code_v = keep["code"][:].rearrange("e (b w) r -> e b w r", w=WB)
        at_rows = io["AT_dram"].rearrange("(b j) i -> b j i", j=B)
        wgroups = [(w, min(w + CB, WB)) for w in range(0, WB, CB)]
        tgroups = [(h, min(h + 8, NB)) for h in range(0, NB, 8)]
        NG, NT = len(wgroups), len(tgroups)
        assert NG == 7 and NT == 4
        act_groups, dve_groups = (1, 2), (0, 3)
        NA, ND = len(act_groups), len(dve_groups)
        captured = keep["captured"][0:1, 0:1]

        def over_blocks(engine, *steps):
            def turn(base, half, o):
                for ahead, step in steps:
                    jb = base + o + ahead
                    if not isinstance(base, int):
                        step(jb, (o + ahead) % 2, False, half + (o + ahead) // 2)
                    elif 0 <= jb < NB:
                        step(jb, jb % 2, jb < 2, jb // 2)
            for t in range(-4, 1):
                turn(0, 0, t)
            with engine.Fori(0, (NB - 5) // 2) as h:
                turn(2 * h, h, 1)
                turn(2 * h, h, 2)
            for t in range(NB - 4, NB - 1):
                turn(0, 0, t)

        src_row = s.sb("src_row", [B, N])
        src_row_i = s.sb("src_row_i", [B, N], I32)
        dst_rel = s.sb("dst_rel", [B, EP])
        oh_src = s.sb("oh_src", [B, 2, N], BF16)
        oh_dst = s.sb("oh_dst", [B, 2, B], BF16)
        g_iota, g_row, g_rel, g_oh, g_mm, g_done, g_at = (s.sem("G_" + n) for n in ("iota", "row", "rel", "oh", "mm", "done", "at"))
        cgroups = [(i, min(i + CB, NB)) for i in range(0, NB, CB)]

        def bank(i):
            if i < 3:
                return count[i][0:B].rearrange("j w n -> j (w n)")
            if i < 6:
                return turned[i - 3][:].rearrange("j b n -> j (b n)").bitcast(F32)
            return small[0:B, P:P + B]

        with nc.Block() as block:
            @block.vector
            def _(dve):
                v = nc.vector
                nv = 0

                def one_hots(jb, k, first, half):
                    if not first:
                        dve.wait_ge(s_mm, NG * (jb - 1))
                    for a, b in wgroups:
                        for oh, code in ((oh_lo, lo_v), (oh_code, code_v)):
                            ins = v.tensor_tensor(oh[:, k, a:b, :].rearrange("e w (n r) -> e w n r", r=2),
                                                  bc(code[:, jb, a:b, :], P // 2, 2),
                                                  bc(c["iota"][:].rearrange("e (n r) -> e n r", r=2), b - a, 1), ALU.is_equal)
                        ins.then_inc(s_oh, 1)

                def rows(jb, k, first, half):
                    if not first:
                        dve.wait_ge(s_store[k], 32 * half)
                        dve.wait_ge(s_deg, jb - 1)
                    for i in dve_groups:
                        a, b = tgroups[i]
                        dve.wait_ge(s_tr, NT * jb + i + 1)
                        v.tensor_copy(at[:, k, a * B:b * B].rearrange("j (h n) -> j h n", n=B),
                                      turned[i][:, 0:b - a, 0:B]).then_inc(s_at, 1)

                def degrees(jb, k, first, half):
                    dve.wait_ge(s_deg, jb + 1)
                    dve.wait_ge(s_degacc, jb + 1)
                    v.tensor_tensor(degs[:], pdeg, degs[:], ALU.add).then_inc(s_degacc, 1)

                v.memset(degs[:], 0.0).then_inc(s_degacc, 1)
                how = dve.value_load(captured, min_val=0, max_val=M)
                with dve.If(how == M):
                    over_blocks(dve, (4, one_hots), (2, rows), (1, degrees))
                with dve.If(how != M):
                    dve.wait_ge(g_iota, 1)
                    v.tensor_copy(src_row[:], src_row_i[:]).then_inc(g_row, 1)
                    v.tensor_copy(dst_rel[:], keep["dstf"][:]).then_inc(g_row, 1)
                    dve.wait_ge(g_row, 2)
                    with dve.Fori(0, NB) as jb:
                        def pair(e, k, first):
                            if not first:
                                dve.wait_ge(g_mm, jb * EP + e - 1)
                            v.tensor_scalar(oh_dst[:, k, :], c["iota"][0:B, 0:B], dst_rel[:, bass.ds(e, 1)], None, ALU.is_equal)
                            v.tensor_scalar(oh_src[:, k, :], src_row[:], keep["srcf"][:, bass.ds(e, 1)], None, ALU.is_equal).then_inc(g_oh, 1)
                        pair(0, 0, True)
                        pair(1, 1, True)
                        pair(2, 0, False)
                        with dve.Fori(0, (EP - 3) // 2) as h:
                            pair(2 * h + 3, 1, False)
                            pair(2 * h + 4, 0, False)
                        dve.wait_ge(g_mm, (jb + 1) * EP)
                        v.tensor_scalar(dst_rel[:], dst_rel[:], float(-B), None, ALU.add).then_inc(g_rel, 1)
                        dve.wait_ge(g_rel, jb + 1)
                        dve.wait_ge(s_deg, jb + 1)
                        v.tensor_tensor(degs[:], pdeg, degs[:], ALU.add).then_inc(s_degacc, 1)
                        dve.wait_ge(s_degacc, jb + 2)
                dve.wait_ge(s_degacc, NB + 1)
                v.tensor_scalar(degs[:], degs[:], 1.0, None, ALU.max).then_inc(s_fin, 1)
                dve.wait_ge(s_fin, 1)
                v.reciprocal(dinv[:], degs[:]).then_inc(s_fin, 1)
                dve.wait_ge(s_fin, 3)
                v.tensor_copy(dinv_t[:], pdt).then_inc(s_fin, 1)

            @block.scalar
            def _(act):
                a_ = nc.scalar

                def counts(jb, k, first, half):
                    if not first:
                        act.wait_ge(s_tr, NT * (jb - 1))
                    for i, (a, b) in enumerate(wgroups):
                        act.wait_ge(s_mm, NG * jb + i + 1)
                        a_.activation(ai[:, k, :, a * W:b * W].rearrange("n h (w d) -> n w h d", d=W),
                                      count[i % 3][0:B, 0:b - a, :].rearrange("n w (h d) -> n w h d", d=W),
                                      ACT.Copy).then_inc(s_ai, 1)

                def rows(jb, k, first, half):
                    if not first:
                        act.wait_ge(s_store[k], 32 * half)
                        act.wait_ge(s_deg, jb - 1)
                    for i in act_groups:
                        a, b = tgroups[i]
                        act.wait_ge(s_tr, NT * jb + i + 1)
                        a_.activation(at[:, k, a * B:b * B].rearrange("j (h n) -> j h n", n=B),
                                      turned[i][:, 0:b - a, 0:B], ACT.Copy).then_inc(s_ata, 1)

                how = act.value_load(captured, min_val=0, max_val=M)
                with act.If(how == M):
                    over_blocks(act, (3, counts), (2, rows))
                with act.If(how != M):
                    with act.Fori(0, NB) as jb:
                        act.wait_ge(g_done, jb + 1)
                        for i, (a, b) in enumerate(cgroups):
                            ins = a_.activation(at[:, 0, a * B:b * B], bank(i)[:, 0:(b - a) * B], ACT.Copy)
                        ins.then_inc(g_at, 1)
                        act.wait_ge(s_store[0], 32 * (jb + 1))

            @block.tensor
            def _(pe):
                t = nc.tensor

                def before(jb, i):
                    return NG * jb + i - 2 if i >= 3 else NG * (jb - 1) + max(g for g in range(NG) if g % 3 == i) + 1

                def windows(i, jb, k):
                    a, b = wgroups[i]
                    pe.wait_ge(s_oh, NG * jb + i + 1)
                    if i >= 3 or not (isinstance(jb, int) and jb == 0):
                        pe.wait_ge(s_ai, before(jb, i))
                    for w in range(a, b):
                        mm = t.matmul(count[i % 3][:, w - a, :], oh_lo[:, k, w, :], oh_code[:, k, w, 0:B], start=True, stop=True)
                    mm.then_inc(s_mm, 1)

                def turned_rows(i, jb, k):
                    a, b = tgroups[i]
                    pe.wait_ge(s_ai, NG * (jb + 1))
                    if not (isinstance(jb, int) and jb == 0):
                        if i in act_groups:
                            pe.wait_ge(s_ata, NA * (jb - 1) + act_groups.index(i) + 1)
                        else:
                            pe.wait_ge(s_at, ND * (jb - 1) + dve_groups.index(i) + 1)
                    for h in range(a, b):
                        mm = t.transpose(turned[i][:, h - a, 0:B], ai[:, k, h, :], c["ident_h"][0:B, 0:B])
                    mm.then_inc(s_tr, 1)

                def degree(i, jb, k):
                    if i == 0:
                        pe.wait_ge(s_at, ND * (jb + 1))
                        pe.wait_ge(s_ata, NA * (jb + 1))
                        pe.wait_ge(s_degacc, jb + 1)
                    a, b = tgroups[i]
                    for h in range(a, b):
                        mm = t.matmul(pdeg[:, h:h + 1], at[:, k, h * B:(h + 1) * B], c["ones_h"][0:B, :], start=True, stop=True)
                    if i == NT - 1:
                        mm.then_inc(s_deg, 1)

                def piece(part, i):
                    return lambda jb, k, first, half: part(i, jb, k)

                how = pe.value_load(captured, min_val=0, max_val=M)
                with pe.If(how == M):
                    over_blocks(pe, *[(ahead, piece(part, i)) for ahead, part, i in (
                        (3, windows, 0), (2, turned_rows, 0), (3, windows, 1), (2, turned_rows, 1),
                        (3, windows, 2), (2, turned_rows, 2), (3, windows, 3), (2, turned_rows, 3), (1, degree, 0),
                        (3, windows, 4), (1, degree, 1), (3, windows, 5), (1, degree, 2), (3, windows, 6), (1, degree, 3))])
                with pe.If(how != M):
                    with pe.Fori(0, NB) as jb:
                        def chunk(e, k, start=False, stop=False):
                            pe.wait_ge(g_oh, jb * EP + e + 1)
                            for i, (a, b) in enumerate(cgroups):
                                mm = t.matmul(bank(i)[:, 0:(b - a) * B], oh_dst[:, k, :], oh_src[:, k, a * B:b * B],
                                              start=start, stop=stop)
                            mm.then_inc(g_mm, 1)
                            return mm
                        chunk(0, 0, start=True)
                        with pe.Fori(0, (EP - 3) // 2) as h:
                            chunk(2 * h + 1, 1)
                            chunk(2 * h + 2, 0)
                        chunk(EP - 2, 1)
                        chunk(EP - 1, 0, stop=True)
                        pe.drain().then_inc(g_done, 1)
                        pe.wait_ge(g_at, jb + 1)
                        for h in range(NB):
                            mm = t.matmul(pdeg[:, h:h + 1], at[:, 0, h * B:(h + 1) * B], c["ones_h"][0:B, :], start=True, stop=True)
                        mm.then_inc(s_deg, 1)
                pe.wait_ge(s_fin, 2)
                t.transpose(pdt, dinv[:], c["ident"][0:B, 0:B]).then_inc(s_fin, 1)

            @block.gpsimd
            def _(pool):
                how = pool.value_load(captured, min_val=0, max_val=M)
                with pool.If(how != M):
                    nc.gpsimd.iota(src_row_i[:], [[1, N]], base=0, channel_multiplier=0).then_inc(g_iota, 1)

            @block.sync
            def _(sp):
                how = sp.value_load(captured, min_val=0, max_val=M)
                with sp.If(how == M):
                    with sp.Fori(0, 12) as h:
                        for k in range(2):
                            sp.wait_ge(s_at, ND * (2 * h + k + 1))
                            sp.wait_ge(s_ata, NA * (2 * h + k + 1))
                            split_dma(sp, at_rows[2 * h + k], at[:, k, :], s_store[k])
                    sp.wait_ge(s_at, ND * NB)
                    sp.wait_ge(s_ata, NA * NB)
                    split_dma(sp, at_rows[NB - 1], at[:, 0, :], s_store[0])
                    sp.wait_ge(s_store[0], 32 * 13)
                    sp.wait_ge(s_store[1], 32 * 12)
                with sp.If(how != M):
                    with sp.Fori(0, NB) as jb:
                        sp.wait_ge(g_at, jb + 1)
                        split_dma(sp, at_rows[jb], at[:, 0, :], s_store[0])
                    sp.wait_ge(s_store[0], 32 * NB)
                sp.wait_ge(s_fin, 4)
                sp.dma_start(io["dinv_dram"].rearrange("(b n) -> b n", n=B), dinv_t[:]).then_inc(s_dinv, 16)
                sp.wait_ge(s_dinv, 16)


def graph_attention(nc, io, c, X, outer):
    HW = D + 1
    with Space(nc, outer) as s:
        h1, t_bias = io["h1"], io["t_bias"]
        s_part = s.sb("s_part", [B, 2, CN])
        a_chunk = s.sb("a_chunk", [B, 2, NB, CN], F16)
        s_sl, s_chunk = ([s.sem(f"C_{n}{i}") for i in range(2)] for n in ("sl", "chunk"))
        s_first = [s.sem(f"C_first{i}") for i in range(NB // UN)]
        s_exp, s_e, s_mm, s_rs, s_o, s_res = (s.sem("C_" + n) for n in ("exp", "e", "mm", "rs", "o", "res"))
        at_v = io["AT_dram"].rearrange("(b j) i -> j b i", j=B)

        def loads(c_, k, loop):
            return c_ // 2 + 1 if isinstance(c_, int) else loop[0] + 1 + (1 - k)

        with Space(nc, s) as s2:
            et, e = (s2.sb(n, [B, UN, CN]) for n in ("et", "e"))
            rs = s2.sb("rs", [B, 2, CB])
            o = s2.sb("o", [B, 2, CB, D])
            acc = [[s2.ps(f"acc{k}_{b}", [B, HW]) for b in range(CB)] for k in range(2)]
            with nc.Block() as block:
                @block.sync
                def _(sp):
                    sp.dma_start(s_part[:, 0], bc(io["s_dram"][0:CN], B, 0)).then_inc(s_sl[0], 16)
                    for i, sem in enumerate(s_first):
                        js = slice(UN * i, UN * (i + 1))
                        split_dma(sp, a_chunk[:, 0, js, :], at_v[:, js, 0:CN], sem)
                    sp.dma_start(s_part[:, 1], bc(io["s_dram"][CN:2 * CN], B, 0)).then_inc(s_sl[1], 16)
                    split_dma(sp, a_chunk[:, 1], at_v[:, :, CN:2 * CN], s_chunk[1])

                    def body(c_, k, nb):
                        sp.wait_ge(s_e, NB * (c_ - 1))
                        split_dma(sp, a_chunk[:, k, :, 0:nb * B], at_v[:, :, bass.ds(c_ * CN, nb * B)], s_chunk[k])
                        sp.dma_start(s_part[:, k, 0:nb * B], bc(io["s_dram"][bass.ds(c_ * CN, nb * B)], B, 0)).then_inc(s_sl[k], 16)
                    with sp.Fori(1, NC // 2) as i:
                        body(2 * i, 0, CB)
                        body(2 * i + 1, 1, CB)
                    body(NC - 1, 0, NB % CB)

                @block.scalar
                def _(act):
                    def body(c_, k, nb):
                        act.wait_ge(s_sl[k], 16 * loads(c_, k, loop))
                        for j in range(NB):
                            n = c_ * NB + j
                            if not (isinstance(c_, int) and n < UN):
                                act.wait_ge(s_e, n - UN + 1)
                            nc.scalar.activation(et[:, j % UN, 0:nb * B], s_part[:, k, 0:nb * B], ACT.Exp,
                                                 bias=t_bias[:, j:j + 1], scale=-0.8).then_inc(s_exp, 1)
                    loop = []
                    body(0, 0, CB)
                    with act.Fori(0, (NC - 3) // 2) as i:
                        loop.append(i)
                        body(2 * i + 1, 1, CB)
                        body(2 * i + 2, 0, CB)
                    body(NC - 2, 1, CB)
                    body(NC - 1, 0, NB % CB)

                @block.vector
                def _(dve):
                    v = nc.vector
                    dve.sem_inc(s_o, 1)

                    def finish(c_, k, nb):
                        dve.wait_ge(s_mm, NB * (c_ + 1))
                        for b in range(nb):
                            ins = v.reciprocal(rs[:, k, b:b + 1], acc[k][b][:, D:D + 1])
                        ins.then_inc(s_rs, 1)
                        dve.wait_ge(s_rs, c_ + 1)
                        for b in range(nb):
                            ins = v.tensor_scalar(o[:, k, b, :], acc[k][b][:, 0:D], rs[:, k, b:b + 1], 0.0, ALU.mult, ALU.max)
                        ins.then_inc(s_o, 1)
                        dve.wait_ge(s_o, c_ + 2)
                        xs = X[:, bass.ds(c_ * CB, nb), :]
                        v.tensor_tensor(xs, xs, o[:, k, 0:nb, :], ALU.add).then_inc(s_res, 1)
                        dve.wait_ge(s_res, c_ + 1)
                        for b in range(nb):
                            v.bn_stats(io["stats"][:, c_ * CB + b, :], X[:, c_ * CB + b, :])

                    def body(c_, k, nb):
                        if not (isinstance(c_, int) and c_ == 0):
                            dve.wait_ge(s_chunk[k], 32 * (loads(c_, k, loop) - (1 - k)))
                        for j in range(NB):
                            if isinstance(c_, int) and c_ == 0 and j % UN == 0:
                                dve.wait_ge(s_first[j // UN], 32)
                            n = c_ * NB + j
                            dve.wait_ge(s_exp, n + 1)
                            if not (isinstance(c_, int) and n < UN):
                                dve.wait_ge(s_mm, n - UN + 1)
                            v.scalar_tensor_tensor(e[:, j % UN, 0:nb * B], et[:, j % UN, 0:nb * B], 1.0,
                                                   a_chunk[:, k, j, 0:nb * B], ALU.min, ALU.mult).then_inc(s_e, 1)
                            if j == 3 and not (isinstance(c_, int) and c_ == 0):
                                finish(c_ - 1, 1 - k, CB)
                    loop = []
                    body(0, 0, CB)
                    with dve.Fori(0, (NC - 3) // 2) as i:
                        loop.append(i)
                        body(2 * i + 1, 1, CB)
                        body(2 * i + 2, 0, CB)
                    body(NC - 2, 1, CB)
                    body(NC - 1, 0, NB % CB)
                    finish(NC - 1, 0, NB % CB)

                @block.tensor
                def _(pe):
                    def body(c_, k, nb):
                        if not (isinstance(c_, int) and c_ < 2):
                            pe.wait_ge(s_o, c_)
                        for j in range(NB):
                            pe.wait_ge(s_e, c_ * NB + j + 1)
                            for b in range(nb):
                                mm = nc.tensor.matmul(acc[k][b][:], e[:, j % UN, b * B:(b + 1) * B], h1[:, j, :],
                                                      start=(j == 0), stop=(j == NB - 1))
                            mm.then_inc(s_mm, 1)
                    chunks(pe, body)


class Tokens:

    def __init__(self, nc, s, io, X):
        self.nc, self.io, self.X = nc, io, X
        self.all = s.sb("rows_all", [P, NB * D])
        self.rows = self.all[0:B].rearrange("p (t d) -> p t d", d=D)
        self.slot_out = s.sb("slot_out", [B, NB], I32)
        self.weight = s.sb("weight", [B, NB])
        self.slots = -(-5 * N // (4 * io["L0_ffn_gate_w"].shape[1])) * io["L0_ffn_gate_w"].shape[1]

    def temporaries(self, s):
        self.low, self.high = (s.sb(n, [B, UN, D]) for n in ("low", "high"))
        self.finite = s.sb("finite", [B, UN, D], U8)
        self.s_g = [s.sem(f"F_g{t}") for t in range(NB)]
        self.s_v, self.s_val, self.s_bn = s.sem("F_v"), s.sem("F_val"), s.sem("F_bn")

    def gather(self, pool):
        for t in range(NB):
            self.nc.gpsimd.indirect_dma_start(self.rows[:, t, :], None, self.io["ybuf_dram"][0:self.slots, :],
                                              bass.IndirectOffsetOnAxis(ap=self.slot_out[:, t:t + 1], axis=0)).then_inc(self.s_g[t], 16)

    def weigh(self, act, t):
        act.wait_ge(self.s_g[t], 16)
        self.nc.scalar.activation(self.rows[:, t, :], self.rows[:, t, :], ACT.Copy, scale=self.weight[:, t:t + 1]).then_inc(self.s_val, 1)

    def add(self, dve, q, piece):
        v, s_v, low, high = self.nc.vector, self.s_v, self.low, self.high
        val, xs = self.rows[:, UN * q:UN * (q + 1), :], self.X[:, UN * q:UN * (q + 1), :]
        if piece == 0:
            dve.wait_ge(self.s_val, UN * (q + 1))
            v.tensor_scalar(self.finite[:], val, 0.0, 0.0, ALU.mult, ALU.is_equal)
            v.tensor_scalar(low[:], val, 0.0, -1e4, ALU.min, ALU.max)
            v.tensor_scalar(high[:], val, 0.0, 1e4, ALU.max, ALU.min).then_inc(s_v, 1)
        elif piece == 1:
            dve.wait_ge(s_v, 4 * q + 1)
            v.tensor_tensor(low[:], low[:], high[:], ALU.add).then_inc(s_v, 1)
        elif piece == 2:
            dve.wait_ge(s_v, 4 * q + 2)
            v.copy_predicated(low[:], self.finite[:], val).then_inc(s_v, 1)
        elif piece == 3:
            dve.wait_ge(s_v, 4 * q + 3)
            v.tensor_tensor(xs, xs, low[:], ALU.add).then_inc(s_v, 1)
        else:
            dve.wait_ge(s_v, 4 * q + 4)
            for t in range(UN * q, UN * (q + 1)):
                ins = v.bn_stats(self.io["stats"][:, t, :], self.X[:, t, :])
            ins.then_inc(self.s_bn, 1)
            dve.wait_ge(self.s_bn, q + 1)


def float16_scale(nc, dve, sem, done, scale, inverse, bound):
    v = nc.vector
    q = inverse
    v.tensor_scalar(q.bitcast(I32), bound.bitcast(I32), 0x7F800000, None, ALU.bitwise_and).then_inc(sem, 1)
    dve.wait_ge(sem, done + 1)
    v.tensor_scalar(q, q, 2.0 ** -60, 2.0 ** 60, ALU.max, ALU.min).then_inc(sem, 1)
    dve.wait_ge(sem, done + 2)
    v.reciprocal(scale, q).then_inc(sem, 1)
    dve.wait_ge(sem, done + 3)
    v.tensor_scalar(scale, scale, 2.0 ** 14, None, ALU.mult).then_inc(sem, 1)
    v.tensor_scalar(q, q, 2.0 ** -14, None, ALU.mult).then_inc(sem, 1)
    dve.wait_ge(sem, done + 5)
    return done + 5


def mixture(nc, io, c, X, tokens, outer):
    E, F = io["L0_ffn_gate_w"].shape[1], io["L0_ffn_w1"].shape[2]
    C = -(-5 * N // (4 * E))
    KF = F // P
    MT = -(-C // P)
    rows = [min(P, C - m * P) for m in range(MT)]
    buf, ybuf = io["buf_dram"], io["ybuf_dram"]
    rows_all, slot_out, weight = tokens.rows, tokens.slot_out, tokens.weight
    with Space(nc, outer) as s:
        slot_in = s.sb("slot_in", [B, NB], I32)
        s_tok = s.sem("D_tok")

        with Space(nc, s) as s1:
            norm = Norm(s1, "n2", io["stats"])
            gw = s1.sb("gw", [P, KD, E])
            gb = s1.sb("gb", [B, E])
            tri = s1.sb("tri", [B, B])
            rank_i = s1.sb("rank_i", [B, E], I32)
            rank = s1.sb("rank", [B, E])
            lg, ex, pr, eq, oh, tot, tin = (s1.sb(n, [B, NB, E]) for n in ("lg", "ex", "pr", "eq", "oh", "tot", "tin"))
            mx, sm, pm, best, pos, kept, place, zero = (s1.sb(n, [B, NB]) for n in ("mx", "sm", "pm", "best", "pos", "kept", "place", "zero"))
            plog = s1.ps("plog", [B, NB, E])
            pcum = s1.ps("pcum", [B, NB, E])
            ptot = s1.ps("ptot", [B, NB, E])
            s_gw, s_gb, s_tri, s_copy, s_v, s_sh, s_ex, s_oh, s_cum = (
                s1.sem("D_" + n) for n in ("gw", "gb", "tri", "copy", "v", "sh", "ex", "oh", "cum"))
            with nc.Block() as block:
                @block.sync
                def _(sp):
                    sp.dma_start(gw[:], io["L0_ffn_gate_w"].rearrange("(k p) e -> p k e", p=P)).then_inc(s_gw, 16)
                    sp.dma_start(gb[:], bc(io["L0_ffn_gate_b"], B, 0)).then_inc(s_gb, 16)

                @block.gpsimd
                def _(pool):
                    g = nc.gpsimd
                    g.iota(rank_i[:], [[-1, E]], base=E, channel_multiplier=0).then_inc(s_tri, 1)
                    g.memset(tri[:], 1.0).then_inc(s_tri, 1)
                    pool.wait_ge(s_tri, 2)
                    g.affine_select(out=tri[:], in_=tri[:], compare_op=ALU.is_ge, fill=0.0, base=0,
                                    pattern=[[1, B]], channel_multiplier=-1).then_inc(s_tri, 1)

                    def body(t, u, first):
                        pool.wait_ge(norm.s_xn, t + 1)
                        g.tensor_copy(rows_all[:, t, :], norm.xn[:, u, :]).then_inc(s_copy, 1)
                    blocks(pool, body)

                @block.scalar
                def _(act):
                    norm.std(nc, act)
                    act.wait_ge(norm.s_rstd, 1)

                    def body(t, u, first):
                        if not first:
                            act.wait_ge(s_copy, t - UN + 1)
                        norm.rows(nc, act, X, t, u, first)
                    blocks(act, body)
                    act.wait_ge(s_sh, 1)
                    nc.scalar.activation(ex[:], lg[:], ACT.Exp).then_inc(s_ex, 1)

                @block.tensor
                def _(pe):
                    pe.wait_ge(s_gw, 16)

                    def turn(t, u, first):
                        norm.turn(nc, pe, c["ident"], t, u, first)

                    def body(t, u, first):
                        pe.wait_ge(norm.s_xt, t + 1)
                        for k in range(KD):
                            mm = nc.tensor.matmul(plog[:, t, :], norm.xt[:, u, k, :], gw[:, k, :], start=(k == 0), stop=(k == KD - 1))
                        mm.then_inc(norm.s_used, 1)
                    staggered(pe, turn, body)
                    pe.wait_ge(s_oh, 1)
                    ohf = oh[:].rearrange("p t e -> p (t e)")
                    nc.tensor.matmul(pcum[:].rearrange("p t e -> p (t e)"), tri[:], ohf, start=True, stop=True)
                    nc.tensor.matmul(ptot[:].rearrange("p t e -> p (t e)"), c["ones"][0:B, 0:B], ohf, start=True, stop=True).then_inc(s_cum, 1)

                @block.vector
                def _(dve):
                    v = nc.vector
                    n = [0]

                    def step(ins):
                        n[0] += 1
                        ins.then_inc(s_v, 1)
                        dve.wait_ge(s_v, n[0])

                    norm.stats(nc, dve)
                    v.memset(zero[:], 0.0)
                    blocks(dve, lambda t, u, first: norm.out(nc, dve, t, u, first))
                    dve.wait_ge(s_gb, 16)
                    dve.wait_ge(s_tri, 3)
                    dve.wait_ge(norm.s_used, NB)
                    v.tensor_copy(rank[:], rank_i[:])
                    step(v.tensor_tensor(lg[:], plog[:], bc(gb[:], NB, 1), ALU.add))
                    step(v.tensor_reduce(mx[:], lg[:], AX.X, ALU.max))
                    v.tensor_tensor(lg[:], lg[:], bc(mx[:], E, 2), ALU.subtract).then_inc(s_sh, 1)
                    dve.wait_ge(s_ex, 1)
                    step(v.tensor_reduce(sm[:], ex[:], AX.X, ALU.add))
                    step(v.reciprocal(mx[:], sm[:]))
                    step(v.tensor_tensor(pr[:], ex[:], bc(mx[:], E, 2), ALU.mult))
                    step(v.tensor_reduce(pm[:], pr[:], AX.X, ALU.max))
                    step(v.tensor_tensor(eq[:], pr[:], bc(pm[:], E, 2), ALU.is_equal))
                    step(v.tensor_tensor(eq[:], eq[:], bc(rank[:], NB, 1), ALU.mult))
                    step(v.tensor_reduce(best[:], eq[:], AX.X, ALU.max))
                    v.tensor_tensor(oh[:], eq[:], bc(best[:], E, 2), ALU.is_equal).then_inc(s_oh, 1)
                    dve.wait_ge(s_cum, 1)
                    step(v.tensor_copy(tot[:], ptot[:]))
                    for e in range(E):
                        ins = v.tensor_tensor_scan(tin[:, :, e], tot[:, :, e], zero[:], 0.0, ALU.add, ALU.add)
                    step(ins)
                    step(v.tensor_tensor(tin[:], tin[:], tot[:], ALU.subtract))
                    step(v.tensor_tensor(tin[:], tin[:], pcum[:], ALU.add))
                    step(v.tensor_tensor(tin[:], tin[:], oh[:], ALU.mult))
                    step(v.tensor_reduce(pos[:], tin[:], AX.X, ALU.add))
                    step(v.tensor_scalar(kept[:], pos[:], float(C), None, ALU.is_le))
                    v.tensor_tensor(weight[:], pm[:], kept[:], ALU.mult)
                    step(v.tensor_scalar(place[:], pos[:], float(C), -1.0, ALU.min, ALU.add))
                    step(v.tensor_scalar(best[:], best[:], -float(C), float(E * C), ALU.mult, ALU.add))
                    step(v.tensor_tensor(place[:], place[:], best[:], ALU.add))
                    v.tensor_copy(slot_out[:], place[:])
                    step(v.tensor_scalar(kept[:], kept[:], -8192.0, 8192.0, ALU.mult, ALU.add))
                    step(v.tensor_tensor(place[:], place[:], kept[:], ALU.add))
                    v.tensor_copy(slot_in[:], place[:]).then_inc(s_tok, 1)

        with Space(nc, s) as s2:
            w1, w2 = s2.sb("w1", [P, 2, KD, F]), s2.sb("w2", [P, 2, KF, D])
            w1p, w2p = s2.sb("w1p", [P, 2, 2, KD, F], F16), s2.sb("w2p", [P, 2, 2, KF, D], F16)
            b1_rows = s2.sb("b1_rows", [E * KF, P])
            b1 = s2.sb("b1", [P, E * KF])
            b2 = s2.sb("b2", [P, E, D])
            xe = s2.sb("xe", [P, 2, MT, D])
            xt = s2.sb("xte", [P, 2, 2, KD, C], F16)
            hm = s2.sb("hm", [P, KF, C])
            hmp = s2.sb("hmp", [P, 2, KF, C], F16)
            yo = s2.sb("yo", [P, MT, D])
            most = s2.sb("most", [P, 2, 2])
            b_most = s2.sb("b_most", [P, 1])
            b_bound = s2.sb("b_bound", [P, 1])
            bound, scale, inv = (s2.sb(n, [P, 2, 3]) for n in ("bounds", "scales", "inverses"))
            inv_y = s2.sb("inv_y", [P, 2])
            pt = [s2.ps(f"pte{k}", [P, C]) for k in range(KD)]
            ph = [s2.ps(f"phe{i}", [P, C]) for i in range(3)]
            py = [s2.ps(f"pye{i}", [P, D]) for i in range(2)]
            ptot = s2.ps("ptot_e", [P, 3])
            s_scat, s_b1, s_b2, s_b1t, s_b1c, s_bm, s_bt = (s2.sem("E_" + n) for n in ("scat", "b1", "b2", "b1t", "b1c", "bm", "bt"))
            s_w1, s_w2, s_xe = ([s2.sem(f"E_{n}{k}") for k in range(2)] for n in ("w1", "w2", "xe"))
            s_y = [s2.sem(f"E_y{m}") for m in range(MT)]
            s_most, s_tot, s_sc, s_scaled, s_tr, s_xhi, s_xlo, s_whi, s_wlo, s_mm1, s_hm, s_hhi, s_hlo, s_mm2, s_yo = (
                s2.sem("E_" + n) for n in ("most", "tot", "sc", "scaled", "tr", "xhi", "xlo", "whi", "wlo", "mm1", "hm", "hhi",
                                           "hlo", "mm2", "yo"))
            s_kept = s2.sem("E_kept")
            C0 = KF

            def experts(engine, step):
                with engine.Fori(0, E // 2 - 1) as i:
                    step(2 * i, 0, i, True, True)
                    step(2 * i + 1, 1, i, True, True)
                step(E - 2, 0, E // 2 - 1, True, False)
                step(E - 1, 1, E // 2 - 1, False, False)

            with nc.Block() as block:
                @block.sync
                def _(sp):
                    sp.dma_start(b1_rows[:], io["L0_ffn_b1"].rearrange("e (f p) -> (e f) p", p=P)).then_inc(s_b1, 16)
                    sp.dma_start(b2[:], bc(io["L0_ffn_b2"], P, 0)).then_inc(s_b2, 16)

                    def weights(e, k):
                        sp.dma_start(w1[:, k], io["L0_ffn_w1"][e].rearrange("(k p) f -> p k f", p=P)).then_inc(s_w1[k], 16)
                        sp.dma_start(w2[:, k], io["L0_ffn_w2"][e].rearrange("(f p) d -> p f d", p=P)).then_inc(s_w2[k], 16)

                    def token_rows(e, k):
                        sp.dma_start(xe[:, k], buf[bass.ds(e * C, MT * P), :].rearrange("(m p) d -> p m d", p=P)).then_inc(s_xe[k], 16)
                    weights(0, 0)
                    weights(1, 1)
                    sp.wait_ge(s_scat, 16 * NB)
                    token_rows(0, 0)
                    token_rows(1, 1)
                    with sp.Fori(1, E // 2) as i:
                        for k in range(2):
                            e = 2 * i + k
                            sp.wait_ge(s_wlo, 2 * (e - 1))
                            weights(e, k)
                            sp.wait_ge(s_tr, e - 1)
                            token_rows(e, k)

                @block.gpsimd
                def _(pool):
                    for t in range(NB):
                        nc.gpsimd.indirect_dma_start(buf, bass.IndirectOffsetOnAxis(ap=slot_in[:, t:t + 1], axis=0),
                                                     rows_all[:, t, :], None, bounds_check=E * C - 1,
                                                     oob_is_err=False).then_inc(s_scat, 16)

                    def step(e, k, r, one, two):
                        for m in range(MT):
                            pool.wait_ge(s_yo, C0 + MT * e + m + 1)
                            pool.dma_start(ybuf[bass.ds(e * C + m * P, rows[m]), :], yo[0:rows[m], m, :]).then_inc(s_y[m], 16)
                        for m in range(MT):
                            pool.wait_ge(s_y[m], 16 * (e + 1))
                        pool.sem_inc(s_kept, 1)
                    experts(pool, step)

                @block.tensor
                def _(pe):
                    t_ = nc.tensor
                    pe.sem_inc(s_mm1, C0)
                    pe.sem_inc(s_mm2, C0)
                    pe.wait_ge(s_b1, 16)
                    t_.transpose(ph[0][:, 0:E * KF], b1_rows[:], c["ident"][0:E * KF, 0:E * KF]).then_inc(s_b1t, 1)
                    pe.wait_ge(s_bm, 1)
                    t_.matmul(ptot[:, 0:1], c["ones"][:], b_most[:], start=True, stop=True).then_inc(s_bt, 1)
                    pe.wait_ge(s_bt, 2)

                    def prepare(e, k, r):
                        pe.wait_ge(s_most, 2 * (e + 1))
                        pe.wait_ge(s_scaled, e + 1)
                        t_.matmul(ptot[:, 0:2], c["ones"][:], most[:, k, :], start=True, stop=True).then_inc(s_tot, 1)
                        pe.wait_ge(s_xe[k], 16 * (r + 1))
                        pe.wait_ge(s_xlo, C0 + e)
                        for m in range(MT):
                            for f in range(KD):
                                tr = t_.transpose(pt[f][:, m * P:m * P + rows[m]], xe[0:rows[m], k, m, f * P:(f + 1) * P],
                                                  c["ident"][0:rows[m], 0:rows[m]])
                        tr.then_inc(s_tr, 1)
                    PARTS = ((0, 1), (1, 0), (0, 0))

                    def step(e, k, r, one, two):
                        pe.wait_ge(s_xlo, C0 + e + 1)
                        pe.wait_ge(s_wlo, 2 * e + 1)
                        for f in range(KF):
                            pe.wait_ge(s_hm, C0 + KF * e + f - 2)
                            for n, (a, b) in enumerate(PARTS):
                                for j in range(KD):
                                    mm = t_.matmul(ph[f % 3][:], w1p[:, k, a, j, f * P:(f + 1) * P], xt[:, k, b, j, :],
                                                   start=(n == 0 and j == 0), stop=(n == 2 and j == KD - 1))
                            mm.then_inc(s_mm1, 1)
                        if one:
                            prepare(e + 1, 1 - k, r + k)
                        pe.wait_ge(s_wlo, 2 * e + 2)
                        pe.wait_ge(s_hlo, C0 + KF * (e + 1))
                        for m in range(MT):
                            pe.wait_ge(s_yo, C0 + MT * e + m - 1)
                            for n, (a, b) in enumerate(PARTS):
                                for f in range(KF):
                                    mm = t_.matmul(py[m % 2][0:rows[m], :], hmp[:, a, f, m * P:m * P + rows[m]], w2p[:, k, b, f, :],
                                                   start=(n == 0 and f == 0), stop=(n == 2 and f == KF - 1))
                            mm.then_inc(s_mm2, 1)
                    prepare(0, 0, 0)
                    experts(pe, step)

                @block.scalar
                def _(act):
                    a_ = nc.scalar
                    act.sem_inc(s_hm, C0)
                    act.sem_inc(s_hhi, C0)
                    act.wait_ge(s_b1c, 1)

                    def rows_hi(e, k):
                        act.wait_ge(s_tr, e + 1)
                        act.wait_ge(s_mm1, C0 + KF * (e - 1))
                        for f in range(KD):
                            ins = a_.activation(xt[:, k, 0, f, :], pt[f][:], ACT.Copy)
                        ins.then_inc(s_xhi, 1)

                    def weights_hi(e, k):
                        act.wait_ge(s_scaled, e + 2)
                        act.wait_ge(s_mm1, C0 + KF * (e - 1))
                        a_.activation(w1p[:, k, 0], w1[:, k], ACT.Copy, scale=scale[:, k, 0:1]).then_inc(s_whi, 1)
                        act.wait_ge(s_mm2, C0 + MT * (e - 1))
                        a_.activation(w2p[:, k, 0], w2[:, k], ACT.Copy, scale=scale[:, k, 1:2]).then_inc(s_whi, 1)

                    def step(e, k, r, one, two):
                        act.wait_ge(s_mm2, C0 + MT * e)
                        for f in range(KF):
                            act.wait_ge(s_mm1, C0 + KF * e + f + 1)
                            act.wait_ge(s_hlo, C0 + KF * (e - 1) + f + 1)
                            a_.activation(hm[:, f, :], ph[f % 3][:], ACT.Relu, scale=inv[:, k, 0:1],
                                          bias=b1[:, bass.ds(e * KF + f, 1)]).then_inc(s_hm, 1)
                            act.wait_ge(s_hm, C0 + KF * e + f + 1)
                            a_.activation(hmp[:, 0, f, :], hm[:, f, :], ACT.Copy, scale=scale[:, k, 2:3]).then_inc(s_hhi, 1)
                        if one:
                            rows_hi(e + 1, 1 - k)
                            weights_hi(e + 1, 1 - k)
                    rows_hi(0, 0)
                    weights_hi(0, 0)
                    experts(act, step)

                @block.vector
                def _(dve):
                    v = nc.vector
                    for s_, n in ((s_scaled, 1), (s_kept, 1), (s_xlo, C0), (s_hlo, C0), (s_yo, C0)):
                        dve.sem_inc(s_, n)
                    dve.wait_ge(s_b1t, 1)
                    v.tensor_copy(b1[:], ph[0][:, 0:E * KF]).then_inc(s_b1c, 1)
                    dve.wait_ge(s_b1c, 1)
                    v.tensor_reduce(b_most[:], b1[:], AX.X, ALU.max, apply_absolute_value=True).then_inc(s_bm, 1)
                    dve.wait_ge(s_bt, 1)
                    v.tensor_copy(b_bound[:], ptot[:, 0:1]).then_inc(s_bt, 1)
                    dve.wait_ge(s_b2, 16)
                    STEPS = 8

                    def largest(e, k, r, n):
                        w, s_w = ((w1, s_w1), (w2, s_w2))[n]
                        dve.wait_ge(s_w[k], 16 * (r + 1))
                        v.tensor_reduce(most[:, k, n:n + 1], w[:, k], AX.XY, ALU.max, apply_absolute_value=True).then_inc(s_most, 1)

                    def scales(e, k):
                        dve.wait_ge(s_tot, e + 1)
                        done = STEPS * e
                        v.tensor_copy(bound[:, k, 0:2], ptot[:, 0:2]).then_inc(s_sc, 1)
                        dve.wait_ge(s_sc, done + 1)
                        v.scalar_tensor_tensor(bound[:, k, 2:3], bound[:, k, 0:1], float(D), b_bound[:], ALU.mult, ALU.add).then_inc(s_sc, 1)
                        dve.wait_ge(s_sc, done + 2)
                        done = float16_scale(nc, dve, s_sc, done + 2, scale[:, k, :], inv[:, k, :], bound[:, k, :])
                        v.tensor_tensor(inv_y[:, k:k + 1], inv[:, k, 1:2], inv[:, k, 2:3], ALU.mult).then_inc(s_sc, 1)
                        dve.wait_ge(s_sc, done + 1)
                        dve.sem_inc(s_scaled, 1)

                    def rows_lo(e, k):
                        dve.wait_ge(s_xhi, e + 1)
                        for f in range(KD):
                            ins = v.tensor_tensor(xt[:, k, 1, f, :], pt[f][:], xt[:, k, 0, f, :], ALU.subtract)
                        ins.then_inc(s_xlo, 1)

                    def weights_lo(e, k, n):
                        w, wp = ((w1, w1p), (w2, w2p))[n]
                        dve.wait_ge(s_whi, 2 * e + n + 1)
                        v.scalar_tensor_tensor(wp[:, k, 1], w[:, k], scale[:, k, n:n + 1], wp[:, k, 0],
                                               ALU.mult, ALU.subtract).then_inc(s_wlo, 1)

                    def step(e, k, r, one, two):
                        for f in range(KF):
                            dve.wait_ge(s_hhi, C0 + KF * e + f + 1)
                            v.scalar_tensor_tensor(hmp[:, 1, f, :], hm[:, f, :], scale[:, k, 2:3], hmp[:, 0, f, :],
                                                   ALU.mult, ALU.subtract).then_inc(s_hlo, 1)
                        if one:
                            scales(e + 1, 1 - k)
                            rows_lo(e + 1, 1 - k)
                        dve.wait_ge(s_kept, e + 1)
                        for m in range(MT):
                            if one and m < 2:
                                weights_lo(e + 1, 1 - k, m)
                            if two and m >= 2:
                                largest(e + 2, k, r + 1, m - 2)
                            dve.wait_ge(s_mm2, C0 + MT * e + m + 1)
                            v.scalar_tensor_tensor(yo[0:rows[m], m, :], py[m % 2][0:rows[m], :], inv_y[0:rows[m], k:k + 1],
                                                   b2[0:rows[m], e, :], ALU.mult, ALU.add).then_inc(s_yo, 1)
                    assert MT == 4
                    for e in range(2):
                        for n in range(2):
                            largest(e, e, 0, n)
                    scales(0, 0)
                    rows_lo(0, 0)
                    weights_lo(0, 0, 0)
                    weights_lo(0, 0, 1)
                    experts(dve, step)


class Chunk:

    def __init__(self, l, c, i=None):
        at = c if i is None else 2 * i + c
        self.c, self.nb = at, NB % CB if i is None and c == NC - 1 else CB
        self.g, self.g2 = NC * l + at, (NC * l + c) // 2 + (0 if i is None else i)
        self.k = (NC * l + c) % 2
        self.pairs = -(-self.nb // 2)
        self.before = PAIRS * l + 2 * at

    def nodes(self):
        return bass.ds(self.c * CN, self.nb * B)


PAIRS = -(-NB // 2)


def layer(engine, l, step):
    step(Chunk(l, 0), None)
    with engine.Fori(0, (NC - 3) // 2) as i:
        step(Chunk(l, 1, i), Chunk(l, 0, i))
        step(Chunk(l, 2, i), Chunk(l, 1, i))
    step(Chunk(l, NC - 2), Chunk(l, NC - 3))
    step(Chunk(l, NC - 1), Chunk(l, NC - 2))
    step(None, Chunk(l, NC - 1))


def mean_network(nc, io, c, X, tokens, outer):
    LAYERS = io["L1_gnn_W_agg"].shape[0]
    C0 = 4
    with Space(nc, outer) as s:
        h_t = s.sb("h_t", [P, 2, KD, N], F16)
        parts = [s.sb(f"parts{i}", [B, 2, NB, D], F16) for i in range(2)]
        dinv = s.sb("dinv_all", [P, N])
        w_out = s.sb("w_out", [P, KD, D])
        bias = s.sb("bias", [P, KD * (LAYERS + 1)])
        b_out = s.sb("b_out", [B, D])
        b_sum = s.sb("b_sum", [P, KD * (LAYERS + 1)])
        bound = s.sb("bound", [P, LAYERS])
        scale = s.sb("scale", [P, LAYERS, 2])
        s_wl, s_dl, s_ol = (s.sem("H_" + n) for n in ("wl", "dl", "ol"))

        with Space(nc, s) as s1:
            norm = Norm(s1, "n3", io["stats"])
            w_in = s1.sb("w_in", [P, KD, D])
            b_in = s1.sb("b_in", [B, D])
            b_rows = s1.sb("b_rows", [KD * (LAYERS + 1), P])
            hn = s1.sb("hn", [B, UN, D])
            tokens.temporaries(s1)
            hf = s1.sb("hf", [P, UN, KD, B])
            bias_s = s1.sb("bias_s", [P, KD])
            s_ft = s1.sem("H_ft")
            GROUPS = NB // UN
            group = [slice(UN * g, UN * (g + 1)) for g in range(GROUPS)]
            pn = [s1.ps(f"pn{i}", [B, D]) for i in range(2)]
            pf = [s1.ps(f"pf{i}", [P, KD, B]) for i in range(2)]
            w_sq = s1.sb("w_sq", [P, KD, D])
            b_abs = s1.sb("b_abs", [P, KD * (LAYERS + 1)])
            col, root = s1.sb("col", [P, 1]), s1.sb("root", [P, 1])
            pb_all = s1.ps("pb_all", [P, 2 * KD * (LAYERS + 1) + D])
            pb, pb_sum, p_sq = (pb_all[:, a:b] for a, b in ((0, KD * (LAYERS + 1)), (KD * (LAYERS + 1), 2 * KD * (LAYERS + 1)),
                                                            (2 * KD * (LAYERS + 1), 2 * KD * (LAYERS + 1) + D)))
            s_abs, s_sq, s_col, s_root, s_sc = (s1.sem("H_" + n) for n in ("abs", "sq", "col", "root", "sc"))
            s_in, s_bin, s_br, s_bt, s_bc, s_pn, s_hn, s_hi, s_lo, s_ht = (
                s1.sem("H_" + n) for n in ("in", "bin", "br", "bt", "bc", "pn", "hn", "hi", "lo", "ht"))
            with nc.Block() as block:
                @block.sync
                def _(sp):
                    sp.dma_start(w_in[:], io["L1_gnn_W_in"].rearrange("(k p) f -> p k f", p=P)).then_inc(s_in, 16)
                    sp.dma_start(b_rows[0:KD], io["L1_gnn_b_in"].rearrange("(m p) -> m p", p=P)).then_inc(s_br, 16)
                    sp.dma_start(b_rows[KD:], io["L1_gnn_b_hid"].rearrange("l (m p) -> (l m) p", p=P)).then_inc(s_br, 16)
                    sp.dma_start(b_in[:], bc(io["L1_gnn_b_in"], B, 0)).then_inc(s_bin, 16)
                    sp.dma_start(w_out[:], io["L1_gnn_W_out"].rearrange("(k p) f -> p k f", p=P)).then_inc(s_wl, 16)
                    sp.dma_start(b_out[:], bc(io["L1_gnn_b_out"], B, 0)).then_inc(s_ol, 16)
                    sp.dma_start(dinv[:], bc(io["dinv_dram"], P, 0)).then_inc(s_dl, 16)
                    sp.wait_ge(s_wl, 16)
                    sp.wait_ge(s_ol, 16)
                    sp.wait_ge(s_dl, 16)

                @block.gpsimd
                def _(pool):
                    tokens.gather(pool)

                    def second_part(t, u, first):
                        pool.wait_ge(s_ft, 2 * t + 2)
                        nc.gpsimd.tensor_tensor(h_t[:, 1, :, bass.ds(t * B, B)], hf[:, u, :, :], h_t[:, 0, :, bass.ds(t * B, B)],
                                                ALU.subtract).then_inc(s_ht, 1)
                    blocks(pool, second_part)

                @block.vector
                def _(dve):
                    v = nc.vector
                    dve.wait_ge(s_bt, 1)
                    v.tensor_copy(bias[:], pb).then_inc(s_bc, 1)
                    dve.wait_ge(s_sq, 1)
                    v.tensor_reduce(col[:], p_sq, AX.X, ALU.max).then_inc(s_col, 1)
                    v.tensor_copy(b_sum[:], pb_sum).then_inc(s_col, 1)
                    dve.wait_ge(s_root, 1)
                    dve.wait_ge(s_col, 2)
                    v.scalar_tensor_tensor(bound[:, 0:1], root[:], b_sum[:, 0:1], b_sum[:, 1:2], ALU.add, ALU.add).then_inc(s_sc, 1)
                    dve.wait_ge(s_sc, 1)
                    float16_scale(nc, dve, s_sc, 1, scale[:, 0, 0:1], scale[:, 0, 1:2], bound[:, 0:1])
                    v.tensor_scalar(bias_s[:], bias[:, 0:KD], scale[:, 0, 0:1], None, ALU.mult).then_inc(s_sc, 1)
                    dve.wait_ge(s_bin, 16)

                    def out(t, u, first):
                        norm.out(nc, dve, t, u, first)

                    def biased(t, u, first):
                        dve.wait_ge(s_pn, t + 1)
                        if not first:
                            dve.wait_ge(s_lo, t - UN + 1)
                            dve.wait_ge(s_hi, t - UN + 1)
                        v.tensor_tensor(hn[:, u, :], pn[u % 2][:], b_in[:], ALU.add).then_inc(s_hn, 1)

                    def second_part(t, u, first):
                        dve.wait_ge(s_hi, t + 1)
                        v.scalar_tensor_tensor(parts[0][:, 1, t, :], hn[:, u, :], scale[0:B, 0, 0:1], parts[0][:, 0, t, :],
                                               ALU.mult, ALU.subtract).then_inc(s_lo, 1)
                    for g in range(2):
                        for piece in range(UN):
                            tokens.add(dve, g, piece)
                        norm.variance(nc, dve, g, group[g])
                        if g == 0:
                            norm.inverse(nc, dve, 0, group[0])
                    for t in range(NB + 2):
                        g, u = divmod(t, UN)
                        for lag, part in enumerate((out, biased, second_part)):
                            if 0 <= t - lag < NB:
                                part(t - lag, (t - lag) % UN, t - lag < UN)
                        if g + 2 < GROUPS:
                            tokens.add(dve, g + 2, u)
                            if u == UN - 1:
                                norm.variance(nc, dve, g + 2, group[g + 2])
                        if u == 1 and g + 1 < GROUPS:
                            norm.inverse(nc, dve, g + 1, group[g + 1])

                @block.scalar
                def _(act):
                    act.wait_ge(s_in, 16)
                    nc.scalar.activation(w_sq[:], w_in[:], ACT.Square).then_inc(s_abs, 1)
                    act.wait_ge(s_bc, 1)
                    nc.scalar.activation(b_abs[:], bias[:], ACT.Abs).then_inc(s_abs, 1)
                    act.wait_ge(s_col, 1)
                    nc.scalar.activation(root[:], col[:], ACT.Sqrt, scale=float(D)).then_inc(s_root, 1)

                    def rows(t, u, first):
                        norm.rows(nc, act, X, t, u, first)

                    def after(t, u, first):
                        act.wait_ge(s_sc, 7)
                        act.wait_ge(s_hn, t + 1)
                        nc.scalar.activation(parts[0][:, 0, t, :], hn[:, u, :], ACT.Copy, scale=scale[0:B, 0, 0:1]).then_inc(s_hi, 1)
                        act.wait_ge(norm.s_used, t + 1)
                        if not first:
                            act.wait_ge(s_ht, t - UN + 1)
                        for m in range(KD):
                            ins = nc.scalar.activation(hf[:, u, m, :], pf[u % 2][:, m, :], ACT.Identity,
                                                       scale=scale[:, 0, 0:1], bias=bias_s[:, m:m + 1])
                        ins.then_inc(s_ft, 1)
                        act.wait_ge(s_ft, 2 * t + 1)
                        nc.scalar.activation(h_t[:, 0, :, bass.ds(t * B, B)], hf[:, u, :, :], ACT.Copy).then_inc(s_ft, 1)
                    for t in range(UN):
                        tokens.weigh(act, t)
                    norm.std(nc, act, 0, group[0])
                    for t in range(UN, 3 * UN):
                        tokens.weigh(act, t)
                    for t in range(NB + 2):
                        g, u = divmod(t, UN)
                        if t < NB:
                            act.wait_ge(norm.s_rstd, g + 1)
                            rows(t, u, t < UN)
                        if t >= 2:
                            after(t - 2, (t - 2) % UN, t - 2 < UN)
                        if t + 3 * UN < NB:
                            tokens.weigh(act, t + 3 * UN)
                        if u == 0 and g + 1 < GROUPS:
                            norm.std(nc, act, g + 1, group[g + 1])

                @block.tensor
                def _(pe):
                    t_ = nc.tensor
                    pe.wait_ge(s_br, 32)
                    t_.transpose(pb, b_rows[:], c["ident"][0:KD * (LAYERS + 1), 0:KD * (LAYERS + 1)]).then_inc(s_bt, 1)
                    pe.wait_ge(s_in, 16)
                    pe.wait_ge(s_abs, 2)
                    t_.matmul(pb_sum, c["ones"][:], b_abs[:], start=True, stop=True)
                    for k in range(KD):
                        mm = t_.matmul(p_sq, c["ones"][:], w_sq[:, k, :], start=(k == 0), stop=(k == KD - 1))
                    mm.then_inc(s_sq, 1)

                    def turn(t, u, first):
                        norm.turn(nc, pe, c["ident"], t, u, first)

                    def body(t, u, first):
                        pe.wait_ge(norm.s_xt, t + 1)
                        if not first or u >= 2:
                            pe.wait_ge(s_hn, t - gap(u, 2) + 1)
                            pe.wait_ge(s_ft, 2 * (t - gap(u, 2)) + 1)
                        for k in range(KD):
                            mm = t_.matmul(pn[u % 2][:], norm.xt[:, u, k, :], w_in[:, k, :], start=(k == 0), stop=(k == KD - 1))
                        mm.then_inc(s_pn, 1)
                        for m in range(KD):
                            for k in range(KD):
                                mm = t_.matmul(pf[u % 2][:, m, :], w_in[:, k, m * P:(m + 1) * P], norm.xt[:, u, k, :], start=(k == 0), stop=(k == KD - 1))
                        mm.then_inc(norm.s_used, 1)
                    staggered(pe, turn, body)

        with Space(nc, s) as s2:
            a_both = s2.sb("a_chunk2", [P, 2, NB, CN], F16)
            a_chunk = a_both[0:B]
            w_agg, w_self = (a_both[:, 1].rearrange("p b n -> p (b n)").bitcast(F32)[:, i * LAYERS * KD * D:(i + 1) * LAYERS * KD * D]
                             .rearrange("p (l k d) -> p l k d", l=LAYERS, k=KD) for i in range(2))
            s_w32 = s2.sem("I_w32")
            agg, hs = (tokens.all[:, i * 2 * KD * CN:(i + 1) * 2 * KD * CN].rearrange("p (s k n) -> p s k n", s=2, k=KD) for i in range(2))
            pa = [[s2.ps(f"pa{k}{m}", [P, CN]) for m in range(KD)] for k in range(2)]
            pw = [s2.ps(f"pw{m}", [P, CN]) for m in range(KD)]
            pt = [s2.ps(f"pt2{i}", [B, 2, D]) for i in range(2)]
            s_chunk = [s2.sem(f"I_chunk{i}") for i in range(2)]
            s_pa, s_agg, s_pw, s_hs, s_ht, s_pt, s_hi, s_lo, s_xb = (
                s2.sem("I_" + n) for n in ("pa", "agg", "pw", "hs", "ht", "pt", "hi", "lo", "xb"))
            at_v = io["AT_dram"].rearrange("(b j) i -> j b i", j=B)
            s_abs, s_norm, s_sc, s_wsc, s_whi, s_wlo, s_ahi, s_alo, s_thi = (
                s2.sem("I_" + n) for n in ("abs", "norm", "sc", "wsc", "whi", "wlo", "ahi", "alo", "thi"))
            aggp = tokens.all[:, 4 * KD * CN:6 * KD * CN].bitcast(F16).rearrange("p (s a k n) -> p s a k n", s=2, a=2, k=KD)
            wp = s2.sb("wp", [P, LAYERS, 2, 2, KD, D], F16)
            w_bound, w_scale, w_inv, inv = (s2.sb(n, [P, LAYERS]) for n in ("w_bound", "w_scale", "w_inv", "inv_all"))
            spare = tokens.all[:, 4 * KD * CN:4 * KD * CN + 2 * KD * D].rearrange("p (n k d) -> p n k d", n=2, k=KD)
            w_abs = [(agg[:, 0, :, 0:D], hs[:, 0, :, 0:D]), (agg[:, 1, :, 0:D], hs[:, 1, :, 0:D]), (spare[:, 0], spare[:, 1])]
            norms = [pw[0][:, 0:D], pw[1][:, 0:D], pa[1][0][:, 0:D]]
            assert LAYERS == 3
            PARTS = ((0, 1), (1, 0), (0, 0))

            with nc.Block() as block:
                @block.sync
                def _(sp):
                    for w, name in ((w_agg, "L1_gnn_W_agg"), (w_self, "L1_gnn_W_self")):
                        for l in range(LAYERS):
                            sp.dma_start(w[:, l], io[name][l].rearrange("(k p) f -> p k f", p=P)).then_inc(s_w32, 16)

                    def load(ch):
                        split_dma(sp, a_chunk[:, ch.k, :, 0:ch.nb * B], at_v[:, :, ch.nodes()], s_chunk[ch.k])
                    for l in range(LAYERS):
                        def step(ch, _):
                            if ch is None:
                                return
                            sp.wait_ge(s_pa, C0 + 2 * (ch.g - 1))
                            if ch.k == 1:
                                sp.wait_ge(s_wlo, LAYERS)
                            load(ch)
                        layer(sp, l, step)

                @block.gpsimd
                def _(pool):
                    nc.gpsimd.tensor_tensor(X[:], X[:], bc(b_out[:], NB, 1), ALU.add).then_inc(s_xb, 1)

                @block.tensor
                def _(pe):
                    t_ = nc.tensor
                    pe.sem_inc(s_pa, C0)
                    pe.sem_inc(s_pw, C0)
                    pe.sem_inc(s_pt, C0)
                    pe.wait_ge(s_abs, 1)
                    for l in range(LAYERS):
                        for n in range(2):
                            for k in range(KD):
                                mm = t_.matmul(norms[l], c["ones"][:], w_abs[l][n][:, k, :], start=(n == 0 and k == 0), stop=(n == 1 and k == KD - 1))
                    mm.then_inc(s_norm, 1)

                    def gather(l, ch, m):
                        if m == 0:
                            pe.wait_ge(s_chunk[ch.k], 32 * (ch.g2 + 1))
                        pe.wait_ge(s_agg, C0 + 2 * (ch.g - 2) + m + 1)
                        if m == 0:
                            pe.wait_ge(s_wsc, 1)
                        for q in range(2):
                            for j in range(NB):
                                mm = t_.matmul(pa[ch.k][m][:, 0:ch.nb * B], parts[l % 2][:, q, j, m * P:(m + 1) * P],
                                               a_chunk[:, ch.k, j, 0:ch.nb * B], start=(q == 0 and j == 0), stop=(q == 1 and j == NB - 1))
                        mm.then_inc(s_pa, 1)

                    def weights(l, ch):
                        w = ch.nb * B
                        pe.wait_ge(s_alo, C0 + 2 * (ch.g + 1))
                        pe.wait_ge(s_hs, C0 + 2 * ch.g)
                        pe.wait_ge(s_wlo, l + 1)
                        if l:
                            pe.wait_ge(s_ht, C0 + ch.g - NC + 1)
                        for m in range(KD):
                            ms = slice(m * P, (m + 1) * P)
                            for n, (a, b) in enumerate(PARTS):
                                for k in range(KD):
                                    t_.matmul(pw[m][:, 0:w], wp[:, l, 0, a, k, ms], aggp[:, ch.k, b, k, 0:w], start=(n == 0 and k == 0), stop=False)
                                for k in range(KD):
                                    mm = t_.matmul(pw[m][:, 0:w], wp[:, l, 1, a, k, ms], h_t[:, b, k, ch.nodes()], start=False,
                                                   stop=(n == 2 and k == KD - 1))
                            mm.then_inc(s_pw, 1)

                    def turn(l, ch):
                        pe.wait_ge(s_hs, C0 + 2 * (ch.g + 1))
                        pe.wait_ge(s_lo, C0 + ch.before)
                        for b in range(ch.nb):
                            bs = slice(b * B, (b + 1) * B)
                            for m in range(KD):
                                if l < LAYERS - 1:
                                    mm = t_.transpose(pt[b // 2][:, b % 2, m * P:(m + 1) * P], hs[:, ch.k, m, bs], c["ident"][:])
                                else:
                                    mm = t_.matmul(pt[b // 2][:, b % 2, :], hs[:, ch.k, m, bs], w_out[:, m, :], start=(m == 0), stop=(m == KD - 1))
                            if b % 2 or b == ch.nb - 1:
                                mm.then_inc(s_pt, 1)

                    for l in range(LAYERS):
                        def step(ch, pr, l=l):
                            if ch is not None:
                                if pr is None and l:
                                    pe.wait_ge(s_lo, C0 + PAIRS * l)
                                gather(l, ch, 0)
                            if pr is not None:
                                weights(l, pr)
                            if ch is not None:
                                gather(l, ch, 1)
                            if pr is not None:
                                turn(l, pr)
                        layer(pe, l, step)

                @block.scalar
                def _(act):
                    act.sem_inc(s_hs, C0)
                    act.sem_inc(s_hi, C0)
                    act.wait_ge(s_w32, 16 * 2 * LAYERS)
                    for l in range(LAYERS):
                        for w, out in zip((w_agg, w_self), w_abs[l]):
                            ins = nc.scalar.activation(out, w[:, l], ACT.Abs)
                    ins.then_inc(s_abs, 1)
                    act.wait_ge(s_wsc, 1)
                    for l in range(LAYERS):
                        for n, w in enumerate((w_agg, w_self)):
                            ins = nc.scalar.activation(wp[:, l, n, 0], w[:, l], ACT.Copy, scale=w_scale[:, l:l + 1])
                        ins.then_inc(s_whi, 1)

                    def means_hi(ch, m):
                        act.wait_ge(s_agg, C0 + 2 * ch.g + m + 1)
                        act.wait_ge(s_pw, C0 + 2 * (ch.g - 1))
                        nc.scalar.activation(aggp[:, ch.k, 0, m, 0:ch.nb * B], agg[:, ch.k, m, 0:ch.nb * B], ACT.Copy).then_inc(s_ahi, 1)
                    for l in range(LAYERS):
                        def step(new, ch, l=l):
                            if new is not None:
                                means_hi(new, 0)
                            if ch is not None:
                                w = ch.nb * B
                                last = isinstance(ch.c, int) and ch.c == 0
                                act.wait_ge(s_pt, C0 + ch.before - (1 if last else 2))
                                if l < LAYERS - 1:
                                    act.wait_ge(s_ht, C0 + ch.g - 1)
                                else:
                                    act.wait_ge(s_ht, C0 + NC * (LAYERS - 1))
                                for m in range(KD):
                                    act.wait_ge(s_pw, C0 + 2 * ch.g + m + 1)
                                    nc.scalar.activation(hs[:, ch.k, m, 0:w], pw[m][:, 0:w], ACT.Relu, scale=inv[:, l:l + 1],
                                                         bias=bias[:, KD * (l + 1) + m:KD * (l + 1) + m + 1]).then_inc(s_hs, 1)
                                if l < LAYERS - 1:
                                    act.wait_ge(s_hs, C0 + 2 * (ch.g + 1))
                                    nc.scalar.activation(h_t[:, 0, :, ch.nodes()], hs[:, ch.k, :, 0:w], ACT.Copy,
                                                         scale=scale[:, l + 1, 0:1]).then_inc(s_thi, 1)
                            if new is not None:
                                means_hi(new, 1)
                            if ch is not None and l < LAYERS - 1:
                                for i in range(ch.pairs):
                                    n = min(2, ch.nb - 2 * i)
                                    act.wait_ge(s_pt, C0 + ch.before + i + 1)
                                    nc.scalar.activation(parts[(l + 1) % 2][:, 0, bass.ds(ch.c * CB + 2 * i, n), :], pt[i][:, 0:n, :],
                                                         ACT.Copy, scale=scale[0:B, l + 1, 0:1]).then_inc(s_hi, 1)
                        layer(act, l, step)

                @block.vector
                def _(dve):
                    v = nc.vector
                    dve.sem_inc(s_agg, C0)
                    dve.sem_inc(s_lo, C0)
                    dve.sem_inc(s_alo, C0)
                    dve.sem_inc(s_ht, C0)
                    dve.wait_ge(s_norm, 1)
                    for l in range(LAYERS):
                        ins = v.tensor_reduce(w_bound[:, l:l + 1], norms[l], AX.X, ALU.max)
                    ins.then_inc(s_sc, 1)
                    dve.wait_ge(s_sc, 1)
                    n = float16_scale(nc, dve, s_sc, 1, w_scale[:], w_inv[:], w_bound[:])
                    for l in range(LAYERS - 1):
                        at = bound[:, l + 1:l + 2]
                        v.tensor_scalar(at, w_bound[:, l:l + 1], bound[:, l:l + 1], b_sum[:, KD * (l + 1):KD * (l + 1) + 1],
                                        ALU.mult, ALU.add).then_inc(s_sc, 1)
                        dve.wait_ge(s_sc, n + 1)
                        v.tensor_scalar(at, at, b_sum[:, KD * (l + 1) + 1:KD * (l + 2)], None, ALU.add).then_inc(s_sc, 1)
                        dve.wait_ge(s_sc, n + 2)
                        n = float16_scale(nc, dve, s_sc, n + 2, scale[:, l + 1, 0:1], scale[:, l + 1, 1:2], at)
                    v.tensor_tensor(inv[:], w_inv[:], scale[:, :, 1], ALU.mult).then_inc(s_wsc, 1)
                    for l in range(LAYERS):
                        dve.wait_ge(s_whi, l + 1)
                        for k, w in enumerate((w_agg, w_self)):
                            ins = v.scalar_tensor_tensor(wp[:, l, k, 1], w[:, l], w_scale[:, l:l + 1], wp[:, l, k, 0], ALU.mult, ALU.subtract)
                        ins.then_inc(s_wlo, 1)

                    def means(ch, m):
                        w = ch.nb * B
                        dve.wait_ge(s_pa, C0 + 2 * ch.g + m + 1)
                        dve.wait_ge(s_alo, C0 + 2 * (ch.g - 1) + m)
                        v.tensor_tensor(agg[:, ch.k, m, 0:w], pa[ch.k][m][:, 0:w], dinv[:, ch.nodes()], ALU.mult).then_inc(s_agg, 1)
                        dve.wait_ge(s_ahi, 2 * ch.g + m + 1)
                        v.tensor_tensor(aggp[:, ch.k, 1, m, 0:w], agg[:, ch.k, m, 0:w], aggp[:, ch.k, 0, m, 0:w], ALU.subtract).then_inc(s_alo, 1)
                    for l in range(LAYERS):
                        def step(ch, pr, l=l):
                            if ch is not None:
                                means(ch, 0)
                            if pr is not None and l < LAYERS - 1:
                                dve.wait_ge(s_thi, pr.g + 1)
                                v.scalar_tensor_tensor(h_t[:, 1, :, pr.nodes()], hs[:, pr.k, :, 0:pr.nb * B], scale[:, l + 1, 0:1],
                                                       h_t[:, 0, :, pr.nodes()], ALU.mult, ALU.subtract).then_inc(s_ht, 1)
                            if ch is not None:
                                means(ch, 1)
                            if pr is not None:
                                for i in range(pr.pairs):
                                    n = min(2, pr.nb - 2 * i)
                                    bs = bass.ds(pr.c * CB + 2 * i, n)
                                    if l < LAYERS - 1:
                                        dve.wait_ge(s_hi, C0 + pr.before + i + 1)
                                        v.scalar_tensor_tensor(parts[(l + 1) % 2][:, 1, bs, :], pt[i][:, 0:n, :], scale[0:B, l + 1, 0:1],
                                                               parts[(l + 1) % 2][:, 0, bs, :], ALU.mult, ALU.subtract).then_inc(s_lo, 1)
                                    else:
                                        dve.wait_ge(s_pt, C0 + pr.before + i + 1)
                                        dve.wait_ge(s_xb, 1)
                                        v.tensor_tensor(X[:, bs, :], pt[i][:, 0:n, :], X[:, bs, :], ALU.add).then_inc(s_lo, 1)
                                        dve.wait_ge(s_lo, C0 + pr.before + i + 1)
                                        for b in range(n):
                                            v.bn_stats(io["stats"][:, pr.c * CB + 2 * i + b, :], X[:, pr.c * CB + 2 * i + b, :])
                        layer(dve, l, step)


def gated_networks(nc, io, c, X, outer):
    H1, H2 = io["L1_ffn_sW1"].shape[1], io["L1_ffn_sW2"].shape[1]
    E, _, G1 = io["L1_ffn_eW1"].shape
    G2 = io["L1_ffn_eW2"].shape[2]
    KH = H1 // P
    Q = E // 2
    assert H2 == G1 == P and 2 * G2 == P and KH == 2
    NBIAS = KH + 1 + E + Q
    with Space(nc, outer) as s:
        x_t = s.sb("x_t", [P, KD, N])
        top = s.sb("top", [B, NB, E + 1])
        top_t = s.sb("top_t", [E + 1, N])
        sw1, sw2, sw3 = s.sb("sw1", [P, KD, H1]), s.sb("sw2", [P, KH, H2]), s.sb("sw3", [P, D])
        ew1, ew2, ew3 = s.sb("ew1", [P, E, KD, G1]), s.sb("ew2", [P, E, G2]), s.sb("ew3", [P, Q, D])
        b_last = s.sb("b_last", [E + 1, D])
        bias = s.sb("biasf", [P, NBIAS])
        spread = s.sb("spread", [E + 1, Q, 2 * G2])
        s_wl = s.sem("J_wl")

        with Space(nc, s) as s1:
            norm = Norm(s1, "n4", io["stats"])
            gw = s1.sb("gw4", [P, KD, E])
            gb = s1.sb("gb4", [B, E])
            rank_i, rank = s1.sb("rank4_i", [B, E], I32), s1.sb("rank4", [B, E])
            b_rows = s1.sb("b_rows4", [NBIAS, P])
            lg, ex, gate, eq, first_, rest, both = (s1.sb("j" + n, [B, NB, E]) for n in ("lg", "ex", "gate", "eq", "first", "rest", "both"))
            mx, sm = (s1.sb("j" + n, [B, NB]) for n in ("mx", "sm"))
            top_rows = s1.sb("top_rows", [NB * (E + 1), B])
            plog = s1.ps("plog4", [B, NB, E])
            pb = s1.ps("pb4", [P, P])
            s_gw, s_gb, s_br, s_bt, s_c, s_copy, s_v, s_sh, s_ex, s_top, s_tt, s_tc, s_to, s_tl = (
                s1.sem("J_" + n) for n in ("gw", "gb", "br", "bt", "c", "copy", "v", "sh", "ex", "top", "tt", "tc", "to", "tl"))
            with nc.Block() as block:
                @block.sync
                def _(sp):
                    sp.dma_start(gw[:], io["L1_ffn_gW"].rearrange("(k p) e -> p k e", p=P)).then_inc(s_gw, 16)
                    sp.dma_start(gb[:], bc(io["L1_ffn_gb"], B, 0)).then_inc(s_gb, 16)
                    at = 0
                    for b_, n in ((io["L1_ffn_sb1"].rearrange("(r p) -> r p", p=P), KH), (io["L1_ffn_sb2"].rearrange("(r p) -> r p", p=P), 1),
                                  (io["L1_ffn_eb1"], E), (io["L1_ffn_eb2"].rearrange("(q r) g -> q (r g)", r=2), Q)):
                        sp.dma_start(b_rows[at:at + n], b_).then_inc(s_br, 16)
                        at += n
                    loads = [(sw1[:], io["L1_ffn_sW1"].rearrange("(k p) h -> p k h", p=P)),
                             (sw2[:], io["L1_ffn_sW2"].rearrange("(k p) h -> p k h", p=P)), (sw3[:], io["L1_ffn_sW3"]),
                             (ew2[:], io["L1_ffn_eW2"].rearrange("e p g -> p e g")),
                             (ew3[:], io["L1_ffn_eW3"].rearrange("(q r) g o -> (r g) q o", r=2)),
                             (b_last[0:E], io["L1_ffn_eb3"]), (b_last[E:E + 1], io["L1_ffn_sb3"].rearrange("(o d) -> o d", o=1))]
                    loads += [(ew1[:, e], io["L1_ffn_eW1"][e].rearrange("(k p) h -> p k h", p=P)) for e in range(E)]
                    for o, i in loads:
                        sp.dma_start(o, i).then_inc(s_wl, 16)
                    sp.wait_ge(s_tc, 1)
                    sp.dma_start(io["top_dram"].rearrange("t e n -> (t e) n"), top_rows[:]).then_inc(s_to, 16)
                    sp.wait_ge(s_to, 16)
                    sp.dma_start(top_t[:].rearrange("e (t n) -> e t n", n=B), io["top_dram"].rearrange("t e n -> e t n")).then_inc(s_tl, 16)
                    sp.wait_ge(s_tl, 16)
                    sp.wait_ge(s_wl, 16 * len(loads))

                @block.gpsimd
                def _(pool):
                    g = nc.gpsimd
                    g.iota(rank_i[:], [[-1, E]], base=E, channel_multiplier=0).then_inc(s_c, 1)
                    g.memset(spread[:], 1.0).then_inc(s_c, 1)
                    pool.wait_ge(s_c, 2)
                    g.affine_select(out=spread[:], in_=spread[:], compare_op=ALU.is_ge, fill=0.0, base=0,
                                    pattern=[[2 * G2, Q], [1, 2 * G2]], channel_multiplier=-G2).then_inc(s_c, 1)
                    pool.wait_ge(s_c, 3)
                    g.affine_select(out=spread[:], in_=spread[:], compare_op=ALU.is_ge, fill=0.0, base=G2 - 1,
                                    pattern=[[-2 * G2, Q], [-1, 2 * G2]], channel_multiplier=G2).then_inc(s_c, 1)

                    def body(t, u, first):
                        pool.wait_ge(norm.s_xt, t + 1)
                        g.tensor_copy(x_t[:, :, bass.ds(t * B, B)], norm.xt[:, u, :, :]).then_inc(s_copy, 1)
                    blocks(pool, body)

                @block.scalar
                def _(act):
                    norm.std(nc, act)
                    act.wait_ge(norm.s_rstd, 1)
                    blocks(act, lambda t, u, first: norm.rows(nc, act, X, t, u, first))
                    act.wait_ge(s_sh, 1)
                    nc.scalar.activation(ex[:], lg[:], ACT.Exp).then_inc(s_ex, 1)
                    act.wait_ge(s_sh, 2)
                    nc.scalar.activation(ex[:], lg[:], ACT.Exp).then_inc(s_ex, 1)

                @block.tensor
                def _(pe):
                    pe.wait_ge(s_br, 64)
                    nc.tensor.transpose(pb[:, 0:NBIAS], b_rows[:], c["ident"][0:NBIAS, 0:NBIAS]).then_inc(s_bt, 1)
                    pe.wait_ge(s_gw, 16)

                    def turn(t, u, first):
                        norm.turn(nc, pe, c["ident"], t, u, first)

                    def body(t, u, first):
                        pe.wait_ge(norm.s_xt, t + 1)
                        for k in range(KD):
                            mm = nc.tensor.matmul(plog[:, t, :], norm.xt[:, u, k, :], gw[:, k, :], start=(k == 0), stop=(k == KD - 1))
                        mm.then_inc(norm.s_used, 1)
                    staggered(pe, turn, body)
                    pe.wait_ge(s_top, 1)
                    nc.tensor.transpose(pb[0:NB * (E + 1), 0:B], top[:].rearrange("p t e -> p (t e)"), c["ident"][0:B, 0:B]).then_inc(s_tt, 1)

                @block.vector
                def _(dve):
                    v = nc.vector
                    n = [0]

                    def step(ins):
                        n[0] += 1
                        ins.then_inc(s_v, 1)
                        dve.wait_ge(s_v, n[0])

                    def first_max(out, x):
                        step(v.tensor_reduce(mx[:], x[:], AX.X, ALU.max))
                        step(v.tensor_tensor(eq[:], x[:], bc(mx[:], E, 2), ALU.is_equal))
                        step(v.tensor_tensor(eq[:], eq[:], bc(rank[:], NB, 1), ALU.mult))
                        step(v.tensor_reduce(sm[:], eq[:], AX.X, ALU.max))
                        step(v.tensor_tensor(out[:], eq[:], bc(sm[:], E, 2), ALU.is_equal))

                    norm.stats(nc, dve)
                    dve.wait_ge(s_bt, 1)
                    v.tensor_copy(bias[:], pb[:, 0:NBIAS])

                    def body(t, u, first):
                        if not first:
                            dve.wait_ge(s_copy, t - UN + 1)
                        norm.out(nc, dve, t, u, first)
                    blocks(dve, body)
                    dve.wait_ge(s_gb, 16)
                    dve.wait_ge(s_c, 4)
                    dve.wait_ge(norm.s_used, NB)
                    v.tensor_copy(rank[:], rank_i[:])
                    step(v.tensor_tensor(lg[:], plog[:], bc(gb[:], NB, 1), ALU.add))
                    step(v.tensor_reduce(mx[:], lg[:], AX.X, ALU.max))
                    v.tensor_tensor(lg[:], lg[:], bc(mx[:], E, 2), ALU.subtract).then_inc(s_sh, 1)
                    dve.wait_ge(s_sh, 1)
                    dve.wait_ge(s_ex, 1)
                    step(v.tensor_reduce(sm[:], ex[:], AX.X, ALU.add))
                    step(v.reciprocal(mx[:], sm[:]))
                    step(v.tensor_tensor(gate[:], ex[:], bc(mx[:], E, 2), ALU.mult))
                    first_max(first_, gate)
                    step(v.scalar_tensor_tensor(rest[:].rearrange("p t e -> p (t e)"), first_[:].rearrange("p t e -> p (t e)"), -4.0,
                                                gate[:].rearrange("p t e -> p (t e)"), ALU.mult, ALU.add))
                    step(v.tensor_reduce(mx[:], gate[:], AX.X, ALU.max))
                    v.tensor_tensor(lg[:], gate[:], bc(mx[:], E, 2), ALU.subtract).then_inc(s_sh, 1)
                    dve.wait_ge(s_sh, 2)
                    first_max(both, rest)
                    step(v.tensor_tensor(both[:], both[:], first_[:], ALU.add))
                    dve.wait_ge(s_ex, 2)
                    step(v.tensor_tensor(ex[:], ex[:], both[:], ALU.mult))
                    step(v.tensor_reduce(sm[:], ex[:], AX.X, ALU.add))
                    step(v.reciprocal(mx[:], sm[:]))
                    v.memset(top[:, :, E:E + 1], 1.0)
                    v.tensor_tensor(top[:, :, 0:E], ex[:], bc(mx[:], E, 2), ALU.mult).then_inc(s_top, 1)
                    dve.wait_ge(s_tt, 1)
                    v.tensor_copy(top_rows[:], pb[0:NB * (E + 1), 0:B]).then_inc(s_tc, 1)

        with Space(nc, s) as s2:
            a1 = s2.sb("shared1", [P, 2, KH, CN])
            g1 = s2.sb("expert1", [P, 2, E, CN])
            a2 = s2.sb("shared2", [P, 2, CN])
            g2, g2w = (s2.sb(n, [P, 2, Q, CN]) for n in ("expert2", "expert2_w"))
            top_c = s2.sb("top_chunk", [E + 1, 2, CN])
            y = s2.sb("y_out", [B, 2, CB, D])
            ring = [s2.ps(f"ring{i}", [P, CN]) for i in range(3)]
            pg = [s2.ps(f"pg{q}", [P, CN]) for q in range(Q)]
            po = [s2.ps(f"po{i}", [B, 2, D]) for i in range(2)]
            s_p, s_a, s_g, s_g2w, s_po, s_y, s_tc = (s2.sem("K_" + n) for n in ("p", "a", "g", "g2w", "po", "y", "tc"))
            s_out = [s2.sem(f"K_out{k}") for k in range(2)]
            NP_ = KH + E + 1 + Q
            assert NP_ % 3 == 0
            C0 = 2 * NP_
            out_v = io["out"].rearrange("(t p) d -> p t d", p=B)
            dest = [lambda k, m=m: a1[:, k, m] for m in range(KH)] + [lambda k, e=e: g1[:, k, e] for e in range(E)] + \
                   [lambda k: a2[:, k]] + [lambda k, q=q: g2[:, k, q] for q in range(Q)]
            bias_of = list(range(KH)) + [KH + 1 + e for e in range(E)] + [KH] + [KH + 1 + E + q for q in range(Q)]

            with nc.Block() as block:
                @block.sync
                def _(sp):
                    def step(_, ch):
                        if ch is None:
                            return
                        sp.wait_ge(s_y, C0 + ch.before + ch.pairs)
                        for a, b in ((0, 112), (112, B)):
                            sp.dma_start(out_v[a:b, bass.ds(ch.c * CB, ch.nb), :], y[a:b, ch.k, 0:ch.nb, :]).then_inc(s_out[ch.k], 16)
                    layer(sp, 0, step)
                    sp.wait_ge(s_out[0], 32 * ((NC + 1) // 2 + 1))
                    sp.wait_ge(s_out[1], 32 * (NC // 2 + 1))

                @block.gpsimd
                def _(pool):
                    pool.sem_inc(s_tc, C0)

                    def step(ch, _):
                        if ch is None:
                            return
                        pool.wait_ge(s_po, C0 + ch.before - 2)
                        nc.gpsimd.tensor_copy(top_c[:, ch.k, 0:ch.nb * B], top_t[:, ch.nodes()]).then_inc(s_tc, 1)
                    layer(pool, 0, step)

                @block.tensor
                def _(pe):
                    t_ = nc.tensor
                    pe.sem_inc(s_p, C0)
                    pe.sem_inc(s_g, C0)
                    pe.sem_inc(s_po, C0)

                    def products(ch):
                        w, k = ch.nb * B, ch.k
                        xs = [x_t[:, j, ch.nodes()] for j in range(KD)]

                        def bank(n):
                            pe.wait_ge(s_a, C0 + NP_ * ch.c + n - 2)
                            return ring[n % 3]

                        def done(n):
                            pe.wait_ge(s_a, C0 + NP_ * ch.c + n + 1)
                        for n in range(KH + E):
                            r = bank(n)
                            for j in range(KD):
                                lhs = sw1[:, j, n * P:(n + 1) * P] if n < KH else ew1[:, n - KH, j, :]
                                mm = t_.matmul(r[:, 0:w], lhs, xs[j], start=(j == 0), stop=(j == KD - 1))
                            mm.then_inc(s_p, 1)
                        r = bank(KH + E)
                        for j in range(KH):
                            mm = t_.matmul(r[:, 0:w], sw2[:, j, :], a1[:, k, j, 0:w], start=(j == 0), stop=(j == KH - 1))
                        mm.then_inc(s_p, 1)
                        for q in range(Q):
                            r = bank(KH + E + 1 + q)
                            done(KH + 2 * q + 1)
                            for e in range(2):
                                mm = t_.matmul(r[e * G2:(e + 1) * G2, 0:w], ew2[:, 2 * q + e, :], g1[:, k, 2 * q + e, 0:w], start=True, stop=True)
                            mm.then_inc(s_p, 1)
                        pe.wait_ge(s_tc, C0 + ch.c + 1)
                        for q in range(Q):
                            pe.wait_ge(s_g2w, C0 + Q * (ch.c - 1) + q + 1)
                            t_.matmul(pg[q][:, 0:w], spread[:, q, :], top_c[:, k, 0:w], start=True, stop=True).then_inc(s_g, 1)

                    def outputs(ch):
                        k = ch.k
                        pe.wait_ge(s_g2w, C0 + Q * (ch.c + 1))
                        pe.wait_ge(s_a, C0 + NP_ * (ch.c + 1))
                        pe.wait_ge(s_y, C0 + ch.before)
                        for b in range(ch.nb):
                            bs = slice(b * B, (b + 1) * B)
                            o = po[b // 2][:, b % 2, :]
                            t_.matmul(o, a2[:, k, bs], sw3[:], start=True, stop=False)
                            for q in range(Q):
                                t_.matmul(o, g2w[:, k, q, bs], ew3[:, q, :], start=False, stop=False)
                            mm = t_.matmul(o, top_c[:, k, bs], b_last[:], start=False, stop=True)
                            if b % 2 or b == ch.nb - 1:
                                mm.then_inc(s_po, 1)

                    def step(ch, pr):
                        if ch is not None:
                            products(ch)
                        if pr is not None:
                            outputs(pr)
                    layer(pe, 0, step)

                @block.scalar
                def _(act):
                    act.sem_inc(s_a, C0)

                    def step(ch, _):
                        if ch is None:
                            return
                        w = ch.nb * B
                        act.wait_ge(s_po, C0 + ch.before - 2)
                        act.wait_ge(s_g2w, C0 + Q * (ch.c - 1))
                        for n in range(NP_):
                            act.wait_ge(s_p, C0 + NP_ * ch.c + n + 1)
                            nc.scalar.activation(dest[n](ch.k)[:, 0:w], ring[n % 3][:, 0:w], ACT.Relu,
                                                 bias=bias[:, bias_of[n]:bias_of[n] + 1]).then_inc(s_a, 1)
                    layer(act, 0, step)

                @block.vector
                def _(dve):
                    v = nc.vector
                    dve.sem_inc(s_g2w, C0)
                    dve.sem_inc(s_y, C0)
                    for k in range(2):
                        dve.sem_inc(s_out[k], 32)

                    def step(ch, pr):
                        if ch is not None:
                            w = ch.nb * B
                            for q in range(Q):
                                dve.wait_ge(s_g, C0 + Q * ch.c + q + 1)
                                dve.wait_ge(s_po, C0 + ch.before - 2)
                                dve.wait_ge(s_a, C0 + NP_ * ch.c + NP_ - Q + q + 1)
                                v.tensor_tensor(g2w[:, ch.k, q, 0:w], pg[q][:, 0:w], g2[:, ch.k, q, 0:w], ALU.mult).then_inc(s_g2w, 1)
                        if pr is not None:
                            dve.wait_ge(s_out[pr.k], 32 * (pr.g2 + 1))
                            for i in range(pr.pairs):
                                nb = min(2, pr.nb - 2 * i)
                                dve.wait_ge(s_po, C0 + pr.before + i + 1)
                                v.tensor_tensor(y[:, pr.k, 2 * i:2 * i + nb, :], po[i][:, 0:nb, :],
                                                X[:, bass.ds(pr.c * CB + 2 * i, nb), :], ALU.add).then_inc(s_y, 1)
                    layer(dve, 0, step)


def program(nc, io):
    with Space(nc) as k:
        io["s_buf_zero"] = k.sem("buf_zero")
        c = constants(nc, k)
        X = k.sb("X", [B, NB, D])
        io["stats"] = k.sb("stats", [B, NB, 6])
        with Space(nc) as graph:
            io["h1"], io["t_bias"] = graph.sb("h1", [B, NB, D + 1]), graph.sb("t_bias", [B, NB])
            with Space(nc, graph) as edges:
                keep = {"srcf": edges.sb("srcf", [B, EP]), "dstf": edges.sb("dstf", [B, EP]),
                        "zeros": edges.sb("zeros", [P, 8 * D]),
                        "lo": edges.sb("lo", [EW, NW, 2], BF16), "code": edges.sb("code", [EW, NW, 2], BF16),
                        "captured": edges.sb("captured", [1, 1], I32)}
                edge_windows(nc, io, c, keep, X, graph)
                count_matrix(nc, io, c, keep, graph)
            graph_attention(nc, io, c, X, graph)
        with Space(nc) as moe:
            tokens = Tokens(nc, moe, io, X)
            mixture(nc, io, c, X, tokens, None)
            mean_network(nc, io, c, X, tokens, moe)
        gated_networks(nc, io, c, X, k)


INPUTS = ['x', 'src', 'dst', 'L0_gnn_W', 'L0_gnn_a', 'L0_ffn_gate_w', 'L0_ffn_gate_b', 'L0_ffn_w1', 'L0_ffn_b1',
          'L0_ffn_w2', 'L0_ffn_b2', 'L1_gnn_W_in', 'L1_gnn_b_in', 'L1_gnn_W_agg', 'L1_gnn_W_self', 'L1_gnn_b_hid',
          'L1_gnn_W_out', 'L1_gnn_b_out', 'L1_ffn_sW1', 'L1_ffn_sb1', 'L1_ffn_sW2', 'L1_ffn_sb2', 'L1_ffn_sW3',
          'L1_ffn_sb3', 'L1_ffn_eW1', 'L1_ffn_eb1', 'L1_ffn_eW2', 'L1_ffn_eb2', 'L1_ffn_eW3', 'L1_ffn_eb3',
          'L1_ffn_gW', 'L1_ffn_gb']


def kernel(**inputs):
    import numpy as np
    import concourse.bacc as bacc
    from concourse.bass_utils import run_bass_kernel_spmd as run

    nc = bacc.Bacc("TRN2", target_bir_lowering=False, num_devices=1)
    arrays, io = {}, {}
    for name in INPUTS:
        a = np.ascontiguousarray(inputs[name])
        arrays["in_" + name] = a
        io[name] = nc.dram_tensor("in_" + name, a.shape, mybir.dt.from_np(a.dtype), kind="ExternalInput").ap()
    io["out"] = nc.dram_tensor("out_x", (N, D), F32, kind="ExternalOutput").ap()
    for name, shape, dt in (("starts_dram", (NW,), I32), ("buf_dram", (4096, D), F32), ("AT_dram", (N, N), F16),
                            ("dinv_dram", (N,), F32), ("s_dram", (N,), F32),
                            ("ybuf_dram", (4096, D), F32), ("top_dram", (NB, 5, B), F32)):
        io[name] = nc.dram_tensor(name, shape, dt).ap()
    program(nc, io)
    r = run(nc, [arrays], core_ids=[0])
    return r.results[0]["out_x"]
```
